# Optimizing a Trainium2 kernel written in Bass

```python
import numpy as np
import jax
import jax.numpy as jnp

def _softmax(x, axis=-1):
    return jax.nn.softmax(x, axis=axis)

def _gelu(x):
    return jax.nn.gelu(x, approximate=True)

def _silu(x):
    return jax.nn.silu(x)

def _sigmoid(x):
    return jax.nn.sigmoid(x)

def _layernorm(x, axis=-1, eps=1e-05):
    m = jnp.mean(x, axis=axis, keepdims=True)
    v = jnp.var(x, axis=axis, keepdims=True)
    return (x - m) / jnp.sqrt(v + eps)

def _scatter_add(tgt, idx, src, axis=0):
    return tgt.at[idx].add(src)

def _segment_sum(src, seg, n):
    return jax.ops.segment_sum(src, seg, n)
kernel_name = 'mk_perceiver_d1_seqx_r4_8a4fc5'

def setup_inputs(seed: int=0):
    np.random.seed(seed)
    _w = jnp.asarray

    def _rec_inputs():
        import jax
        import jax.numpy as jnp
        _rk = jax.random.key(seed)
        x = -0.0002928 + 1 * jax.random.normal(jax.random.fold_in(_rk, 1), (8, 64, 256), jnp.float32)
        _lenS = 64 - jax.random.randint(jax.random.fold_in(_rk, 7), (8,), 0, max(1, 64 // 4) + 1, jnp.int32)
        _lenS2 = 1601 - jax.random.randint(jax.random.fold_in(_rk, 8), (8,), 0, max(1, 1601 // 4) + 1, jnp.int32)
        _ctx_1024P = jax.random.normal(jax.random.fold_in(_rk, 11), (8, 16, 256), jnp.float32)
        _ctx_1024c = jax.random.dirichlet(jax.random.fold_in(_rk, 511), 0.3 * jnp.ones((16,), jnp.float32), (8, 1601))
        _ctx_1024t = jnp.einsum('bsk,bkd->bsd', _ctx_1024c, _ctx_1024P)
        _ctx_1024t = _ctx_1024t * jax.lax.rsqrt(jnp.mean(jnp.square(_ctx_1024t)) + 1e-12) * 0.953939
        ctx_1024 = -1.39393e-06 + 0.999914 * (_ctx_1024t + 0.3 * jax.random.normal(jax.random.fold_in(_rk, 611), (8, 1601, 256), jnp.float32))
        _validS = jnp.arange(64)[None, :] < _lenS[:, None]
        _validS2 = jnp.arange(1601)[None, :] < _lenS2[:, None]
        _causal = jnp.tril(jnp.ones((64, 64), dtype=bool))
        mask_Bx1xSxS2_bf0 = jnp.logical_not(jnp.ones((8, 1, 64, 1601), dtype=bool))
        return (x, ctx_1024, mask_Bx1xSxS2_bf0)
    x, ctx_1024, mask_Bx1xSxS2_bf0 = _rec_inputs()

    def _L0_xattn_setup():
        import jax, jax.numpy as jnp
        import numpy as np
        B, S, D, H = (2, 512, 256, 16)
        HD = D // H
        LN_EPS = 1e-05

        def _linear(x, w, b):
            return jnp.einsum('bsd,od->bso', x, w) + b

        def _split_heads(x):
            b, s, _ = x.shape
            return x.reshape(b, s, H, HD).transpose(0, 2, 1, 3)
        key = jax.random.key(seed)
        ks = jax.random.split(key, 14)
        w = 0.02
        return {'q': jax.random.normal(ks[0], (B, S, D), jnp.float32), 'k': jax.random.normal(ks[1], (B, S, D), jnp.float32), 'v': jax.random.normal(ks[2], (B, S, D), jnp.float32), 'mask': jnp.zeros((B, 1, S, S), dtype=bool), 'training': 0, 'wq_w': jax.random.normal(ks[3], (D, D), jnp.float32) * w, 'wq_b': jnp.zeros((D,), jnp.float32), 'wk_w': jax.random.normal(ks[4], (D, D), jnp.float32) * w, 'wk_b': jnp.zeros((D,), jnp.float32), 'wv_w': jax.random.normal(ks[5], (D, D), jnp.float32) * w, 'wv_b': jnp.zeros((D,), jnp.float32), 'wo_w': jax.random.normal(ks[6], (D, D), jnp.float32) * w, 'wo_b': jnp.zeros((D,), jnp.float32), 'ln_g': jnp.ones((D,), jnp.float32), 'ln_b': jnp.zeros((D,), jnp.float32)}
    _L0_xattn_all = _L0_xattn_setup()
    _L0_xattn_in = {k: v for k, v in _L0_xattn_all.items() if k in ('wq_w', 'wq_b', 'wk_w', 'wk_b', 'wv_w', 'wv_b', 'wo_w', 'wo_b', 'ln_g', 'ln_b')}
    del _L0_xattn_all

    def _L0_attn_setup():
        import jax, jax.numpy as jnp
        import numpy as np
        MODEL_DIM = 256
        NUM_HEADS = 16
        HEAD_DIM = MODEL_DIM // NUM_HEADS
        WINDOW_SIZE = 64
        BATCH = 1
        SEQ_LEN = 1024

        def local_causal_bias(seq_len, window_size, dtype):
            i = jnp.arange(seq_len)[:, None]
            j = jnp.arange(seq_len)[None, :]
            allowed = (j <= i) & (j > i - window_size)
            neg_inf = jnp.array(-jnp.inf, dtype=dtype)
            return jnp.where(allowed, jnp.array(0.0, dtype=dtype), neg_inf)
        key = jax.random.key(seed)
        k_h, k_q, k_k, k_v, k_o = jax.random.split(key, 5)
        s = 1.0 / np.sqrt(MODEL_DIM)
        hidden = jax.random.normal(k_h, (BATCH, SEQ_LEN, MODEL_DIM), dtype=jnp.float32)
        Wq = jax.random.normal(k_q, (MODEL_DIM, MODEL_DIM), dtype=jnp.float32) * s
        Wk = jax.random.normal(k_k, (MODEL_DIM, MODEL_DIM), dtype=jnp.float32) * s
        Wv = jax.random.normal(k_v, (MODEL_DIM, MODEL_DIM), dtype=jnp.float32) * s
        Wo = jax.random.normal(k_o, (MODEL_DIM, MODEL_DIM), dtype=jnp.float32) * s
        return {'hidden': hidden, 'Wq': Wq, 'Wk': Wk, 'Wv': Wv, 'Wo': Wo}
    _L0_attn_all = _L0_attn_setup()
    _L0_attn_in = {k: v for k, v in _L0_attn_all.items() if k in ('Wq', 'Wk', 'Wv', 'Wo')}
    del _L0_attn_all

    def _L0_ffn_setup():
        import jax, jax.numpy as jnp
        import numpy as np
        D = 256
        H = 16
        DH = D // H
        DC = D // 4
        HID = 512
        G = 2
        EPG = 4
        E = G * EPG
        TOPK = 2
        EPS = 1e-06
        B, T = (2, 512)

        def _rope_sincos(t, dh):
            inv_freq = 1.0 / 10000.0 ** (jnp.arange(0, dh, 2, dtype=jnp.float32) / dh)
            ang = jnp.arange(t, dtype=jnp.float32)[:, None] * inv_freq[None, :]
            return (jnp.sin(ang), jnp.cos(ang))

        def _apply_rope(x, sin, cos):
            x1 = x[..., ::2]
            x2 = x[..., 1::2]
            r = jnp.stack([x1 * cos - x2 * sin, x1 * sin + x2 * cos], axis=-1)
            return r.reshape(x.shape)

        def _swiglu(x):
            a, b = jnp.split(x, 2, axis=-1)
            return jax.nn.silu(a) * b

        def _rmsnorm(x, w):
            return x * jax.lax.rsqrt(jnp.mean(x * x, axis=-1, keepdims=True) + EPS) * w
        key = jax.random.key(seed)
        ks = jax.random.split(key, 14)
        s = 0.02
        return {'src': jax.random.normal(ks[0], (B, T, D), jnp.float32), 'Wq': jax.random.normal(ks[1], (D, D), jnp.float32) * s, 'Wk_c': jax.random.normal(ks[2], (D, DC), jnp.float32) * s, 'Wv_c': jax.random.normal(ks[3], (D, DC), jnp.float32) * s, 'Wk': jax.random.normal(ks[4], (DC, D), jnp.float32) * s, 'Wv': jax.random.normal(ks[5], (DC, D), jnp.float32) * s, 'Wo': jax.random.normal(ks[6], (D, D), jnp.float32) * s, 'W_shared_in': jax.random.normal(ks[7], (D, 2 * HID), jnp.float32) * s, 'W_shared_out': jax.random.normal(ks[8], (HID, D), jnp.float32) * s, 'W1_shared': jax.random.normal(ks[9], (D, 2 * HID), jnp.float32) * s, 'W2_experts': jax.random.normal(ks[10], (E, HID, D), jnp.float32) * s, 'Wg_gate': jax.random.normal(ks[11], (D, G), jnp.float32) * s, 'We_gate': jax.random.normal(ks[12], (D, E), jnp.float32) * s, 'group_bias': jnp.zeros((G,), jnp.float32), 'expert_bias': jnp.zeros((E,), jnp.float32), 'norm1_w': jnp.ones((D,), jnp.float32), 'norm2_w': jnp.ones((D,), jnp.float32)}
    _L0_ffn_all = _L0_ffn_setup()
    _L0_ffn_in = {k: v for k, v in _L0_ffn_all.items() if k in ('Wq', 'Wk_c', 'Wv_c', 'Wk', 'Wv', 'Wo', 'W_shared_in', 'W_shared_out', 'W1_shared', 'W2_experts', 'Wg_gate', 'We_gate', 'group_bias', 'expert_bias', 'norm1_w', 'norm2_w')}
    del _L0_ffn_all
    return {'x': x, 'ctx_1024': ctx_1024, 'mask_Bx1xSxS2_bf0': mask_Bx1xSxS2_bf0, 'L0_xattn_wq_w': _L0_xattn_in['wq_w'], 'L0_xattn_wq_b': _L0_xattn_in['wq_b'], 'L0_xattn_wk_w': _L0_xattn_in['wk_w'], 'L0_xattn_wk_b': _L0_xattn_in['wk_b'], 'L0_xattn_wv_w': _L0_xattn_in['wv_w'], 'L0_xattn_wv_b': _L0_xattn_in['wv_b'], 'L0_xattn_wo_w': _L0_xattn_in['wo_w'], 'L0_xattn_wo_b': _L0_xattn_in['wo_b'], 'L0_xattn_ln_g': _L0_xattn_in['ln_g'], 'L0_xattn_ln_b': _L0_xattn_in['ln_b'], 'L0_attn_Wq': _L0_attn_in['Wq'], 'L0_attn_Wk': _L0_attn_in['Wk'], 'L0_attn_Wv': _L0_attn_in['Wv'], 'L0_attn_Wo': _L0_attn_in['Wo'], 'L0_ffn_Wq': _L0_ffn_in['Wq'], 'L0_ffn_Wk_c': _L0_ffn_in['Wk_c'], 'L0_ffn_Wv_c': _L0_ffn_in['Wv_c'], 'L0_ffn_Wk': _L0_ffn_in['Wk'], 'L0_ffn_Wv': _L0_ffn_in['Wv'], 'L0_ffn_Wo': _L0_ffn_in['Wo'], 'L0_ffn_W_shared_in': _L0_ffn_in['W_shared_in'], 'L0_ffn_W_shared_out': _L0_ffn_in['W_shared_out'], 'L0_ffn_W1_shared': _L0_ffn_in['W1_shared'], 'L0_ffn_W2_experts': _L0_ffn_in['W2_experts'], 'L0_ffn_Wg_gate': _L0_ffn_in['Wg_gate'], 'L0_ffn_We_gate': _L0_ffn_in['We_gate'], 'L0_ffn_group_bias': _L0_ffn_in['group_bias'], 'L0_ffn_expert_bias': _L0_ffn_in['expert_bias'], 'L0_ffn_norm1_w': _L0_ffn_in['norm1_w'], 'L0_ffn_norm2_w': _L0_ffn_in['norm2_w']}

def reference(x, ctx_1024, mask_Bx1xSxS2_bf0, L0_xattn_wq_w, L0_xattn_wq_b, L0_xattn_wk_w, L0_xattn_wk_b, L0_xattn_wv_w, L0_xattn_wv_b, L0_xattn_wo_w, L0_xattn_wo_b, L0_xattn_ln_g, L0_xattn_ln_b, L0_attn_Wq, L0_attn_Wk, L0_attn_Wv, L0_attn_Wo, L0_ffn_Wq, L0_ffn_Wk_c, L0_ffn_Wv_c, L0_ffn_Wk, L0_ffn_Wv, L0_ffn_Wo, L0_ffn_W_shared_in, L0_ffn_W_shared_out, L0_ffn_W1_shared, L0_ffn_W2_experts, L0_ffn_Wg_gate, L0_ffn_We_gate, L0_ffn_group_bias, L0_ffn_expert_bias, L0_ffn_norm1_w, L0_ffn_norm2_w):
    import jax
    import jax.numpy as jnp

    def _L0_xattn_ref(q, k, v, mask, training, wq_w, wq_b, wk_w, wk_b, wv_w, wv_b, wo_w, wo_b, ln_g, ln_b):
        import jax, jax.numpy as jnp
        import numpy as np
        B, S, D, H = (2, 512, 256, 16)
        HD = D // H
        LN_EPS = 1e-05

        def _linear(x, w, b):
            return jnp.einsum('bsd,od->bso', x, w) + b

        def _split_heads(x):
            b, s, _ = x.shape
            return x.reshape(b, s, H, HD).transpose(0, 2, 1, 3)
        residual = q
        Q = _split_heads(_linear(q, wq_w, wq_b))
        K = _split_heads(_linear(k, wk_w, wk_b))
        V = _split_heads(_linear(v, wv_w, wv_b))
        dk = jnp.sqrt(jnp.asarray(HD, jnp.float16)).astype(jnp.float32) + 1e-08
        score = jnp.einsum('bhqd,bhkd->bhqk', Q, K) / dk
        attn = jnp.where(mask, -jnp.inf, score)
        ctx = jnp.einsum('bhqk,bhkd->bhqd', attn, V)
        b, _, s, _ = ctx.shape
        ctx = ctx.transpose(0, 2, 1, 3).reshape(b, s, D)
        o = _linear(ctx, wo_w, wo_b)
        x = residual + o
        mu = jnp.mean(x, axis=-1, keepdims=True)
        var = jnp.mean(jnp.square(x - mu), axis=-1, keepdims=True)
        return ln_g * (x - mu) * jax.lax.rsqrt(var + LN_EPS) + ln_b

    def _L0_attn_ref(hidden, Wq, Wk, Wv, Wo):
        import jax, jax.numpy as jnp
        import numpy as np
        MODEL_DIM = 256
        NUM_HEADS = 16
        HEAD_DIM = MODEL_DIM // NUM_HEADS
        WINDOW_SIZE = 64
        BATCH = 1
        SEQ_LEN = 1024

        def local_causal_bias(seq_len, window_size, dtype):
            i = jnp.arange(seq_len)[:, None]
            j = jnp.arange(seq_len)[None, :]
            allowed = (j <= i) & (j > i - window_size)
            neg_inf = jnp.array(-jnp.inf, dtype=dtype)
            return jnp.where(allowed, jnp.array(0.0, dtype=dtype), neg_inf)
        B, S, D = hidden.shape

        def proj(x, W):
            y = jnp.einsum('bsd,ed->bse', x, W)
            return y.reshape(B, S, NUM_HEADS, HEAD_DIM).transpose(0, 2, 1, 3)
        q = proj(hidden, Wq)
        k = proj(hidden, Wk)
        v = proj(hidden, Wv)
        scale = 1.0 / np.sqrt(HEAD_DIM)
        bias = local_causal_bias(S, WINDOW_SIZE, hidden.dtype)
        scores = jnp.einsum('bhqd,bhkd->bhqk', q, k) * scale + bias
        attn = jax.nn.softmax(scores, axis=-1)
        out = jnp.einsum('bhqk,bhkd->bhqd', attn, v)
        out = out.transpose(0, 2, 1, 3).reshape(B, S, D)
        return jnp.einsum('bsd,ed->bse', out, Wo)

    def _L0_ffn_ref(src, Wq, Wk_c, Wv_c, Wk, Wv, Wo, W_shared_in, W_shared_out, W1_shared, W2_experts, Wg_gate, We_gate, group_bias, expert_bias, norm1_w, norm2_w):
        import jax, jax.numpy as jnp
        import numpy as np
        D = 256
        H = 16
        DH = D // H
        DC = D // 4
        HID = 512
        G = 2
        EPG = 4
        E = G * EPG
        TOPK = 2
        EPS = 1e-06
        B, T = (2, 512)

        def _rope_sincos(t, dh):
            inv_freq = 1.0 / 10000.0 ** (jnp.arange(0, dh, 2, dtype=jnp.float32) / dh)
            ang = jnp.arange(t, dtype=jnp.float32)[:, None] * inv_freq[None, :]
            return (jnp.sin(ang), jnp.cos(ang))

        def _apply_rope(x, sin, cos):
            x1 = x[..., ::2]
            x2 = x[..., 1::2]
            r = jnp.stack([x1 * cos - x2 * sin, x1 * sin + x2 * cos], axis=-1)
            return r.reshape(x.shape)

        def _swiglu(x):
            a, b = jnp.split(x, 2, axis=-1)
            return jax.nn.silu(a) * b

        def _rmsnorm(x, w):
            return x * jax.lax.rsqrt(jnp.mean(x * x, axis=-1, keepdims=True) + EPS) * w
        Bb, Tt, C = src.shape
        q = (src @ Wq).reshape(Bb, Tt, H, DH).transpose(0, 2, 1, 3)
        k = (src @ Wk_c @ Wk).reshape(Bb, Tt, H, DH).transpose(0, 2, 1, 3)
        v = (src @ Wv_c @ Wv).reshape(Bb, Tt, H, DH).transpose(0, 2, 1, 3)
        sin, cos = _rope_sincos(Tt, DH)
        q = _apply_rope(q, sin, cos)
        k = _apply_rope(k, sin, cos)
        attn = jnp.einsum('bhqd,bhkd->bhqk', q, k) / np.sqrt(DH).astype(np.float32)
        attn = jax.nn.softmax(attn, axis=-1)
        sa = jnp.einsum('bhqk,bhkd->bhqd', attn, v)
        sa = sa.transpose(0, 2, 1, 3).reshape(Bb, Tt, C) @ Wo
        x = _rmsnorm(src + sa, norm1_w)
        S = Bb * Tt
        flat = x.reshape(S, C)
        shared = _swiglu(flat @ W_shared_in) @ W_shared_out
        g_probs = jax.nn.softmax(flat @ Wg_gate + group_bias, -1)
        g_idx = jnp.argmax(g_probs, axis=-1)
        e_logits = flat @ We_gate + expert_bias
        e_group = jnp.arange(E) // EPG
        in_group = e_group[None, :] == g_idx[:, None]
        e_probs = jax.nn.softmax(jnp.where(in_group, e_logits, -jnp.inf), -1)
        g_prob = jnp.take_along_axis(g_probs, g_idx[:, None], axis=1)
        p_expert = e_probs * g_prob
        topv, topi = jax.lax.top_k(p_expert, TOPK)
        w = jnp.zeros((S, E), flat.dtype).at[jnp.arange(S)[:, None], topi].set(topv)
        h = _swiglu(flat @ W1_shared)
        routed = jnp.zeros_like(shared)
        for e in range(E):
            routed = routed + h @ W2_experts[e] * w[:, e:e + 1]
        out = x + (shared + routed).reshape(Bb, Tt, C)
        return _rmsnorm(out, norm2_w)
    x = x + _L0_xattn_ref(_layernorm(x, axis=-1), ctx_1024, ctx_1024, mask_Bx1xSxS2_bf0, 0, L0_xattn_wq_w, L0_xattn_wq_b, L0_xattn_wk_w, L0_xattn_wk_b, L0_xattn_wv_w, L0_xattn_wv_b, L0_xattn_wo_w, L0_xattn_wo_b, L0_xattn_ln_g, L0_xattn_ln_b)
    x = x + _L0_attn_ref(_layernorm(x, axis=-1), L0_attn_Wq, L0_attn_Wk, L0_attn_Wv, L0_attn_Wo)
    x = x + _L0_ffn_ref(_layernorm(x, axis=-1), L0_ffn_Wq, L0_ffn_Wk_c, L0_ffn_Wv_c, L0_ffn_Wk, L0_ffn_Wv, L0_ffn_Wo, L0_ffn_W_shared_in, L0_ffn_W_shared_out, L0_ffn_W1_shared, L0_ffn_W2_experts, L0_ffn_Wg_gate, L0_ffn_We_gate, L0_ffn_group_bias, L0_ffn_expert_bias, L0_ffn_norm1_w, L0_ffn_norm2_w)
    return x

_drawn_inputs = setup_inputs


def setup_inputs(seed=0):
    import zlib

    import numpy as np

    out = dict(_drawn_inputs(seed))
    spreads = {'L0_xattn_wq_b': (0.0, 0.1),
     'L0_xattn_wk_b': (0.0, 0.1),
     'L0_xattn_wv_b': (0.0, 0.1),
     'L0_xattn_wo_b': (0.0, 0.697),
     'L0_xattn_ln_g': (1.0, 0.2),
     'L0_xattn_ln_b': (0.0, 0.1),
     'L0_ffn_group_bias': (0.0, 0.8),
     'L0_ffn_expert_bias': (0.0, 0.8),
     'L0_ffn_norm1_w': (1.0, 0.2),
     'L0_ffn_norm2_w': (1.0, 0.2)}
    factors = {'L0_ffn_Wq': 8.0,
     'L0_ffn_Wk_c': 8.0,
     'L0_ffn_Wv_c': 8.0,
     'L0_ffn_Wk': 8.0,
     'L0_ffn_Wv': 8.0,
     'L0_ffn_Wo': 8.0,
     'L0_ffn_W_shared_in': 5.621,
     'L0_ffn_W_shared_out': 5.673,
     'L0_ffn_W1_shared': 8.0,
     'L0_ffn_W2_experts': 8.0,
     'L0_ffn_Wg_gate': 8.0,
     'L0_ffn_We_gate': 8.0}
    for name, (base, spread) in spreads.items():
        noise = np.random.default_rng([zlib.crc32(name.encode()), seed]).standard_normal(out[name].shape)
        drawn = base * np.exp(spread * noise) if base else spread * noise
        out[name] = jnp.asarray(drawn.astype(out[name].dtype))
    for name, factor in factors.items():
        out[name] = (out[name] * factor).astype(out[name].dtype)
    return out
```

```python
from contextlib import ExitStack

import numpy as np

import concourse.bass as bass
from concourse import mybir

ALU = mybir.AluOpType
ACT = mybir.ActivationFunctionType
AX = mybir.AxisListType
F32 = mybir.dt.float32
F32R = mybir.dt.float32r
U8 = mybir.dt.uint8
I32 = mybir.dt.int32
U32 = mybir.dt.uint32

P = 128
B, S, D = 8, 64, 256
N = 1601
H, HD = 16, 16
KC = D // P
T = B * S // P
HALVES = 2
TH = T // HALVES
BH = B // HALVES
TOK = TH * P
ROWS = 4
CH_B = 3
TAIL = N - CH_B * ROWS * P
SLOT = ROWS + 1
HROW = D + 4
HID = 512
E = 8
GRP = 2
LN_EPS = 1e-5
RMS_EPS = 1e-6
LOW = -3.0e38
SCALE = 1.0 / float(np.sqrt(HD))
XSCALE = 1.0 / float(np.float32(np.float16(np.sqrt(np.float16(HD)))) + np.float32(1e-8))

CONST = {}
_at = 0
for _name, _width in (("ident", P), ("parity", 2), ("heads", P), ("causal", S), ("cos", S), ("sin", S),
                      ("rot", P), ("side", P), ("tile_of", T), ("iota", E)):
    CONST[_name] = (_at, _at + _width)
    _at += _width
NCONST = _at


def constants():
    c = np.zeros((P, NCONST), np.float32)
    p = np.arange(P)

    def put(name, a):
        lo, hi = CONST[name]
        c[:, lo:hi] = a

    put("ident", np.eye(P))
    put("parity", (p[:, None] // HD) % 2 == np.arange(2)[None, :])
    put("heads", (p[:, None] // HD == p[None, :] // HD) * XSCALE)
    put("causal", np.where(np.arange(S)[None, :] <= p[:, None] % S, 0.0, LOW))
    freq = (1.0 / np.float32(10000.0) ** (np.arange(0, HD, 2, dtype=np.float32) / np.float32(HD))).astype(np.float32)
    ang = np.arange(S, dtype=np.float32)[None, :] * freq[(p % HD) // 2][:, None]
    put("cos", np.cos(ang.astype(np.float32)))
    put("sin", np.sin(ang.astype(np.float32)))
    rot = np.zeros((P, P), np.float32)
    rot[p[1::2], p[0::2]] = -1.0
    rot[p[0::2], p[1::2]] = 1.0
    put("rot", rot)
    put("side", (p[:, None] // (P // B)) % 2 == p[None, :] // S)
    put("tile_of", p[:, None] // (2 * P // B) == np.arange(T)[None, :])
    put("iota", np.arange(E)[None, :])
    return c


NU = 5 + 8
STAGED = 4
GRAM_B = (0, 1)
CROSS_B = (6, 7)
CHAIN_B = 2
DENSE_B = (0, 1, 6, 7)
USES = 8 + TH * (1 + E // 2)


def merged(a, b):
    marks = [((k + 0.5) / len(a), 0, x) for k, x in enumerate(a)] + [((k + 0.5) / len(b), 1, x) for k, x in enumerate(b)]
    return [x for _, _, x in sorted(marks, key=lambda m: m[:2])]


def gram_steps():
    out = [("split", 0), ("split", 1)]
    for b in range(B):
        for c in range(CH_B):
            n = CH_B * b + c
            if n + 2 < CH_B * B:
                out.append(("split", n + 2))
            out.append(("gram", n))
            if b > 1 and c == 0:
                out.append(("cross4", b - 2))
            if b:
                out.append((f"cross{c + 1}", b - 1))
        out.append(("evac", b))
    return out + [("cross4", B - 2)] + [(f"cross{k}", B - 1) for k in (1, 2, 3, 4)]


def chain_steps(g):
    out = [("xo", g), ("turn_z", (g, 0)), ("proj1", g)]
    for kind in range(2):
        n = 4 * g + 2 * kind
        for what in ("score", "turn_p", "values", "turn_o", "project"):
            out += [(what, n), (what, n + 1)]
        if kind == 0:
            out += [("norm2", g), ("turn_z", (g, 1)), ("proj2", g)]
    return out + [("rms1", g), ("turn_x", g), ("gate", g)]


def dense_steps(g):
    out = [("hidden", 8 * g + m) for m in range(8)]
    for t in range(TH * g, TH * g + TH):
        out += [("shared", t)] + [("experts", (t, u)) for u in range(E // 2)] + [("finish", t)]
    return out


def steps_in_order():
    gram = gram_steps()
    cut = gram.index(("cross4", BH - 1)) + 1
    pieces = [("piece", u) for u in range(NU)]
    plan = [("pre", 0)] + gram[:cut]
    plan += merged(chain_steps(0), merged(gram[cut:], pieces[:STAGED]))
    plan += [("xo", 1), pieces[STAGED]]
    dense = dense_steps(0)
    spread = merged(dense[:8], pieces[STAGED + 1:]) + dense[8:]
    return plan + merged(chain_steps(1)[1:], spread) + dense_steps(1)


def layer(nc, d_x, d_ctx, d_mask, d_const, d_w0, d_w1, d_wq, d_wkvc, d_wkv, d_wo, d_gate, d_dense, d_w2,
          d_cols, d_rows, d_ebias, out):
    sb_at = (nc.sbuf_base + 63) // 64 * 64
    where = {}

    def place(name, shape, dt=F32, at=None):
        nonlocal sb_at
        size = int(np.prod(shape[1:])) * (1 if dt == U8 else 4)
        size = (size + 31) // 32 * 32
        if at is None:
            at = sb_at
            sb_at += size
        where[name] = at
        return nc.alloc_sbuf_tensor_at(name, shape, dt, offset=at), at + size

    half_arena = E // 4 * 2 * (HID // P) * 2 * D * 4
    w2, _ = place("w2", [P, E // 2, 2, HID // P, 2 * D], F32R)
    arena = where["w2"]
    ch, nxt = place("ch", [P, CH_B, SLOT, HROW], F32R, at=arena)
    cl, nxt = place("cl", [P, CH_B, SLOT, D], F32R, at=nxt)
    assert nxt <= arena + half_arena
    w0, nxt = place("w0", [P, 4, KC, D], at=arena + half_arena)
    q0T, nxt = place("q0T", [P, KC, T * P], at=nxt)
    ga, nxt = place("ga", [P, 2, 3 * P + 2], at=nxt)
    gb, nxt = place("gb", [P, 2, 2 * P + 2], at=nxt)
    gpre, nxt = place("gpre", [P, 3, P], at=nxt)
    gs, nxt = place("gs", [P, 3, P], at=nxt)
    crep, nxt = place("crep", [P, KC, P], at=nxt)
    cv, nxt = place("cv", [P, KC, D], at=nxt)
    svn, nxt = place("svn", [P, D], at=nxt)
    m1, nxt = place("m1", [P, KC, P], at=nxt)
    mb, nxt = place("mb", [P, KC, P], at=nxt)
    ctxT, nxt = place("ctxT", [P, HALVES, KC, TOK], at=nxt)
    assert nxt <= arena + 2 * half_arena
    dense, _ = place("dense", [P, 2, 5, 1024], F32R)
    raw, _ = place("raw", [P, CH_B * ROWS + 1, D])
    cst, _ = place("cst", [P, NCONST])
    w1, _ = place("w1", [P, 4, KC, D])
    wq, _ = place("wq", [P, KC, D])
    wkvc, _ = place("wkvc", [P, KC, P])
    wkv, _ = place("wkv", [P, D])
    wo, _ = place("wo", [P, KC, D])
    gate, _ = place("gate", [P, KC, GRP + E])
    cols, _ = place("cols", [P, 4])
    rows, _ = place("rows", [P, 6, D])
    ebias, _ = place("ebias", [P, GRP + E])
    X, _ = place("X", [P, T, D])
    Z, _ = place("Z", [P, T, D])
    zT, _ = place("zT", [P, KC, T * P])
    st, _ = place("st", [P, T, 6])
    mv, _ = place("mv", [P, T, 2])
    ve, _ = place("ve", [P, T])
    rstd, _ = place("rstd", [P, T])
    half_exp, _ = place("half_exp", [P, T])
    flag, _ = place("flag", [P, 1])
    flags, _ = place("flags", [P, T])
    nan_a, _ = place("nan_a", [P, T])
    nan_b, _ = place("nan_b", [P, T])
    qp, _ = place("qp", [P, KC * BH, 2, S])
    kT, _ = place("kT", [P, KC, TOK])
    v, _ = place("v", [P, TH, D])
    qs, _ = place("qs", [P, KC * BH, S])
    ks, _ = place("ks", [P, KC * BH, S])
    kvcT, _ = place("kvcT", [P, TOK])
    prob, _ = place("prob", [P, TH, 4, 4, S])
    on = [place(f"on{k}", [P, 2, KC, 4, 2 * HD], at=where["prob"] + k * 4096)[0] for k in range(TH)]
    aT = [place(f"aT{k}", [P, KC, 2, S], at=where["prob"] + k * 4096 + 2048)[0] for k in range(TH)]
    probT, _ = place("probT", [P, TH, 8, P])
    xT, _ = place("xT", [P, KC, TOK], at=where["probT"])
    ropet, _ = place("ropet", [P, KC * BH, S], at=where["probT"] + 4096)
    mx, _ = place("mx", [P, TH, H])
    sm, _ = place("sm", [P, TH, H])
    rs, _ = place("rs", [P, TH, H])
    hT, _ = place("hT", [P, 2, 2, HID // P, TOK], F32R)
    mask, _ = place("mask", [P, B * S * N // P], U8, at=where["hT"])
    stage, _ = place("stage", [P, STAGED, 1024], at=where["hT"])
    sa, _ = place("sa", [P, 2, TOK])
    h32, _ = place("h32", [P, 2, TOK])
    xHL, _ = place("xHL", [P, 2, KC, TOK], F32R)
    sq, _ = place("sq", [P, D])
    ms, _ = place("ms", [P, T])
    lg, _ = place("lg", [P, TH, GRP + E])
    gm, _ = place("gm", [P, TH])
    eg, _ = place("eg", [P, TH, GRP])
    gsum, _ = place("gsum", [P, TH])
    gprob, _ = place("gprob", [P, TH])
    ind, _ = place("ind", [P, TH, GRP])
    off, _ = place("off", [P, TH, GRP])
    em, _ = place("em", [P, TH, E])
    emax, _ = place("emax", [P, TH])
    esum, _ = place("esum", [P, TH])
    erec, _ = place("erec", [P, TH])
    pe8, _ = place("pe8", [P, TH, E])
    top, _ = place("top", [P, TH, 8])
    topi, _ = place("topi", [P, TH, 8], U32)
    topf, _ = place("topf", [P, TH, 8])
    w8a, _ = place("w8a", [P, T, E])
    w8, _ = place("w8", [P, T, E])
    assert sb_at <= nc.sbuf_usable_end, (sb_at, nc.sbuf_usable_end)

    def const(name):
        lo, hi = CONST[name]
        return cst[:, lo:hi]

    ident = const("ident")

    def parity(hl):
        lo, _ = CONST["parity"]
        return cst[:, lo + hl:lo + hl + 1]

    def f32(ap):
        return ap.bitcast(F32)

    def halves(ap):
        return ap.rearrange("p r (h n) -> p r h n", h=KC)

    def raw_piece(u):
        if u < STAGED:
            return stage[:, u, :]
        c = (u - STAGED) % CH_B
        return raw[:, ROWS * c:ROWS * (c + 1), :].rearrange("p r d -> p (r d)")

    def piece(u, part):
        if u < 5:
            return dense[:, part, u, :]
        u -= 5
        return w2[:, u // 2, part, 2 * (u % 2):2 * (u % 2) + 2, :].rearrange("p k n -> p (k n)")

    def dense_use(step, i):
        if step == "hidden":
            return USES * (i // 8) + i % 8
        t, k = (i, 0) if step == "shared" else (i[0], 1 + i[1])
        return USES * (t // TH) + 8 + (1 + E // 2) * (t % TH) + k

    plan = steps_in_order()

    with ExitStack() as stack:
        ps = stack.enter_context(nc.psum_tensor("ps", [P, 8, 512], F32))
        sems = {}

        def sem(name):
            if name not in sems:
                sems[name] = stack.enter_context(nc.semaphore(name))
            return sems[name]

        block = stack.enter_context(nc.Block())

        @block.sync
        def _(sp):
            sp.dma_start(X[:, :, :], d_x).then_inc(sem("x_in"), 16)
            sp.dma_start(cst[:, :], d_const).then_inc(sem("const_in"), 16)
            sp.dma_start(w0[:, :, :, :], d_w0).then_inc(sem("w0_in"), 16)
            for n in range(CH_B * B):
                b, c = divmod(n, CH_B)
                if b:
                    sp.wait_ge(sem("low_done"), n - CH_B + 1)
                sp.dma_start(raw[:, ROWS * c:ROWS * (c + 1), :], d_ctx[b, 0:CH_B * ROWS * P, :].rearrange(
                    "(p r) d -> p r d", r=CH_B * ROWS)[:, c * ROWS:(c + 1) * ROWS, :]).then_inc(sem(f"raw{c}"), 16)
                if c == CH_B - 1:
                    sp.dma_start(raw[0:TAIL, ROWS * CH_B, :], d_ctx[b, CH_B * ROWS * P:N, :]).then_inc(sem(f"raw{c}"), 16)
                if CH_B * BH <= n < CH_B * BH + STAGED:
                    u = n - CH_B * BH
                    sp.wait_ge(sem("flag"), 1)
                    sp.dma_start(raw_piece(u), d_dense[:, u, :]).then_inc(sem(f"staged{u}"), 16)
            for u in range(STAGED, NU):
                if u < STAGED + CH_B:
                    sp.wait_ge(sem("low_done"), CH_B * (B - 1) + u - STAGED + 1)
                else:
                    sp.wait_ge(sem("piece_low"), u - CH_B + 1)
                src = d_dense[:, u, :] if u < 5 else d_w2[:, u - 5, :]
                sp.dma_start(raw_piece(u), src).then_inc(sem(f"raw{(u - STAGED) % CH_B}"), 16)
            for t in range(T):
                sp.wait_ge(sem("x3"), t + 1)
                sp.dma_start(out[t * P:(t + 1) * P, :], X[:, t, :]).then_inc(sem("stored"), 16)
            sp.wait_ge(sem("stored"), 16 * T)

        def chunk_landed(eng, n):
            b, c = divmod(n, CH_B)
            eng.wait_ge(sem(f"raw{c}"), (32 if c == CH_B - 1 else 16) * (b + 1))

        def piece_landed(eng, u):
            if u < STAGED:
                eng.wait_ge(sem(f"staged{u}"), 16)
            else:
                k, c = divmod(u - STAGED, CH_B)
                eng.wait_ge(sem(f"raw{c}"), (32 if c == CH_B - 1 else 16) * B + 16 * (k + 1))

        @block.gpsimd
        def _(pool):
            ones = f32(ch[:, :, :, :]).rearrange("p c r (h n) -> p c r h n", h=KC)
            for c in range(CH_B):
                pool.memset(ones[:, c, :, :, P:P + 2], 1.0).then_inc(sem("ones"), 1)
            pool.memset(gpre[:, 2, :], 0.0).then_inc(sem("ones"), 1)
            pool.memset(half_exp[:, :], -0.5).then_inc(sem("ones"), 1)
            pool.wait_ge(sem("ones"), CH_B + 2)
            pool.wait_ge(sem("const_in"), 16)
            roots = [0]

            def inverse_roots(lo, hi):
                roots[0] += 1
                pool.wait_ge(sem("var"), roots[0])
                pool.tensor_tensor(rstd[:, lo:hi], ve[:, lo:hi], half_exp[:, lo:hi], ALU.pow).then_inc(sem("rstd"), 1)

            for step, i in plan:
                if step == "pre":
                    inverse_roots(0, T)
                elif step == "cross1":
                    pool.wait_ge(sem("ga"), i + 1)
                    pool.wait_ge(sem("gb"), i + 1)
                    if i:
                        pool.wait_ge(sem("gs"), i)
                    pool.tensor_tensor(gpre[:, 0, :], ga[:, i % 2, 0:P], ga[:, i % 2, 2 * P + 2:3 * P + 2], ALU.add)
                    pool.tensor_tensor(gpre[:, 1, :], gb[:, i % 2, 0:P], gb[:, i % 2, P + 2:2 * P + 2],
                                       ALU.add).then_inc(sem("gpre"), 1)
                elif step == "xo":
                    inverse_roots(TH * i, TH * i + TH)
                    inverse_roots(TH * i, TH * i + TH)
                elif step in ("norm2", "rms1"):
                    inverse_roots(TH * i, TH * i + TH)
                elif step == "proj2":
                    for n, src in enumerate((qs, ks)):
                        pool.wait_ge(sem("rot"), 2 * i + n + 1)
                        pool.tensor_tensor(src[:, :, :], src[:, :, :],
                                           const("cos").unsqueeze(1).to_broadcast([P, KC * BH, S]),
                                           ALU.mult).then_inc(sem("by_cos"), 1)
                elif step == "piece":
                    pool.wait_ge(sem("piece_high"), i + 1)
                    pool.tensor_tensor(piece(i, 1), raw_piece(i), f32(piece(i, 0)), ALU.subtract).then_inc(sem("piece_low"), 1)
                elif step == "hidden":
                    m = i % 8
                    pool.wait_ge(sem("h_high"), i + 1)
                    pool.tensor_tensor(hT[:, m // 4, 1, m % 4, :], h32[:, m % 2, :], f32(hT[:, m // 4, 0, m % 4, :]),
                                       ALU.subtract).then_inc(sem("h_low"), 1)
                elif step == "finish":
                    inverse_roots(i, i + 1)

        @block.scalar
        def _(act):
            act.dma_start(cols[:, :], d_cols).then_inc(sem("cols_in"), 16)
            act.dma_start(rows[:, :, :], d_rows.partition_broadcast(P)).then_inc(sem("rows_in"), 16)
            act.dma_start(mask[:, :], d_mask).then_inc(sem("mask_in"), 16)
            act.dma_start(w1[:, :, :, :], d_w1).then_inc(sem("w_in"), 16)
            act.dma_start(wq[:, :, :], d_wq).then_inc(sem("w_in"), 16)
            act.dma_start(wkvc[:, :, :], d_wkvc).then_inc(sem("w_in"), 16)
            act.dma_start(wkv[:, :], d_wkv).then_inc(sem("w_in"), 16)
            act.dma_start(wo[:, :, :], d_wo).then_inc(sem("w_in"), 16)
            act.dma_start(gate[:, :, :], d_gate).then_inc(sem("w_in"), 16)
            act.dma_start(ebias[:, :], d_ebias.partition_broadcast(P)).then_inc(sem("w_in"), 16)
            squares = [0]

            def copy(dst, src, name):
                act.activation(dst, src, ACT.Copy).then_inc(sem(name), 1)

            def z_out(tiles, bank):
                lo, hi = tiles
                copy(zT[:, :, lo * P:hi * P].rearrange("p k (t c) -> p t k c", c=P),
                     ps[:, bank, 0:(hi - lo) * D].rearrange("p (t k c) -> p t k c", k=KC, c=P), "zT")

            def mean_square(t):
                if squares[0]:
                    act.wait_ge(sem("ms"), squares[0])
                squares[0] += 1
                act.activation(sq[:, :], Z[:, t, :], ACT.Square, scale=D ** -0.5,
                               accum_out=ms[:, t:t + 1]).then_inc(sem("ms"), 1)

            for step, i in plan:
                if step == "pre":
                    act.wait_ge(sem("const_in"), 16)
                    act.wait_ge(sem("cols_in"), 16)
                    act.wait_ge(sem("turned"), 1)
                    z_out((0, TH), CROSS_B[0])
                    act.wait_ge(sem("turned"), 2)
                    z_out((TH, T), CROSS_B[1])
                    for ob in range(KC):
                        act.wait_ge(sem("q0"), ob + 1)
                        act.activation(q0T[:, ob, :], ps[:, CHAIN_B + ob, :], ACT.Identity,
                                       bias=cols[:, ob:ob + 1]).then_inc(sem("q0T"), 1)
                elif step == "split":
                    c = i % CH_B
                    chunk_landed(act, i)
                    if i >= CH_B:
                        act.wait_ge(sem("gram_chunk"), i - CH_B + 1)
                    if i == 0:
                        act.wait_ge(sem("ones"), CH_B)
                    for p, lo, hi in [(P, 0, ROWS)] + ([(TAIL, ROWS, ROWS + 1)] if c == CH_B - 1 else []):
                        last = act.activation(halves(ch[0:p, c, lo:hi, :])[:, :, :, 0:P],
                                              halves(raw[0:p, ROWS * c + lo:ROWS * c + hi, :]), ACT.Copy)
                    last.then_inc(sem("high_done"), 1)
                elif step == "evac":
                    act.wait_ge(sem("gram_chunk"), CH_B * (i + 1))
                    if i >= 2:
                        act.wait_ge(sem("cv"), i - 1)
                    copy(ga[:, i % 2, :], ps[:, GRAM_B[0], 0:3 * P + 2], "ga")
                elif step == "cross1":
                    act.wait_ge(sem("ga"), i + 1)
                    act.wait_ge(sem("gb"), i + 1)
                    if i:
                        act.wait_ge(sem("sv"), i)
                    for k, src in ((0, ga), (1, gb)):
                        last = act.activation(crep[:, k, :], ident, ACT.Identity, scale=0.0,
                                              bias=src[:, i % 2, P:P + 1])
                    last.then_inc(sem("crep"), 1)
                elif step == "cross4":
                    act.wait_ge(sem("ctx"), i + 1)
                    copy(ctxT[:, i // BH, :, (i % BH) * S:(i % BH + 1) * S],
                         ps[:, CROSS_B[1], 0:KC * S].rearrange("p (k n) -> p k n", k=KC), "ctxT")
                elif step == "turn_z":
                    g, k = i
                    act.wait_ge(sem("turned"), 3 + 3 * g + k)
                    z_out((TH * g, TH * g + TH), CHAIN_B + 1)
                elif step == "proj1":
                    act.wait_ge(sem("k1"), i + 1)
                    if i:
                        act.wait_ge(sem("scores"), 4 * i)
                    copy(kT[:, :, :], ps[:, CHAIN_B + 3, :].rearrange("p (k n) -> p k n", k=KC), "kT")
                    act.wait_ge(sem("v1"), i + 1)
                    if i:
                        act.wait_ge(sem("pv"), 4 * i)
                    copy(v[:, :, :], ps[:, CHAIN_B, :].rearrange("p (t n) -> p t n", t=TH), "v")
                elif step == "score":
                    act.wait_ge(sem("shifted"), i + 1)
                    act.activation(prob[:, i % 2, :, :, :], prob[:, i % 2, :, :, :], ACT.Exp,
                                   scale=SCALE).then_inc(sem("prob"), 1)
                elif step == "turn_p":
                    for j in range(2):
                        act.wait_ge(sem("p_turned"), 2 * i + j + 1)
                        if i >= 2:
                            act.wait_ge(sem("pv"), i - 1)
                        copy(probT[:, i % 2, 4 * j:4 * j + 4, :],
                             ps[:, CHAIN_B + 2 * (i % 2) + j, :].rearrange("p (c n) -> p c n", n=P), "probT")
                elif step == "proj2":
                    act.wait_ge(sem("q2"), i + 1)
                    copy(qs[:, :, :], ps[:, CHAIN_B, :].rearrange("p (c n) -> p c n", n=S), "qs")
                    act.wait_ge(sem("kvc"), i + 1)
                    if i:
                        act.wait_ge(sem("v2"), i)
                    copy(kvcT[:, :], ps[:, CHAIN_B + 1, 0:TOK], "kvcT")
                    act.wait_ge(sem("k2"), i + 1)
                    copy(ks[:, :, :], ps[:, CHAIN_B + 3, :].rearrange("p (c n) -> p c n", n=S), "ks")
                    act.wait_ge(sem("v2"), i + 1)
                    act.wait_ge(sem("pv"), 4 * i + 2)
                    copy(v[:, :, :], ps[:, CHAIN_B + 1, :].rearrange("p (t n) -> p t n", t=TH), "v")
                elif step == "rms1":
                    act.wait_ge(sem("s2"), TH * i + TH)
                    for t in range(TH * i, TH * i + TH):
                        mean_square(t)
                elif step == "turn_x":
                    act.wait_ge(sem("turned"), 5 + 3 * i)
                    copy(xT[:, :, :].rearrange("p k (t c) -> p t k c", c=P),
                         ps[:, CHAIN_B, :].rearrange("p (t k c) -> p t k c", k=KC, c=P), "xT")
                    act.wait_ge(sem("xT"), i + 1)
                    if i:
                        act.wait_ge(sem("products"), USES * (i - 1) + 8)
                    copy(xHL[:, 0, :, :], xT[:, :, :], "xH")
                elif step == "gate":
                    act.wait_ge(sem("gates_a"), i + 1)
                    act.activation(eg[:, :, :], eg[:, :, :], ACT.Exp).then_inc(sem("eg"), 1)
                    act.wait_ge(sem("gates_b"), i + 1)
                    act.activation(pe8[:, :, :], em[:, :, :], ACT.Exp).then_inc(sem("ee"), 1)
                elif step == "piece":
                    piece_landed(act, i)
                    if 5 <= i < 9:
                        act.wait_ge(sem("gram_chunk"), CH_B * B)
                    if i >= 9:
                        act.wait_ge(sem("xo"), HALVES)
                    copy(piece(i, 0), raw_piece(i), "piece_high")
                elif step == "hidden":
                    use = dense_use(step, i)
                    m = i % 8
                    act.wait_ge(sem("products"), use + 1)
                    if i >= 2:
                        act.wait_ge(sem("h_high"), i - 1)
                    act.activation(sa[:, m % 2, :], ps[:, DENSE_B[use % 4], 0:TOK], ACT.Silu).then_inc(sem("silu"), 1)
                    act.wait_ge(sem("taken"), use + 1)
                    if m == 0 and i:
                        act.wait_ge(sem("products"), USES)
                    copy(hT[:, m // 4, 0, m % 4, :], h32[:, m % 2, :], "h_high")
                elif step == "finish":
                    act.wait_ge(sem("taken"), dense_use("experts", (i, E // 2 - 1)) + 1)
                    mean_square(i)

        @block.tensor
        def _(pe):
            def mm(o, l, r, start, stop, check=True):
                return pe.matmul(o, l, r, start=start, stop=stop, skip_group_check=not check)

            def turn(o, src):
                return pe.transpose(o, src, ident)

            def turn_rows(lo_tile, bank):
                for t in range(TH):
                    for k in range(KC):
                        last = turn(ps[:, bank, t * D + k * P:t * D + (k + 1) * P], Z[:, lo_tile + t, k * P:(k + 1) * P])
                last.then_inc(sem("turned"), 1)

            def gram_tile(slot, r, p, first, last):
                row = ch[0:p, slot, r, :]
                h0, h1 = row[:, 0:P], row[:, P + 2:2 * P + 2]
                l0, l1 = cl[0:p, slot, r, 0:P], cl[0:p, slot, r, P:2 * P]
                a, b = ps[:, GRAM_B[0], :], ps[:, GRAM_B[1], :]
                mm(a[:, 0:2 * P + 2], h0, row[:, 0:2 * P + 2], first, False, False)
                mm(a[:, P + 2:2 * P + 2], h0, l1, False, False, False)
                mm(a[:, P:2 * P + 2], l0, row[:, P:2 * P + 2], False, False, False)
                mm(a[:, 2 * P + 2:3 * P + 2], l0, h0, False, last, False)
                mm(b[:, 0:P + 2], h1, row[:, P + 2:2 * P + 4], first, False, False)
                return mm(b[:, P:2 * P + 2], l1, row[:, P:2 * P + 2], False, last, False)

            def split_products(o, pairs):
                todo = [(l[a], r[c]) for l, r in pairs for a, c in ((0, 0), (0, 1), (1, 0))]
                for k, (l, r) in enumerate(todo):
                    last = mm(o, l, r, k == 0, k == len(todo) - 1)
                return last

            def project(bank, width, weights, rows_, name):
                for ob in range(KC):
                    for k in range(KC):
                        last = mm(ps[:, bank, ob * width:(ob + 1) * width], weights[:, k, ob * P:(ob + 1) * P],
                                  rows_[k], k == 0, k == KC - 1)
                last.then_inc(sem(name), 1)

            pe.wait_ge(sem("const_in"), 16)
            for step, i in plan:
                if step == "pre":
                    pe.wait_ge(sem("z"), 1)
                    turn_rows(0, CROSS_B[0])
                    turn_rows(TH, CROSS_B[1])
                    pe.wait_ge(sem("w0_in"), 16)
                    pe.wait_ge(sem("zT"), 2)
                    for ob in range(KC):
                        for k in range(KC):
                            last = mm(ps[:, CHAIN_B + ob, :], w0[:, 0, k, ob * P:(ob + 1) * P], zT[:, k, :],
                                      k == 0, k == KC - 1)
                        last.then_inc(sem("q0"), 1)
                    pe.wait_ge(sem("flag"), 1)
                    mm(ps[:, CHAIN_B + 2, 0:T], const("side"), flags[:, :], True, True).then_inc(sem("flags"), 1)
                elif step == "gram":
                    b, c = divmod(i, CH_B)
                    pe.wait_ge(sem("high_done"), i + 1)
                    pe.wait_ge(sem("low_done"), i + 1)
                    if b and c == 0:
                        pe.wait_ge(sem("ga"), b)
                        pe.wait_ge(sem("gb"), b)
                    for r in range(ROWS):
                        last = gram_tile(c, r, P, c == 0 and r == 0, False)
                    if c == CH_B - 1:
                        last = gram_tile(c, ROWS, TAIL, False, True)
                    last.then_inc(sem("gram_chunk"), 1)
                elif step == "cross1":
                    s = i % 2
                    pe.wait_ge(sem("ga"), i + 1)
                    pe.wait_ge(sem("gb"), i + 1)
                    if i:
                        pe.wait_ge(sem("mb"), i)
                    bank = ps[:, CROSS_B[0], :]
                    turn(bank[:, 0:P], ga[:, s, 2 * P + 2:3 * P + 2])
                    turn(bank[:, P:2 * P], gb[:, s, P + 2:2 * P + 2])
                    turn(bank[:, 2 * P:3 * P], ga[:, s, P + 2:2 * P + 2]).then_inc(sem("g_turned"), 1)
                elif step == "cross2":
                    s = i % 2
                    pe.wait_ge(sem("gs"), i + 1)
                    if i:
                        pe.wait_ge(sem("ctxT"), i)
                    lhs = ((gs[:, 0, :], gs[:, 2, :]), (ga[:, s, P + 2:2 * P + 2], gs[:, 1, :]))
                    for ib in range(KC):
                        for k in range(KC):
                            last = mm(ps[:, CROSS_B[1], ib * D:(ib + 1) * D], lhs[ib][k], w0[:, 2, k, :],
                                      k == 0, k == KC - 1)
                    last.then_inc(sem("u"), 1)
                    pe.wait_ge(sem("crep"), i + 1)
                    for k in range(KC):
                        last = mm(ps[:, CROSS_B[0], 0:D], crep[:, k, :], w0[:, 2, k, :], k == 0, k == KC - 1)
                    last.then_inc(sem("sv"), 1)
                elif step == "cross3":
                    pe.wait_ge(sem("cv"), i + 1)
                    for ob in range(KC):
                        for k in range(KC):
                            last = mm(ps[:, CROSS_B[0], D + ob * P:D + (ob + 1) * P], w0[:, 1, k, ob * P:(ob + 1) * P],
                                      cv[:, k, ob * P:(ob + 1) * P], k == 0, k == KC - 1)
                    last.then_inc(sem("kv"), 1)
                elif step == "cross4":
                    pe.wait_ge(sem("mb"), i + 1)
                    pe.wait_ge(sem("q0T"), KC)
                    for ob in range(KC):
                        last = mm(ps[:, CROSS_B[1], ob * S:(ob + 1) * S], mb[:, ob, :], q0T[:, ob, i * S:(i + 1) * S],
                                  True, True)
                    last.then_inc(sem("ctx"), 1)
                elif step == "xo":
                    pe.wait_ge(sem("ctxT"), BH * (i + 1))
                    if i:
                        pe.wait_ge(sem("xT"), i)
                    for t in range(TH):
                        for ob in range(KC):
                            last = mm(ps[:, CHAIN_B, t * D:(t + 1) * D], ctxT[:, i, ob, t * P:(t + 1) * P],
                                      w0[:, 3, ob, :], ob == 0, ob == KC - 1)
                    last.then_inc(sem("xo"), 1)
                elif step == "turn_z":
                    g, k = i
                    pe.wait_ge(sem("z"), 2 + 3 * g + k)
                    if g and k == 0:
                        pe.wait_ge(sem("logits"), g)
                    if k:
                        pe.wait_ge(sem("x2"), TH * g + TH)
                    turn_rows(TH * g, CHAIN_B + 1)
                elif step == "proj1":
                    pe.wait_ge(sem("w_in"), 16 * 7)
                    pe.wait_ge(sem("zT"), 3 + 2 * i)
                    if i:
                        pe.wait_ge(sem("aT"), 4 * i)
                        pe.wait_ge(sem("s2"), TH * i)
                    else:
                        pe.wait_ge(sem("nan"), 1)
                    z = [zT[:, k, i * TOK:(i + 1) * TOK] for k in range(KC)]
                    project(CHAIN_B + 2, TOK, w1[:, 0, :, :], z, "q1")
                    project(CHAIN_B + 3, TOK, w1[:, 1, :, :], z, "k1")
                    pe.wait_ge(sem("y"), i + 1)
                    for t in range(TH):
                        for k in range(KC):
                            last = mm(ps[:, CHAIN_B, t * D:(t + 1) * D], zT[:, k, (TH * i + t) * P:(TH * i + t + 1) * P],
                                      w1[:, 2, k, :], k == 0, k == KC - 1)
                    last.then_inc(sem("v1"), 1)
                elif step == "score":
                    g, kind = i // 4, i // 2 % 2
                    pe.wait_ge(sem("qp"), 2 * g + kind + 1)
                    pe.wait_ge(sem("v"), 2 * g + kind + 1)
                    if kind:
                        pe.wait_ge(sem("roped"), 2 * g + 2)
                    else:
                        pe.wait_ge(sem("kT"), g + 1)
                    for phase in range(2):
                        if phase:
                            pe.wait_ge(sem("scores_a"), i + 1)
                        for j in range(KC):
                            for bb in range(2):
                                b = 2 * (i % 2) + bb
                                for r in (phase, 2 + phase):
                                    col = ((r % 2) * 4 + 2 * j + bb) * S
                                    last = mm(ps[:, CHAIN_B + 2 * (i % 2) + r // 2, col:col + S],
                                              qp[32 * r:32 * r + 32, j * BH + b, :, :].rearrange("p h q -> p (h q)"),
                                              kT[32 * r:32 * r + 32, j, b * S:(b + 1) * S], True, True)
                        last.then_inc(sem("scores" if phase else "scores_a"), 1)
                elif step == "turn_p":
                    pe.wait_ge(sem("prob"), i + 1)
                    for half in range(2):
                        for c in range(4):
                            r, j = divmod(4 * half + c, 2)
                            last = turn(ps[:, CHAIN_B + 2 * (i % 2) + half, c * P:(c + 1) * P],
                                        prob[:, i % 2, r, 2 * j:2 * j + 2, :].rearrange("p b k -> p (b k)"))
                        last.then_inc(sem("p_turned"), 1)
                elif step == "values":
                    pe.wait_ge(sem("probT"), 2 * i + 2)
                    for r in range(4):
                        for j in range(KC):
                            for bb in range(2):
                                col = (2 * r + j) * 2 * HD
                                f = j * P + 32 * r
                                last = mm(ps[:, CHAIN_B + 2 * (i % 2) + bb, col:col + 2 * HD],
                                          probT[bb * S:bb * S + S, i % 2, 2 * r + j, :],
                                          v[bb * S:bb * S + S, i % 2, f:f + 2 * HD], True, True)
                    last.then_inc(sem("pv"), 1)
                elif step == "turn_o":
                    pe.wait_ge(sem("on"), i + 1)
                    for bb in range(2):
                        for j in range(KC):
                            c = 2 * j + bb
                            last = turn(ps[:, CHAIN_B + 2 * (i % 2), c * P:(c + 1) * P],
                                        on[i % 2][:, bb, j, :, :].rearrange("p i d -> p (i d)"))
                    last.then_inc(sem("o_turned"), 1)
                elif step == "project":
                    pe.wait_ge(sem("aT"), i + 1)
                    w = wo if i // 2 % 2 else w1[:, 3, :, :]
                    for j in range(KC):
                        last = mm(ps[:, CHAIN_B + 2 * (i % 2) + 1, 0:D], aT[i % 2][:, j, :, :].rearrange("p b q -> p (b q)"),
                                  w[:, j, :], j == 0, j == KC - 1)
                    last.then_inc(sem("ao"), 1)
                elif step == "proj2":
                    pe.wait_ge(sem("zT"), 4 + 2 * i)
                    z = [zT[:, k, i * TOK:(i + 1) * TOK] for k in range(KC)]
                    project(CHAIN_B, TOK, wq, z, "q2")
                    for k in range(KC):
                        last = mm(ps[:, CHAIN_B + 1, 0:TOK], wkvc[:, k, :], z[k], k == 0, k == KC - 1)
                    last.then_inc(sem("kvc"), 1)
                    pe.wait_ge(sem("qs"), i + 1)
                    mm(ps[:, CHAIN_B + 2, :], const("rot"), qs[:, :, :].rearrange("p c n -> p (c n)"),
                       True, True).then_inc(sem("rot"), 1)
                    pe.wait_ge(sem("kvcT"), i + 1)
                    for ob in range(KC):
                        last = mm(ps[:, CHAIN_B + 3, ob * TOK:(ob + 1) * TOK], wkv[0:P // 2, ob * P:(ob + 1) * P],
                                  kvcT[0:P // 2, :], True, True)
                    last.then_inc(sem("k2"), 1)
                    for t in range(TH):
                        last = mm(ps[:, CHAIN_B + 1, t * D:(t + 1) * D], kvcT[P // 2:P, t * P:(t + 1) * P],
                                  wkv[P // 2:P, :], True, True)
                    last.then_inc(sem("v2"), 1)
                    pe.wait_ge(sem("ks"), i + 1)
                    mm(ps[:, CHAIN_B, :], const("rot"), ks[:, :, :].rearrange("p c n -> p (c n)"),
                       True, True).then_inc(sem("rot"), 1)
                elif step == "turn_x":
                    pe.wait_ge(sem("z"), 4 + 3 * i)
                    turn_rows(TH * i, CHAIN_B)
                elif step == "gate":
                    pe.wait_ge(sem("xT"), i + 1)
                    pe.wait_ge(sem("s2"), TH * i + TH)
                    for t in range(TH):
                        for k in range(KC):
                            last = mm(ps[:, CHAIN_B + 1, t * 16:t * 16 + GRP + E], xT[:, k, t * P:(t + 1) * P],
                                      gate[:, k, :], k == 0, k == KC - 1)
                    last.then_inc(sem("gates"), 1)
                elif step == "hidden":
                    use = dense_use(step, i)
                    m = i % 8
                    if m == 0:
                        pe.wait_ge(sem("xL"), i // 8 + 1)
                        pe.wait_ge(sem("piece_low"), 4)
                    if use == 0:
                        pe.wait_ge(sem("ga"), B)
                        pe.wait_ge(sem("gb"), B)
                        pe.wait_ge(sem("mb"), B)
                        pe.wait_ge(sem("ctxT"), B)
                    if use >= 4:
                        pe.wait_ge(sem("taken"), use - 3)
                    for side in range(2):
                        col = side * HID + (m % 4) * P
                        last = split_products(
                            ps[:, DENSE_B[use % 4], side * TOK:(side + 1) * TOK],
                            [([dense[:, a, 2 * (m // 4) + k, col:col + P] for a in range(2)],
                              [xHL[:, a, k, :] for a in range(2)]) for k in range(KC)])
                    last.then_inc(sem("products"), 1)
                elif step == "shared":
                    use = dense_use(step, i)
                    tok = slice((i % TH) * P, (i % TH + 1) * P)
                    pe.wait_ge(sem("h_low"), 8 * (i // TH) + 8)
                    pe.wait_ge(sem("piece_low"), 5)
                    pe.wait_ge(sem("taken"), use - 3)
                    split_products(
                        ps[:, DENSE_B[use % 4], 0:D],
                        [([hT[:, 0, a, k, tok] for a in range(2)], [dense[:, a, 4, k * D:(k + 1) * D] for a in range(2)])
                         for k in range(HID // P)]).then_inc(sem("products"), 1)
                elif step == "experts":
                    use = dense_use(step, i)
                    t, u = i
                    tok = slice((t % TH) * P, (t % TH + 1) * P)
                    pe.wait_ge(sem("piece_low"), 5 + 2 * u + 2)
                    pe.wait_ge(sem("taken"), use - 3)
                    split_products(
                        ps[:, DENSE_B[use % 4], :],
                        [([hT[:, 1, a, k, tok] for a in range(2)], [w2[:, u, a, k, :] for a in range(2)])
                         for k in range(HID // P)]).then_inc(sem("products"), 1)

        @block.vector
        def _(dve):
            steps = [0]
            roots = [0]
            squares = [0]
            zs = [0]

            def link(ins):
                steps[0] += 1
                ins.then_inc(sem("dve_step"), 1)
                dve.wait_ge(sem("dve_step"), steps[0])

            def roots_of(src, eps, lo, hi):
                roots[0] += 1
                dve.tensor_scalar(ve[:, lo:hi], src, eps, None, ALU.add).then_inc(sem("var"), 1)
                dve.wait_ge(sem("rstd"), roots[0])

            def normalise(src, dst, lo, hi):
                for t in range(lo, hi):
                    last = dve.bn_stats(st[:, t, :], src[:, t, :])
                link(last)
                for t in range(lo, hi):
                    last = dve.bn_aggr(mv[:, t, :], st[:, t, :])
                link(last)
                roots_of(mv[:, lo:hi, 1], LN_EPS, lo, hi)
                for t in range(lo, hi):
                    last = dve.tensor_scalar(dst[:, t, :], src[:, t, :], mv[:, t, 0:1], rstd[:, t:t + 1],
                                             ALU.subtract, ALU.mult)
                return last

            def rms_scaled(w, lo, hi):
                squares[0] += hi - lo
                dve.wait_ge(sem("ms"), squares[0])
                roots_of(ms[:, lo:hi], RMS_EPS, lo, hi)
                for t in range(lo, hi):
                    last = dve.scalar_tensor_tensor(out=Z[:, t, :], in0=Z[:, t, :], scalar=rstd[:, t:t + 1],
                                                    in1=rows[:, w, :], op0=ALU.mult, op1=ALU.mult)
                return last

            def to_z(ins):
                zs[0] += 1
                ins.then_inc(sem("z"), 1)
                dve.wait_ge(sem("z"), zs[0])

            def queries(src):
                for hl in range(2):
                    last = dve.tensor_scalar(qp[:, :, hl, :], src, parity(hl), None, ALU.mult)
                last.then_inc(sem("qp"), 1)

            def gates(g):
                n = TH
                got = ps[:, CHAIN_B + 1, 0:16 * TH].rearrange("p (t c) -> p t c", c=16)[:, :, 0:GRP + E]
                dve.tensor_tensor(lg[:, :, :], got, ebias[:, :].unsqueeze(1).to_broadcast([P, n, GRP + E]),
                                  ALU.add).then_inc(sem("logits"), 1)
                dve.wait_ge(sem("logits"), g + 1)
                link(dve.tensor_reduce(gm[:, :], lg[:, :, 0:GRP], AX.X, ALU.max))
                dve.tensor_tensor(eg[:, :, :], lg[:, :, 0:GRP], gm[:, :].unsqueeze(2).to_broadcast([P, n, GRP]),
                                  ALU.subtract).then_inc(sem("gates_a"), 1)
                dve.wait_ge(sem("eg"), g + 1)
                link(dve.tensor_reduce(gsum[:, :], eg[:, :, :], AX.X, ALU.add))
                link(dve.reciprocal(gprob[:, :], gsum[:, :]))
                link(dve.tensor_tensor(ind[:, :, 0], eg[:, :, 0], eg[:, :, 1], ALU.is_ge))
                link(dve.tensor_scalar(ind[:, :, 1], ind[:, :, 0], -1.0, 1.0, ALU.mult, ALU.add))
                link(dve.tensor_scalar(off[:, :, :], ind[:, :, :], -LOW, LOW, ALU.mult, ALU.add))
                by_group = lg[:, :, GRP:GRP + E].rearrange("p t (g e) -> p t g e", g=GRP)
                em4 = em[:, :, :].rearrange("p t (g e) -> p t g e", g=GRP)
                wide = [P, n, GRP, E // GRP]
                link(dve.tensor_tensor(em4, by_group, ind[:, :, :].unsqueeze(3).to_broadcast(wide), ALU.mult))
                link(dve.tensor_tensor(em4, em4, off[:, :, :].unsqueeze(3).to_broadcast(wide), ALU.add))
                link(dve.tensor_reduce(emax[:, :], em[:, :, :], AX.X, ALU.max))
                dve.tensor_tensor(em[:, :, :], em[:, :, :], emax[:, :].unsqueeze(2).to_broadcast([P, n, E]),
                                  ALU.subtract).then_inc(sem("gates_b"), 1)
                dve.wait_ge(sem("ee"), g + 1)
                link(dve.tensor_reduce(esum[:, :], pe8[:, :, :], AX.X, ALU.add))
                link(dve.reciprocal(erec[:, :], esum[:, :]))
                link(dve.tensor_tensor(erec[:, :], erec[:, :], gprob[:, :], ALU.mult))
                link(dve.tensor_tensor(pe8[:, :, :], pe8[:, :, :], erec[:, :].unsqueeze(2).to_broadcast([P, n, E]), ALU.mult))
                for t in range(n):
                    last = dve.max(top[:, t, :], pe8[:, t, :])
                link(last)
                for t in range(n):
                    last = dve.max_index(topi[:, t, :], top[:, t, :], pe8[:, t, :])
                link(last)
                link(dve.tensor_copy(topf[:, :, :], topi[:, :, :]))
                for t in range(n):
                    for k, dst in enumerate((w8a, w8)):
                        last = dve.tensor_scalar(dst[:, TH * g + t, :], const("iota"), topf[:, t, k:k + 1],
                                                 top[:, t, k:k + 1], ALU.is_equal, ALU.mult)
                link(last)
                both = slice(TH * g, TH * g + TH)
                link(dve.tensor_tensor(w8[:, both, :], w8[:, both, :], w8a[:, both, :], ALU.add))

            for step, i in plan:
                if step == "pre":
                    dve.wait_ge(sem("x_in"), 16)
                    dve.wait_ge(sem("const_in"), 16)
                    dve.wait_ge(sem("cols_in"), 16)
                    dve.wait_ge(sem("ones"), CH_B + 2)
                    to_z(normalise(X, Z, 0, T))
                    dve.wait_ge(sem("mask_in"), 16)
                    link(dve.tensor_reduce(flag[:, 0:1], mask[:, :].bitcast(I32), AX.X, ALU.max))
                    dve.tensor_scalar(flags[:, :], const("tile_of"), flag[:, 0:1], 0.0, ALU.mult, ALU.is_gt).then_inc(sem("flag"), 1)
                    dve.wait_ge(sem("rows_in"), 16)
                    dve.tensor_tensor(X[:, :, :], X[:, :, :], rows[:, 1, :].unsqueeze(1).to_broadcast([P, T, D]), ALU.add)
                    dve.wait_ge(sem("flags"), 1)
                    dve.tensor_scalar(nan_a[:, :], ps[:, CHAIN_B + 2, 0:T], -LOW, -LOW, ALU.mult, ALU.mult).then_inc(sem("nan"), 1)
                    dve.wait_ge(sem("nan"), 1)
                    link(dve.tensor_tensor(nan_b[:, :], nan_a[:, :], nan_a[:, :], ALU.subtract))
                    dve.wait_ge(sem("turned"), 2)
                    for t in range(T):
                        last = dve.scalar_tensor_tensor(out=Z[:, t, :], in0=Z[:, t, :], scalar=nan_b[:, t:t + 1],
                                                        in1=rows[:, 2, :], op0=ALU.add, op1=ALU.add)
                    link(last)
                elif step == "split":
                    c = i % CH_B
                    dve.wait_ge(sem("high_done"), i + 1)
                    if i >= CH_B:
                        dve.wait_ge(sem("gram_chunk"), i - CH_B + 1)
                    for p, lo, hi in [(P, 0, ROWS)] + ([(TAIL, ROWS, ROWS + 1)] if c == CH_B - 1 else []):
                        last = dve.tensor_tensor(halves(cl[0:p, c, lo:hi, :]),
                                                 halves(raw[0:p, ROWS * c + lo:ROWS * c + hi, :]),
                                                 halves(f32(ch[0:p, c, lo:hi, :]))[:, :, :, 0:P], ALU.subtract)
                    last.then_inc(sem("low_done"), 1)
                elif step == "evac":
                    dve.wait_ge(sem("gram_chunk"), CH_B * (i + 1))
                    if i >= 2:
                        dve.wait_ge(sem("gpre"), i - 1)
                        dve.wait_ge(sem("crep"), i - 1)
                    dve.tensor_copy(gb[:, i % 2, :], ps[:, GRAM_B[1], 0:2 * P + 2]).then_inc(sem("gb"), 1)
                elif step == "cross1":
                    dve.wait_ge(sem("g_turned"), i + 1)
                    dve.wait_ge(sem("gpre"), i + 1)
                    if i:
                        dve.wait_ge(sem("u"), i)
                    dve.tensor_tensor(gs[:, :, :], gpre[:, :, :],
                                      ps[:, CROSS_B[0], 0:3 * P].rearrange("p (c n) -> p c n", n=P),
                                      ALU.add).then_inc(sem("gs"), 1)
                elif step == "cross2":
                    dve.wait_ge(sem("sv"), i + 1)
                    dve.scalar_tensor_tensor(out=svn[:, :], in0=rows[:, 3, :], scalar=float(N),
                                             in1=ps[:, CROSS_B[0], 0:D], op0=ALU.mult, op1=ALU.add)
                    dve.wait_ge(sem("u"), i + 1)
                    dve.wait_ge(sem("ga"), i + 1)
                    if i:
                        dve.wait_ge(sem("kv"), i)
                    for ib, src in ((0, ga), (1, gb)):
                        last = dve.scalar_tensor_tensor(out=cv[:, ib, :], in0=rows[:, 3, :], scalar=src[:, i % 2, P:P + 1],
                                                        in1=ps[:, CROSS_B[1], ib * D:(ib + 1) * D],
                                                        op0=ALU.mult, op1=ALU.add)
                    last.then_inc(sem("cv"), 1)
                elif step == "cross3":
                    dve.wait_ge(sem("kv"), i + 1)
                    for ob in range(KC):
                        last = dve.scalar_tensor_tensor(
                            out=m1[:, ob, :], in0=svn[:, ob * P:(ob + 1) * P], scalar=cols[:, 2 + ob:3 + ob],
                            in1=ps[:, CROSS_B[0], D + ob * P:D + (ob + 1) * P], op0=ALU.mult, op1=ALU.add)
                    link(last)
                    if i:
                        dve.wait_ge(sem("ctx"), i)
                    dve.tensor_tensor(mb[:, :, :], m1[:, :, :], const("heads").unsqueeze(1).to_broadcast([P, KC, P]),
                                      ALU.mult).then_inc(sem("mb"), 1)
                elif step == "xo":
                    lo, hi = TH * i, TH * i + TH
                    dve.wait_ge(sem("xo"), i + 1)
                    dve.tensor_tensor(Z[:, lo:hi, :], Z[:, lo:hi, :],
                                      ps[:, CHAIN_B, :].rearrange("p (t n) -> p t n", t=TH), ALU.add).then_inc(sem("y"), 1)
                    dve.wait_ge(sem("y"), i + 1)
                    link(normalise(Z, Z, lo, hi))
                    link(dve.tensor_tensor(Z[:, lo:hi, :], Z[:, lo:hi, :],
                                           rows[:, 0, :].unsqueeze(1).to_broadcast([P, TH, D]), ALU.mult))
                    link(dve.tensor_tensor(X[:, lo:hi, :], X[:, lo:hi, :], Z[:, lo:hi, :], ALU.add))
                    to_z(normalise(X, Z, lo, hi))
                elif step == "proj1":
                    dve.wait_ge(sem("q1"), i + 1)
                    if i:
                        dve.wait_ge(sem("scores"), 4 * i)
                    queries(ps[:, CHAIN_B + 2, :].rearrange("p (c n) -> p c n", n=S))
                elif step == "score":
                    k = i % 2
                    rows_of = prob[:, k, :, :, :].rearrange("p i c k -> p (i c) k")
                    wide = [P, H, S]
                    dve.wait_ge(sem("scores"), i + 1)
                    got = ps[:, CHAIN_B + 2 * k:CHAIN_B + 2 * k + 2, :].rearrange("p b (c k) -> p (b c) k", k=S)
                    if i // 2 % 2 == 0:
                        link(dve.tensor_tensor(rows_of, got, const("causal").unsqueeze(1).to_broadcast(wide), ALU.add))
                        got = rows_of
                    link(dve.tensor_reduce(mx[:, k, :], got, AX.X, ALU.max))
                    dve.tensor_tensor(rows_of, got, mx[:, k, :].unsqueeze(2).to_broadcast(wide),
                                      ALU.subtract).then_inc(sem("shifted"), 1)
                elif step == "turn_p":
                    k = i % 2
                    dve.wait_ge(sem("prob"), i + 1)
                    link(dve.tensor_reduce(sm[:, k, :], prob[:, k, :, :, :].rearrange("p i c k -> p (i c) k"), AX.X, ALU.add))
                    link(dve.reciprocal(rs[:, k, :], sm[:, k, :]))
                elif step == "values":
                    k = i % 2
                    dve.wait_ge(sem("pv"), i + 1)
                    for bb in range(2):
                        inv = rs[:, k, :].rearrange("p (c b) -> p c b", b=2)[:, :, bb].rearrange("p (i j) -> p i j", i=4)
                        last = dve.tensor_tensor(on[k][:, bb, :, :, :].rearrange("p j i d -> p i j d"),
                                                 ps[:, CHAIN_B + 2 * k + bb, 0:D].rearrange("p (i j d) -> p i j d", i=4, j=KC),
                                                 inv.unsqueeze(3).to_broadcast([P, 4, KC, 2 * HD]), ALU.mult)
                    last.then_inc(sem("on"), 1)
                elif step == "turn_o":
                    k = i % 2
                    dve.wait_ge(sem("o_turned"), i + 1)
                    both = ps[:, CHAIN_B + 2 * k, :].rearrange("p (c h q) -> p c h q", h=2, q=S)
                    a = aT[k][:, :, :, :].rearrange("p j b q -> p (j b) q")
                    link(dve.tensor_scalar(a, both[:, :, 0, :], parity(0), None, ALU.mult))
                    dve.scalar_tensor_tensor(out=a, in0=both[:, :, 1, :], scalar=parity(1), in1=a,
                                             op0=ALU.mult, op1=ALU.add).then_inc(sem("aT"), 1)
                elif step == "project":
                    kind, t = i // 2 % 2, TH * (i // 4) + i % 2
                    dve.wait_ge(sem("ao"), i + 1)
                    o = ps[:, CHAIN_B + 2 * (i % 2) + 1, 0:D]
                    if kind == 0:
                        dve.tensor_tensor(X[:, t, :], X[:, t, :], o, ALU.add).then_inc(sem("x2"), 1)
                    else:
                        dve.tensor_tensor(Z[:, t, :], Z[:, t, :], o, ALU.add).then_inc(sem("s2"), 1)
                elif step == "norm2":
                    dve.wait_ge(sem("x2"), TH * i + TH)
                    to_z(normalise(X, Z, TH * i, TH * i + TH))
                elif step == "proj2":
                    dve.wait_ge(sem("scores"), 4 * i + 2)
                    sin = const("sin").unsqueeze(1).to_broadcast([P, KC * BH, S])
                    for n, (src, bank) in enumerate(((qs, CHAIN_B + 2), (ks, CHAIN_B))):
                        dve.wait_ge(sem("rot"), 2 * i + n + 1)
                        link(dve.tensor_tensor(ropet[:, :, :], ps[:, bank, :].rearrange("p (c n) -> p c n", n=S), sin, ALU.mult))
                        dve.wait_ge(sem("by_cos"), 2 * i + n + 1)
                        dst = src[:, :, :] if n == 0 else kT[:, :, :].rearrange("p k (b n) -> p (k b) n", n=S)
                        dve.tensor_tensor(dst, src[:, :, :], ropet[:, :, :], ALU.add).then_inc(sem("roped"), 1)
                        dve.wait_ge(sem("roped"), 2 * i + n + 1)
                        if n == 0:
                            queries(qs[:, :, :])
                elif step == "rms1":
                    to_z(rms_scaled(4, TH * i, TH * i + TH))
                elif step == "turn_x":
                    dve.wait_ge(sem("xH"), i + 1)
                    dve.tensor_tensor(xHL[:, 1, :, :], xT[:, :, :], f32(xHL[:, 0, :, :]), ALU.subtract).then_inc(sem("xL"), 1)
                elif step == "gate":
                    dve.wait_ge(sem("gates"), i + 1)
                    gates(i)
                elif step == "hidden":
                    use = dense_use(step, i)
                    m = i % 8
                    dve.wait_ge(sem("silu"), i + 1)
                    if i >= 2:
                        dve.wait_ge(sem("h_low"), i - 1)
                    dve.tensor_tensor(h32[:, m % 2, :], sa[:, m % 2, :], ps[:, DENSE_B[use % 4], TOK:2 * TOK],
                                      ALU.mult).then_inc(sem("taken"), 1)
                elif step == "shared":
                    use = dense_use(step, i)
                    dve.wait_ge(sem("products"), use + 1)
                    dve.tensor_tensor(Z[:, i, :], Z[:, i, :], ps[:, DENSE_B[use % 4], 0:D], ALU.add).then_inc(sem("taken"), 1)
                    dve.wait_ge(sem("taken"), use + 1)
                elif step == "experts":
                    use = dense_use(step, i)
                    t, u = i
                    dve.wait_ge(sem("products"), use + 1)
                    for e in range(2):
                        ins = dve.scalar_tensor_tensor(
                            out=Z[:, t, :], in0=ps[:, DENSE_B[use % 4], e * D:(e + 1) * D],
                            scalar=w8[:, t, 2 * u + e:2 * u + e + 1], in1=Z[:, t, :], op0=ALU.mult, op1=ALU.add)
                        if e == 0:
                            link(ins)
                    ins.then_inc(sem("taken"), 1)
                    dve.wait_ge(sem("taken"), use + 1)
                elif step == "finish":
                    link(rms_scaled(5, i, i + 1))
                    dve.tensor_tensor(X[:, i, :], X[:, i, :], Z[:, i, :], ALU.add).then_inc(sem("x3"), 1)


def kernel(x, ctx_1024, mask_Bx1xSxS2_bf0, L0_xattn_wq_w, L0_xattn_wq_b, L0_xattn_wk_w, L0_xattn_wk_b, L0_xattn_wv_w,
           L0_xattn_wv_b, L0_xattn_wo_w, L0_xattn_wo_b, L0_xattn_ln_g, L0_xattn_ln_b, L0_attn_Wq, L0_attn_Wk,
           L0_attn_Wv, L0_attn_Wo, L0_ffn_Wq, L0_ffn_Wk_c, L0_ffn_Wv_c, L0_ffn_Wk, L0_ffn_Wv, L0_ffn_Wo,
           L0_ffn_W_shared_in, L0_ffn_W_shared_out, L0_ffn_W1_shared, L0_ffn_W2_experts, L0_ffn_Wg_gate,
           L0_ffn_We_gate, L0_ffn_group_bias, L0_ffn_expert_bias, L0_ffn_norm1_w, L0_ffn_norm2_w):
    import concourse.bacc as bacc
    from concourse.bass_utils import run_bass_kernel_spmd as run

    def a(v):
        return np.asarray(v)

    def chunks(w):
        w = a(w)
        return w.reshape(w.shape[0] // P, P, w.shape[1]).transpose(1, 0, 2)

    arrays = {
        "x": a(x).reshape(T, P, D).transpose(1, 0, 2),
        "ctx": a(ctx_1024),
        "mask": a(mask_Bx1xSxS2_bf0).reshape(P, B * S * N // P),
        "const": constants(),
        "w0": np.stack([chunks(a(w).T) for w in (L0_xattn_wq_w, L0_xattn_wk_w, L0_xattn_wv_w, L0_xattn_wo_w)], 1),
        "w1": np.stack([chunks(a(w).T) for w in (L0_attn_Wq, L0_attn_Wk, L0_attn_Wv, L0_attn_Wo)], 1),
        "wq": chunks(L0_ffn_Wq),
        "wkvc": np.concatenate([chunks(L0_ffn_Wk_c), chunks(L0_ffn_Wv_c)], 2),
        "wkv": np.concatenate([a(L0_ffn_Wk), a(L0_ffn_Wv)], 0),
        "wo": chunks(L0_ffn_Wo),
        "gate": np.concatenate([chunks(L0_ffn_Wg_gate), chunks(L0_ffn_We_gate)], 2),
        "dense": np.concatenate([chunks(L0_ffn_W_shared_in), chunks(L0_ffn_W1_shared),
                                 chunks(L0_ffn_W_shared_out).reshape(P, 1, 4 * D)], 1),
        "w2": a(L0_ffn_W2_experts).reshape(E // 2, 2, HID // P, P, D).transpose(3, 0, 2, 1, 4).reshape(P, 8, 1024),
        "cols": np.concatenate([a(L0_xattn_wq_b).reshape(KC, P).T, a(L0_xattn_wk_b).reshape(KC, P).T], 1),
        "rows": np.stack([a(r) for r in (L0_xattn_ln_g, L0_xattn_ln_b, L0_xattn_wo_b, L0_xattn_wv_b,
                                         L0_ffn_norm1_w, L0_ffn_norm2_w)], 0),
        "ebias": np.concatenate([a(L0_ffn_group_bias), a(L0_ffn_expert_bias)], 0),
    }
    arrays = {k: np.ascontiguousarray(v) for k, v in arrays.items()}
    nc = bacc.Bacc("TRN2", target_bir_lowering=False, num_devices=1)
    args = [nc.dram_tensor("in_" + k, v.shape, mybir.dt.from_np(v.dtype), kind="ExternalInput").ap()
            for k, v in arrays.items()]
    o = nc.dram_tensor("out_x", (B * S, D), F32, kind="ExternalOutput").ap()
    layer(nc, *args, o)
    r = run(nc, [{"in_" + k: v for k, v in arrays.items()}], core_ids=[0])
    return r.results[0]["out_x"].reshape(B, S, D)
```

```python
from contextlib import ExitStack

import numpy as np

import concourse.bass as bass
from concourse import mybir

ALU = mybir.AluOpType
ACT = mybir.ActivationFunctionType
AX = mybir.AxisListType
F32 = mybir.dt.float32
F32R = mybir.dt.float32r
U8 = mybir.dt.uint8
I32 = mybir.dt.int32
U32 = mybir.dt.uint32

P = 128
B, S, D = 8, 64, 256
N = 1601
H, HD = 16, 16
KC = D // P
T = B * S // P
HALVES = 2
TH = T // HALVES
BH = B // HALVES
TOK = TH * P
ROWS = 4
CH_B = 3
TAIL = N - CH_B * ROWS * P
SLOT = ROWS + 1
HROW = D + 4
HID = 512
E = 8
GRP = 2
LN_EPS = 1e-5
RMS_EPS = 1e-6
LOW = -3.0e38
SCALE = 1.0 / float(np.sqrt(HD))
XSCALE = 1.0 / float(np.float32(np.float16(np.sqrt(np.float16(HD)))) + np.float32(1e-8))

CONST = {}
_at = 0
for _name, _width in (("ident", P), ("parity", 2), ("heads", P), ("causal", S), ("cos", S), ("sin", S),
                      ("rot", P), ("side", P), ("tile_of", T), ("iota", E)):
    CONST[_name] = (_at, _at + _width)
    _at += _width
NCONST = _at


def constants():
    c = np.zeros((P, NCONST), np.float32)
    p = np.arange(P)

    def put(name, a):
        lo, hi = CONST[name]
        c[:, lo:hi] = a

    put("ident", np.eye(P))
    put("parity", (p[:, None] // HD) % 2 == np.arange(2)[None, :])
    put("heads", (p[:, None] // HD == p[None, :] // HD) * XSCALE)
    put("causal", np.where(np.arange(S)[None, :] <= p[:, None] % S, 0.0, LOW))
    freq = (1.0 / np.float32(10000.0) ** (np.arange(0, HD, 2, dtype=np.float32) / np.float32(HD))).astype(np.float32)
    ang = np.arange(S, dtype=np.float32)[None, :] * freq[(p % HD) // 2][:, None]
    put("cos", np.cos(ang.astype(np.float32)))
    put("sin", np.sin(ang.astype(np.float32)))
    rot = np.zeros((P, P), np.float32)
    rot[p[1::2], p[0::2]] = -1.0
    rot[p[0::2], p[1::2]] = 1.0
    put("rot", rot)
    put("side", (p[:, None] // (P // B)) % 2 == p[None, :] // S)
    put("tile_of", p[:, None] // (2 * P // B) == np.arange(T)[None, :])
    put("iota", np.arange(E)[None, :])
    return c


NU = 5 + 8
STAGED = 4
GBLK = P + 2
GRAM_B = (0, 1)
CROSS_B = (6, 7)
CHAIN_B = 2
DENSE_B = (0, 1, 6, 7)
USES = 8 + TH * (1 + E // 2)


def context_steps():
    out = [("split", 0), ("norm0", 0), ("split", 1)]
    for b in range(BH + 1):
        for c in range(CH_B):
            n = CH_B * b + c
            out += [("split", n + 2), ("gram", n)]
            if c == CH_B - 1:
                out.append(("evac", b))
            if b > 1 and c == 0:
                out.append(("cross4", b - 2))
            if b:
                out.append((f"cross{c + 1}", b - 1))
            if n == 1:
                out.append(("pre", 0))
            if n == 8:
                out.append(("masked", 0))
    n = CH_B * (BH + 1)
    return out + [("split", n + 2), ("gram", n), ("cross4", BH - 1)]


def first_chain_steps():
    b = BH
    n = CH_B * (b + 1)
    return [
        ("cross1", b), ("split", n + 3),
        ("xo_product", 0), ("xo", 0), ("cross2", b), ("gram", n + 1), ("norm1", 0), ("gram", n + 2), ("evac", b + 1),
        ("gram", n + 3), ("split", n + 4), ("turn_z", (0, 0)), ("cross3", b), ("split", n + 5), ("proj1", 0),
        ("cross4", b), ("cross1", b + 1), ("split", n + 6), ("piece", 0),
        ("score", 0), ("cross2", b + 1), ("score", 1), ("gram", n + 4), ("turn_p", 0), ("cross3", b + 1),
        ("gram", n + 5), ("evac", b + 2), ("turn_p", 1), ("piece", 1),
        ("values", 0), ("cross4", b + 1), ("values", 1), ("cross1", b + 2),
        ("turn_o", 0), ("turn_o", 1), ("project", 0), ("project", 1), ("split", n + 7),
        ("norm2", 0), ("cross2", b + 2), ("gram", n + 6), ("split", n + 8), ("turn_z", (0, 1)),
        ("cross3", b + 2), ("gram", n + 7), ("proj2", 0), ("gram", n + 8), ("evac", b + 3), ("cross4", b + 2),
        ("score", 2), ("cross1", b + 3), ("score", 3), ("cross2", b + 3), ("piece", 2),
        ("turn_p", 2), ("turn_p", 3), ("piece", 3), ("values", 2), ("cross3", b + 3), ("values", 3),
        ("turn_o", 2), ("turn_o", 3), ("cross4", b + 3), ("project", 2), ("project", 3),
        ("xo_product", 1), ("rms1", 0), ("turn_x", 0), ("piece", 4),
    ]


def second_chain_steps():
    hidden = [("hidden", m) for m in range(8)]
    piece = [("piece", u) for u in range(5, NU)]
    a, b = ([("shared", t)] + [("experts", (t, u)) for u in range(E // 2)] for t in range(TH))
    return [
        ("xo", 1), ("gates", 0), *hidden[0:2], piece[0], *hidden[2:4], ("norm1", 1), hidden[4], piece[1],
        ("turn_z", (1, 0)), hidden[5], piece[2], ("gate", 0), ("proj1", 1), piece[3], hidden[6], hidden[7], piece[4],
        ("score", 4), ("score", 5), a[0], a[1], piece[5], ("turn_p", 4), a[2], ("turn_p", 5), piece[6],
        ("values", 4), ("values", 5), ("turn_o", 4), ("turn_o", 5), ("project", 4), ("project", 5),
        ("norm2", 1), a[3], ("turn_z", (1, 1)), piece[7], ("proj2", 1), a[4], ("score", 6), ("score", 7),
        b[0], b[1], ("turn_p", 6), b[2], ("turn_p", 7), ("values", 6), ("values", 7), ("turn_o", 6), ("turn_o", 7),
        ("project", 6), ("project", 7), ("rms1", 1), b[3], ("turn_x", 1), b[4], ("gates", 1),
    ]


def second_dense_steps():
    a, b = ([("shared", t)] + [("experts", (t, u)) for u in range(E // 2)] for t in range(TH, T))
    return [*(("hidden", 8 + m) for m in range(8)), a[0], ("gate", 1), a[1], a[2], ("finish", 0), a[3], ("finish", 1), a[4],
            b[0], b[1], ("finish", TH), *b[2:], ("finish", TH + 1)]


def steps_in_order():
    return context_steps() + first_chain_steps() + second_chain_steps() + second_dense_steps()


def layer(nc, d_x, d_ctx, d_mask, d_const, d_w0, d_w1, d_wq, d_wkvc, d_wkv, d_wo, d_gate, d_dense, d_w2,
          d_cols, d_rows, d_ebias, out):
    sb_at = (nc.sbuf_base + 63) // 64 * 64
    where = {}

    def place(name, shape, dt=F32, at=None):
        nonlocal sb_at
        size = int(np.prod(shape[1:])) * (1 if dt == U8 else 4)
        size = (size + 31) // 32 * 32
        if at is None:
            at = sb_at
            sb_at += size
        where[name] = at
        return nc.alloc_sbuf_tensor_at(name, shape, dt, offset=at), at + size

    half_arena = E // 4 * 2 * (HID // P) * 2 * D * 4
    w2, _ = place("w2", [P, E // 2, 2, HID // P, 2 * D], F32R)
    arena = where["w2"]
    ch, nxt = place("ch", [P, CH_B, SLOT, HROW], F32R, at=arena)
    cl, nxt = place("cl", [P, CH_B, SLOT, D], F32R, at=nxt)
    svn, nxt = place("svn", [P, D], at=nxt)
    assert nxt <= arena + half_arena
    w0, nxt = place("w0", [P, 4, KC, D], at=arena + half_arena)
    q0T, nxt = place("q0T", [P, KC, T * P], at=nxt)
    gab, nxt = place("gab", [P, 2, KC, 3, GBLK], at=nxt)
    gpre, nxt = place("gpre", [P, 2, KC, GBLK], at=nxt)
    gs, nxt = place("gs", [P, 4, P], at=nxt)
    crep, nxt = place("crep", [P, KC, P], at=nxt)
    cv, nxt = place("cv", [P, KC, D], at=nxt)
    m1, nxt = place("m1", [P, KC, P], at=nxt)
    mb, nxt = place("mb", [P, KC, P], at=nxt)
    ctxT, nxt = place("ctxT", [P, HALVES, KC, TOK], at=nxt)
    assert nxt <= arena + 2 * half_arena
    dense, _ = place("dense", [P, 2, 5, 1024], F32R)
    raw, _ = place("raw", [P, CH_B * ROWS + 1, D])
    cst, _ = place("cst", [P, NCONST])
    w1, _ = place("w1", [P, 4, KC, D])
    wq, _ = place("wq", [P, KC, D])
    wkvc, _ = place("wkvc", [P, KC, P])
    wkv, _ = place("wkv", [P, D])
    wo, _ = place("wo", [P, KC, D])
    gate, _ = place("gate", [P, KC, GRP + E])
    cols, _ = place("cols", [P, 4])
    rows, _ = place("rows", [P, 6, D])
    ebias, _ = place("ebias", [P, GRP + E])
    X, _ = place("X", [P, T, D])
    Z, _ = place("Z", [P, T, D])
    zT, _ = place("zT", [P, KC, TOK])
    st, _ = place("st", [P, T, 6])
    mv, _ = place("mv", [P, T, 2])
    ve, _ = place("ve", [P, T])
    rstd, _ = place("rstd", [P, T])
    half_exp, _ = place("half_exp", [P, T])
    flag, _ = place("flag", [P, 1])
    flags, _ = place("flags", [P, T])
    nan_a, _ = place("nan_a", [P, T])
    nan_b, _ = place("nan_b", [P, T])
    qp, _ = place("qp", [P, KC * BH, 2, S])
    z0T, _ = place("z0T", [P, KC, T * P], at=where["qp"])
    kblk, _ = place("kblk", [P, KC * BH, 4, S])
    vblk, _ = place("vblk", [P, TH, H // 2, 2, 2 * HD])
    prob, _ = place("prob", [P, TH, H // 2, 2 * S])
    on = [place(f"on{k}", [P, 2, KC, 4, 2 * HD], at=where["prob"] + k * 4096)[0] for k in range(TH)]
    aT = [place(f"aT{k}", [P, KC, 2, S], at=where["prob"] + k * 4096 + 2048)[0] for k in range(TH)]
    probT, _ = place("probT", [P, TH, H // 2, P])
    xT, _ = place("xT", [P, KC, TOK], at=where["probT"])
    qs, _ = place("qs", [P, KC * BH, S], at=where["probT"] + 2048)
    ropet, _ = place("ropet", [P, KC * BH, S], at=where["probT"] + 4096)
    ks, _ = place("ks", [P, KC * BH, S], at=where["probT"] + 6144)
    kvcT, _ = place("kvcT", [P, TOK], at=where["prob"])
    mx, _ = place("mx", [P, TH, H])
    sm, _ = place("sm", [P, TH, H])
    rs, _ = place("rs", [P, TH, H])
    hT, _ = place("hT", [P, 2, 2, HID // P, TOK], F32R)
    mask, _ = place("mask", [P, B * S * N // P], U8, at=where["hT"])
    stage, _ = place("stage", [P, STAGED, 1024], at=where["hT"])
    sa, _ = place("sa", [P, 2, TOK])
    xHL, _ = place("xHL", [P, 2, KC, TOK], F32R)
    sq, _ = place("sq", [P, D])
    ms, _ = place("ms", [P, T])
    lg, _ = place("lg", [P, TH, GRP + E])
    gm, _ = place("gm", [P, TH])
    eg, _ = place("eg", [P, TH, GRP])
    gsum, _ = place("gsum", [P, TH])
    gprob, _ = place("gprob", [P, TH])
    ind, _ = place("ind", [P, TH, GRP])
    off, _ = place("off", [P, TH, GRP])
    em, _ = place("em", [P, TH, E])
    emax, _ = place("emax", [P, TH])
    esum, _ = place("esum", [P, TH])
    erec, _ = place("erec", [P, TH])
    pe8, _ = place("pe8", [P, TH, E])
    top, _ = place("top", [P, TH, 8])
    topi, _ = place("topi", [P, TH, 8], U32)
    topf, _ = place("topf", [P, TH, 8])
    w8a, _ = place("w8a", [P, T, E])
    w8, _ = place("w8", [P, T, E])
    assert sb_at <= nc.sbuf_usable_end, (sb_at, nc.sbuf_usable_end)

    def const(name):
        lo, hi = CONST[name]
        return cst[:, lo:hi]

    ident = const("ident")

    def parity(hl):
        lo, _ = CONST["parity"]
        return cst[:, lo + hl:lo + hl + 1]

    def f32(ap):
        return ap.bitcast(F32)

    def halves(ap):
        return ap.rearrange("p r (h n) -> p r h n", h=KC)

    def raw_piece(u):
        if u < STAGED:
            return stage[:, u, :]
        c = (u - STAGED) % CH_B
        return raw[:, ROWS * c:ROWS * (c + 1), :].rearrange("p r d -> p (r d)")

    def piece(u, part):
        if u < 5:
            return dense[:, part, u, :]
        u -= 5
        return w2[:, u // 2, part, 2 * (u % 2):2 * (u % 2) + 2, :].rearrange("p k n -> p (k n)")

    def dense_use(step, i):
        if step == "hidden":
            return USES * (i // 8) + i % 8
        t, k = (i, 0) if step == "shared" else (i[0], 1 + i[1])
        return USES * (t // TH) + 8 + (1 + E // 2) * (t % TH) + k

    plan = steps_in_order()

    with ExitStack() as stack:
        ps = stack.enter_context(nc.psum_tensor("ps", [P, 8, 512], F32))
        sems = {}

        def sem(name):
            if name not in sems:
                sems[name] = stack.enter_context(nc.semaphore(name))
            return sems[name]

        block = stack.enter_context(nc.Block())

        @block.sync
        def _(sp):
            for n in range(CH_B * B):
                b, c = divmod(n, CH_B)
                if b:
                    sp.wait_ge(sem("low_done"), n - CH_B + 1)
                sp.dma_start(raw[:, ROWS * c:ROWS * (c + 1), :], d_ctx[b, 0:CH_B * ROWS * P, :].rearrange(
                    "(p r) d -> p r d", r=CH_B * ROWS)[:, c * ROWS:(c + 1) * ROWS, :]).then_inc(sem(f"raw{c}"), 16)
                if c == CH_B - 1:
                    sp.dma_start(raw[0:TAIL, ROWS * CH_B, :], d_ctx[b, CH_B * ROWS * P:N, :]).then_inc(sem(f"raw{c}"), 16)
                if CH_B * BH <= n < CH_B * BH + STAGED:
                    u = n - CH_B * BH
                    sp.wait_ge(sem("flag"), 1)
                    sp.dma_start(raw_piece(u), d_dense[:, u, :]).then_inc(sem(f"staged{u}"), 16)
            for u in range(STAGED, NU):
                if u < STAGED + CH_B:
                    sp.wait_ge(sem("low_done"), CH_B * (B - 1) + u - STAGED + 1)
                else:
                    sp.wait_ge(sem("piece_low"), u - CH_B + 1)
                src = d_dense[:, u, :] if u < 5 else d_w2[:, u - 5, :]
                sp.dma_start(raw_piece(u), src).then_inc(sem(f"raw{(u - STAGED) % CH_B}"), 16)
            for t in range(T):
                sp.wait_ge(sem("x3"), t + 1)
                sp.dma_start(out[t * P:(t + 1) * P, :], X[:, t, :]).then_inc(sem("stored"), 16)
            sp.wait_ge(sem("stored"), 16 * T)

        def chunk_landed(eng, n):
            b, c = divmod(n, CH_B)
            eng.wait_ge(sem(f"raw{c}"), (32 if c == CH_B - 1 else 16) * (b + 1))

        def piece_landed(eng, u):
            if u < STAGED:
                eng.wait_ge(sem(f"staged{u}"), 16)
            else:
                k, c = divmod(u - STAGED, CH_B)
                eng.wait_ge(sem(f"raw{c}"), (32 if c == CH_B - 1 else 16) * B + 16 * (k + 1))

        @block.gpsimd
        def _(pool):
            ones = f32(ch[:, :, :, :]).rearrange("p c r (h n) -> p c r h n", h=KC)
            for c in range(CH_B):
                pool.memset(ones[:, c, :, :, P:P + 2], 1.0).then_inc(sem("ones"), 1)
            pool.memset(half_exp[:, :], -0.5).then_inc(sem("ones"), 1)
            pool.memset(kblk[:, :, :, :], 0.0).then_inc(sem("zeros"), 1)
            pool.memset(vblk[:, :, :, :, :], 0.0).then_inc(sem("zeros"), 1)
            pool.wait_ge(sem("ones"), CH_B + 1)
            pool.wait_ge(sem("const_in"), 16)
            roots = [0]

            def inverse_roots(lo, hi):
                roots[0] += 1
                pool.wait_ge(sem("var"), roots[0])
                pool.tensor_tensor(rstd[:, lo:hi], ve[:, lo:hi], half_exp[:, lo:hi], ALU.pow).then_inc(sem("rstd"), 1)

            for step, i in plan:
                if step == "norm0":
                    inverse_roots(0, T)
                elif step == "cross1":
                    pool.wait_ge(sem("ga"), i + 1)
                    pool.wait_ge(sem("gb"), i + 1)
                    if i >= 2:
                        pool.wait_ge(sem("cv"), i - 1)
                        pool.wait_ge(sem("crep"), i - 1)
                    for k in range(KC):
                        last = pool.tensor_tensor(gpre[:, i % 2, k, :], gab[:, i % 2, k, k, :], gab[:, i % 2, k, k + 1, :], ALU.add)
                    last.then_inc(sem("gpre"), 1)
                elif step in ("xo", "norm1", "norm2", "rms1"):
                    inverse_roots(TH * i, TH * i + TH)
                elif step == "proj2":
                    for n, src in enumerate((qs, ks)):
                        pool.wait_ge(sem("rot"), 2 * i + n + 1)
                        pool.tensor_tensor(src[:, :, :], src[:, :, :],
                                           const("cos").unsqueeze(1).to_broadcast([P, KC * BH, S]),
                                           ALU.mult).then_inc(sem("by_cos"), 1)
                elif step == "piece":
                    pool.wait_ge(sem("piece_high"), i + 1)
                    pool.tensor_tensor(piece(i, 1), raw_piece(i), f32(piece(i, 0)), ALU.subtract).then_inc(sem("piece_low"), 1)
                elif step == "hidden":
                    m = i % 8
                    pool.wait_ge(sem("h_high"), i + 1)
                    pool.tensor_tensor(hT[:, m // 4, 1, m % 4, :], sa[:, m % 2, :], f32(hT[:, m // 4, 0, m % 4, :]),
                                       ALU.subtract).then_inc(sem("h_low"), 1)
                elif step == "finish":
                    inverse_roots(i, i + 1)

        @block.scalar
        def _(act):
            act.dma_start(X[:, :, :], d_x).then_inc(sem("x_in"), 16)
            act.dma_start(cst[:, :], d_const).then_inc(sem("const_in"), 16)
            act.dma_start(w0[:, :, :, :], d_w0).then_inc(sem("w0_in"), 16)
            act.dma_start(cols[:, :], d_cols).then_inc(sem("cols_in"), 16)
            act.dma_start(rows[:, :, :], d_rows.partition_broadcast(P)).then_inc(sem("rows_in"), 16)
            squares = [0]

            def copy(dst, src, name):
                act.activation(dst, src, ACT.Copy).then_inc(sem(name), 1)

            def z_out(dst, bank):
                copy(dst.rearrange("p k (t c) -> p t k c", c=P),
                     ps[:, bank, :].rearrange("p (t k c) -> p t k c", k=KC, c=P), "zT")

            def block_values(bank):
                for bb in range(2):
                    q = slice(bb * S, bb * S + S)
                    last = act.activation(vblk[q, :, :, bb, :].rearrange("p t c d -> p (t c) d"),
                                          ps[q, bank, :].rearrange("p (c d) -> p c d", d=2 * HD), ACT.Copy)
                last.then_inc(sem("v"), 1)

            def mean_square(t):
                if squares[0]:
                    act.wait_ge(sem("ms"), squares[0])
                squares[0] += 1
                act.activation(sq[:, :], Z[:, t, :], ACT.Square, scale=D ** -0.5,
                               accum_out=ms[:, t:t + 1]).then_inc(sem("ms"), 1)

            for step, i in plan:
                if step == "pre":
                    act.wait_ge(sem("const_in"), 16)
                    act.wait_ge(sem("cols_in"), 16)
                    act.wait_ge(sem("turned"), 1)
                    z_out(z0T[:, :, 0:TOK], CROSS_B[0])
                    act.wait_ge(sem("turned"), 2)
                    z_out(z0T[:, :, TOK:T * P], CROSS_B[1])
                    for ob in range(KC):
                        act.wait_ge(sem("q0"), ob + 1)
                        act.activation(q0T[:, ob, :], ps[:, CHAIN_B + ob, :], ACT.Identity,
                                       bias=cols[:, ob:ob + 1]).then_inc(sem("q0T"), 1)
                elif step == "split":
                    c = i % CH_B
                    chunk_landed(act, i)
                    if i >= CH_B:
                        act.wait_ge(sem("gram_chunk"), i - CH_B + 1)
                    if i == 0:
                        act.wait_ge(sem("ones"), CH_B)
                    for p, lo, hi in [(P, 0, ROWS)] + ([(TAIL, ROWS, ROWS + 1)] if c == CH_B - 1 else []):
                        last = act.activation(halves(ch[0:p, c, lo:hi, :])[:, :, :, 0:P],
                                              halves(raw[0:p, ROWS * c + lo:ROWS * c + hi, :]), ACT.Copy)
                    last.then_inc(sem("high_done"), 1)
                elif step == "evac":
                    act.wait_ge(sem("gram_chunk"), CH_B * (i + 1))
                    if i >= 2:
                        act.wait_ge(sem("gs"), i - 1)
                    copy(gab[:, i % 2, 0, :, :].rearrange("p c n -> p (c n)"), ps[:, GRAM_B[0], 0:3 * GBLK], "ga")
                    if i == 0:
                        act.dma_start(mask[:, :], d_mask).then_inc(sem("mask_in"), 16)
                        act.dma_start(w1[:, :, :, :], d_w1).then_inc(sem("w_in"), 16)
                        act.dma_start(wq[:, :, :], d_wq).then_inc(sem("w_in"), 16)
                        act.dma_start(wkvc[:, :, :], d_wkvc).then_inc(sem("w_in"), 16)
                        act.dma_start(wkv[:, :], d_wkv).then_inc(sem("w_in"), 16)
                        act.dma_start(wo[:, :, :], d_wo).then_inc(sem("w_in"), 16)
                        act.dma_start(gate[:, :, :], d_gate).then_inc(sem("w_in"), 16)
                        act.dma_start(ebias[:, :], d_ebias.partition_broadcast(P)).then_inc(sem("w_in"), 16)
                elif step == "cross1":
                    act.wait_ge(sem("gpre"), i + 1)
                    if i:
                        act.wait_ge(sem("sv"), i)
                    for k in range(KC):
                        last = act.activation(crep[:, k, :], ident, ACT.Identity, scale=0.0,
                                              bias=gpre[:, i % 2, k, P:P + 1])
                    last.then_inc(sem("crep"), 1)
                elif step == "cross4":
                    act.wait_ge(sem("ctx"), i + 1)
                    copy(ctxT[:, i // BH, :, (i % BH) * S:(i % BH + 1) * S],
                         ps[:, CROSS_B[1], 0:KC * S].rearrange("p (k n) -> p k n", k=KC), "ctxT")
                elif step == "turn_z":
                    g, k = i
                    act.wait_ge(sem("turned"), 3 + 3 * g + k)
                    z_out(zT[:, :, :], CHAIN_B + 1)
                elif step == "proj1":
                    act.wait_ge(sem("k1"), i + 1)
                    if i:
                        act.wait_ge(sem("scores"), 4 * i)
                    else:
                        act.wait_ge(sem("zeros"), 2)
                    for r in range(4):
                        q = slice(32 * r, 32 * r + 32)
                        last = act.activation(kblk[q, :, r, :], ps[q, CHAIN_B + 3, :].rearrange("p (c n) -> p c n", n=S), ACT.Copy)
                    last.then_inc(sem("kblk"), 1)
                    act.wait_ge(sem("v1"), i + 1)
                    if i:
                        act.wait_ge(sem("pv"), 4 * i)
                    block_values(CHAIN_B)
                elif step == "score":
                    act.wait_ge(sem("shifted"), i + 1)
                    act.activation(prob[:, i % 2, :, :], prob[:, i % 2, :, :], ACT.Exp,
                                   scale=SCALE).then_inc(sem("prob"), 1)
                elif step == "turn_p":
                    for j in range(2):
                        act.wait_ge(sem("p_turned"), 2 * i + j + 1)
                        if i >= 2:
                            act.wait_ge(sem("pv"), i - 1)
                        copy(probT[:, i % 2, 4 * j:4 * j + 4, :],
                             ps[:, CHAIN_B + 2 * (i % 2) + j, :].rearrange("p (c n) -> p c n", n=P), "probT")
                elif step == "proj2":
                    act.wait_ge(sem("q2"), i + 1)
                    copy(qs[:, :, :], ps[:, CHAIN_B, :].rearrange("p (c n) -> p c n", n=S), "qs")
                    act.wait_ge(sem("kvc"), i + 1)
                    if i:
                        act.wait_ge(sem("v2"), i)
                    copy(kvcT[:, :], ps[:, CHAIN_B + 1, 0:TOK], "kvcT")
                    act.wait_ge(sem("k2"), i + 1)
                    copy(ks[:, :, :], ps[:, CHAIN_B + 3, :].rearrange("p (c n) -> p c n", n=S), "ks")
                    act.wait_ge(sem("v2"), i + 1)
                    act.wait_ge(sem("pv"), 4 * i + 2)
                    block_values(CHAIN_B + 1)
                elif step == "rms1":
                    act.wait_ge(sem("s2"), TH * i + TH)
                    for t in range(TH * i, TH * i + TH):
                        mean_square(t)
                elif step == "turn_x":
                    act.wait_ge(sem("turned"), 5 + 3 * i)
                    copy(xT[:, :, :].rearrange("p k (t c) -> p t k c", c=P),
                         ps[:, CHAIN_B + 2, :].rearrange("p (t k c) -> p t k c", k=KC, c=P), "xT")
                    act.wait_ge(sem("xT"), i + 1)
                    if i:
                        act.wait_ge(sem("products"), USES * (i - 1) + 8)
                    copy(xHL[:, 0, :, :], xT[:, :, :], "xH")
                elif step == "gate":
                    act.wait_ge(sem("gates_a"), i + 1)
                    act.activation(eg[:, :, :], eg[:, :, :], ACT.Exp).then_inc(sem("eg"), 1)
                    act.wait_ge(sem("gates_b"), i + 1)
                    act.activation(pe8[:, :, :], em[:, :, :], ACT.Exp).then_inc(sem("ee"), 1)
                elif step == "piece":
                    piece_landed(act, i)
                    if i >= 5:
                        act.wait_ge(sem("xo"), HALVES)
                    copy(piece(i, 0), raw_piece(i), "piece_high")
                elif step == "hidden":
                    use = dense_use(step, i)
                    m = i % 8
                    act.wait_ge(sem("products"), use + 1)
                    if i >= 2:
                        act.wait_ge(sem("h_low"), i - 1)
                    act.activation(sa[:, m % 2, :], ps[:, DENSE_B[use % 4], 0:TOK], ACT.Silu).then_inc(sem("silu"), 1)
                    act.wait_ge(sem("taken"), use + 1)
                    if m == 0 and i:
                        act.wait_ge(sem("products"), USES)
                    copy(hT[:, m // 4, 0, m % 4, :], sa[:, m % 2, :], "h_high")
                elif step == "finish":
                    act.wait_ge(sem("taken"), dense_use("experts", (i, E // 2 - 1)) + 1)
                    mean_square(i)

        @block.tensor
        def _(pe):
            def mm(o, l, r, start, stop, check=True):
                return pe.matmul(o, l, r, start=start, stop=stop, skip_group_check=not check)

            def turn(o, src):
                return pe.transpose(o, src, ident)

            def turn_rows(lo_tile, bank):
                for t in range(TH):
                    for k in range(KC):
                        last = turn(ps[:, bank, t * D + k * P:t * D + (k + 1) * P], Z[:, lo_tile + t, k * P:(k + 1) * P])
                last.then_inc(sem("turned"), 1)

            def gram_tile(slot, r, p, first, last):
                row = ch[0:p, slot, r, :].rearrange("p (h n) -> p h n", h=KC)
                h0, h1 = row[:, 0, 0:P], row[:, 1, 0:P]
                l0, l1 = cl[0:p, slot, r, 0:P], cl[0:p, slot, r, P:2 * P]
                a, b = (ps[:, bank, 0:3 * GBLK].rearrange("p (c n) -> p c n", n=GBLK) for bank in GRAM_B)
                mm(a[:, 0, :], h0, row[:, 0, :], first, False, False)
                mm(a[:, 1:3, :], l0, row, False, last, False)
                mm(b[:, 0:2, :], h1, row, first, False, False)
                return mm(b[:, 0:3:2, :], l1, row, False, last, False)

            def split_products(o, pairs):
                todo = [(l[a], r[c]) for l, r in pairs for a, c in ((0, 0), (0, 1), (1, 0))]
                for k, (l, r) in enumerate(todo):
                    last = mm(o, l, r, k == 0, k == len(todo) - 1)
                return last

            def project(bank, width, weights, rows_, name):
                for ob in range(KC):
                    for k in range(KC):
                        last = mm(ps[:, bank, ob * width:(ob + 1) * width], weights[:, k, ob * P:(ob + 1) * P],
                                  rows_[k], k == 0, k == KC - 1)
                last.then_inc(sem(name), 1)

            for step, i in plan:
                if step == "pre":
                    pe.wait_ge(sem("const_in"), 16)
                    pe.wait_ge(sem("z"), 1)
                    turn_rows(0, CROSS_B[0])
                    turn_rows(TH, CROSS_B[1])
                    pe.wait_ge(sem("w0_in"), 16)
                    pe.wait_ge(sem("zT"), 2)
                    for ob in range(KC):
                        for k in range(KC):
                            last = mm(ps[:, CHAIN_B + ob, :], w0[:, 0, k, ob * P:(ob + 1) * P], z0T[:, k, :],
                                      k == 0, k == KC - 1)
                        last.then_inc(sem("q0"), 1)
                elif step == "masked":
                    pe.wait_ge(sem("flag"), 1)
                    mm(ps[:, CHAIN_B + 2, 0:T], const("side"), flags[:, :], True, True).then_inc(sem("flags"), 1)
                elif step == "gram":
                    b, c = divmod(i, CH_B)
                    pe.wait_ge(sem("high_done"), i + 1)
                    pe.wait_ge(sem("low_done"), i + 1)
                    if b and c == 0:
                        pe.wait_ge(sem("ga"), b)
                        pe.wait_ge(sem("gb"), b)
                    for r in range(ROWS):
                        last = gram_tile(c, r, P, c == 0 and r == 0, False)
                    if c == CH_B - 1:
                        last = gram_tile(c, ROWS, TAIL, False, True)
                    last.then_inc(sem("gram_chunk"), 1)
                elif step == "cross1":
                    s = i % 2
                    pe.wait_ge(sem("ga"), i + 1)
                    pe.wait_ge(sem("gb"), i + 1)
                    if i:
                        pe.wait_ge(sem("mb"), i)
                    bank = ps[:, CROSS_B[0], :]
                    turn(bank[:, 0:P], gab[:, s, 0, 1, 0:P])
                    turn(bank[:, P:2 * P], gab[:, s, 1, 2, 0:P])
                    turn(bank[:, 2 * P:3 * P], gab[:, s, 1, 0, 0:P])
                    turn(bank[:, 3 * P:4 * P], gab[:, s, 0, 2, 0:P]).then_inc(sem("g_turned"), 1)
                elif step == "cross2":
                    pe.wait_ge(sem("gs"), i + 1)
                    if i:
                        pe.wait_ge(sem("ctxT"), i)
                    lhs = ((gs[:, 0, :], gs[:, 3, :]), (gs[:, 2, :], gs[:, 1, :]))
                    for ib in range(KC):
                        for k in range(KC):
                            last = mm(ps[:, CROSS_B[1], ib * D:(ib + 1) * D], lhs[ib][k], w0[:, 2, k, :],
                                      k == 0, k == KC - 1)
                    last.then_inc(sem("u"), 1)
                    pe.wait_ge(sem("crep"), i + 1)
                    for k in range(KC):
                        last = mm(ps[:, CROSS_B[0], 0:D], crep[:, k, :], w0[:, 2, k, :], k == 0, k == KC - 1)
                    last.then_inc(sem("sv"), 1)
                elif step == "cross3":
                    pe.wait_ge(sem("cv"), i + 1)
                    for ob in range(KC):
                        for k in range(KC):
                            last = mm(ps[:, CROSS_B[0], D + ob * P:D + (ob + 1) * P], w0[:, 1, k, ob * P:(ob + 1) * P],
                                      cv[:, k, ob * P:(ob + 1) * P], k == 0, k == KC - 1)
                    last.then_inc(sem("kv"), 1)
                elif step == "cross4":
                    pe.wait_ge(sem("mb"), i + 1)
                    pe.wait_ge(sem("q0T"), KC)
                    for ob in range(KC):
                        last = mm(ps[:, CROSS_B[1], ob * S:(ob + 1) * S], mb[:, ob, :], q0T[:, ob, i * S:(i + 1) * S],
                                  True, True)
                    last.then_inc(sem("ctx"), 1)
                elif step == "xo_product":
                    pe.wait_ge(sem("ctxT"), BH * (i + 1))
                    if i:
                        pe.wait_ge(sem("aT"), 4 * i)
                    for t in range(TH):
                        for ob in range(KC):
                            last = mm(ps[:, CHAIN_B, t * D:(t + 1) * D], ctxT[:, i, ob, t * P:(t + 1) * P],
                                      w0[:, 3, ob, :], ob == 0, ob == KC - 1)
                    last.then_inc(sem("xo"), 1)
                elif step == "turn_z":
                    g, k = i
                    pe.wait_ge(sem("z"), 2 + 3 * g + k)
                    if g and k == 0:
                        pe.wait_ge(sem("s2"), TH * g)
                    if k:
                        pe.wait_ge(sem("x2"), TH * g + TH)
                    turn_rows(TH * g, CHAIN_B + 1)
                elif step == "proj1":
                    pe.wait_ge(sem("w_in"), 16 * 7)
                    pe.wait_ge(sem("zT"), 3 + 2 * i)
                    if i:
                        pe.wait_ge(sem("xT"), i)
                        pe.wait_ge(sem("logits"), i)
                    else:
                        pe.wait_ge(sem("nan"), 1)
                    z = [zT[:, k, :] for k in range(KC)]
                    project(CHAIN_B + 2, TOK, w1[:, 0, :, :], z, "q1")
                    project(CHAIN_B + 3, TOK, w1[:, 1, :, :], z, "k1")
                    pe.wait_ge(sem("y"), i + 1)
                    for t in range(TH):
                        for k in range(KC):
                            last = mm(ps[:, CHAIN_B, t * D:(t + 1) * D], zT[:, k, t * P:(t + 1) * P],
                                      w1[:, 2, k, :], k == 0, k == KC - 1)
                    last.then_inc(sem("v1"), 1)
                elif step == "score":
                    g, kind = i // 4, i // 2 % 2
                    pe.wait_ge(sem("qp"), 2 * g + kind + 1)
                    pe.wait_ge(sem("v"), 2 * g + kind + 1)
                    if kind:
                        pe.wait_ge(sem("roped"), 2 * g + 2)
                    else:
                        pe.wait_ge(sem("kblk"), g + 1)
                    for j in range(KC):
                        for bb in range(2):
                            jb = j * BH + 2 * (i % 2) + bb
                            last = mm(ps[:, CHAIN_B + 2 * (i % 2) + j, :].rearrange("p (r b k) -> p r b k", b=2, k=S)[:, :, bb, :],
                                      qp[:, jb, :, :].rearrange("p h q -> p (h q)"), kblk[:, jb, :, :], True, True)
                    last.then_inc(sem("scores"), 1)
                elif step == "turn_p":
                    pe.wait_ge(sem("prob"), i + 1)
                    for half in range(2):
                        for c in range(4):
                            last = turn(ps[:, CHAIN_B + 2 * (i % 2) + half, c * P:(c + 1) * P],
                                        prob[:, i % 2, 4 * half + c, :])
                        last.then_inc(sem("p_turned"), 1)
                elif step == "values":
                    pe.wait_ge(sem("probT"), 2 * i + 2)
                    for c in range(H // 2):
                        last = mm(ps[:, CHAIN_B + 2 * (i % 2), c * 4 * HD:(c + 1) * 4 * HD], probT[:, i % 2, c, :],
                                  vblk[:, i % 2, c, :, :].rearrange("p b d -> p (b d)"), True, True)
                    last.then_inc(sem("pv"), 1)
                elif step == "turn_o":
                    pe.wait_ge(sem("on"), i + 1)
                    for bb in range(2):
                        for j in range(KC):
                            c = 2 * j + bb
                            last = turn(ps[:, CHAIN_B + 2 * (i % 2), c * P:(c + 1) * P],
                                        on[i % 2][:, bb, j, :, :].rearrange("p i d -> p (i d)"))
                    last.then_inc(sem("o_turned"), 1)
                elif step == "project":
                    pe.wait_ge(sem("aT"), i + 1)
                    w = wo if i // 2 % 2 else w1[:, 3, :, :]
                    for j in range(KC):
                        last = mm(ps[:, CHAIN_B + 2 * (i % 2) + 1, 0:D], aT[i % 2][:, j, :, :].rearrange("p b q -> p (b q)"),
                                  w[:, j, :], j == 0, j == KC - 1)
                    last.then_inc(sem("ao"), 1)
                elif step == "proj2":
                    pe.wait_ge(sem("zT"), 4 + 2 * i)
                    z = [zT[:, k, :] for k in range(KC)]
                    project(CHAIN_B, TOK, wq, z, "q2")
                    for k in range(KC):
                        last = mm(ps[:, CHAIN_B + 1, 0:TOK], wkvc[:, k, :], z[k], k == 0, k == KC - 1)
                    last.then_inc(sem("kvc"), 1)
                    pe.wait_ge(sem("qs"), i + 1)
                    mm(ps[:, CHAIN_B + 2, :], const("rot"), qs[:, :, :].rearrange("p c n -> p (c n)"),
                       True, True).then_inc(sem("rot"), 1)
                    pe.wait_ge(sem("kvcT"), i + 1)
                    for ob in range(KC):
                        last = mm(ps[:, CHAIN_B + 3, ob * TOK:(ob + 1) * TOK], wkv[0:P // 2, ob * P:(ob + 1) * P],
                                  kvcT[0:P // 2, :], True, True)
                    last.then_inc(sem("k2"), 1)
                    for t in range(TH):
                        last = mm(ps[:, CHAIN_B + 1, t * D:(t + 1) * D], kvcT[P // 2:P, t * P:(t + 1) * P],
                                  wkv[P // 2:P, :], True, True)
                    last.then_inc(sem("v2"), 1)
                    pe.wait_ge(sem("ks"), i + 1)
                    mm(ps[:, CHAIN_B, :], const("rot"), ks[:, :, :].rearrange("p c n -> p (c n)"),
                       True, True).then_inc(sem("rot"), 1)
                elif step == "turn_x":
                    pe.wait_ge(sem("z"), 4 + 3 * i)
                    turn_rows(TH * i, CHAIN_B + 2)
                elif step == "gates":
                    pe.wait_ge(sem("xT"), i + 1)
                    pe.wait_ge(sem("s2"), TH * i + TH)
                    for t in range(TH):
                        for k in range(KC):
                            last = mm(ps[:, CHAIN_B + 3, t * 16:t * 16 + GRP + E], xT[:, k, t * P:(t + 1) * P],
                                      gate[:, k, :], k == 0, k == KC - 1)
                    last.then_inc(sem("gates"), 1)
                elif step == "hidden":
                    use = dense_use(step, i)
                    m = i % 8
                    if m == 0:
                        pe.wait_ge(sem("xL"), i // 8 + 1)
                        pe.wait_ge(sem("piece_low"), 4)
                    if use == 0:
                        pe.wait_ge(sem("ga"), B)
                        pe.wait_ge(sem("gb"), B)
                        pe.wait_ge(sem("mb"), B)
                        pe.wait_ge(sem("ctxT"), B)
                    if use >= 4:
                        pe.wait_ge(sem("taken"), use - 3)
                    for side in range(2):
                        col = side * HID + (m % 4) * P
                        last = split_products(
                            ps[:, DENSE_B[use % 4], side * TOK:(side + 1) * TOK],
                            [([dense[:, a, 2 * (m // 4) + k, col:col + P] for a in range(2)],
                              [xHL[:, a, k, :] for a in range(2)]) for k in range(KC)])
                    last.then_inc(sem("products"), 1)
                elif step == "shared":
                    use = dense_use(step, i)
                    tok = slice((i % TH) * P, (i % TH + 1) * P)
                    pe.wait_ge(sem("h_low"), 8 * (i // TH) + 4)
                    pe.wait_ge(sem("piece_low"), 5)
                    pe.wait_ge(sem("taken"), use - 3)
                    split_products(
                        ps[:, DENSE_B[use % 4], 0:D],
                        [([hT[:, 0, a, k, tok] for a in range(2)], [dense[:, a, 4, k * D:(k + 1) * D] for a in range(2)])
                         for k in range(HID // P)]).then_inc(sem("products"), 1)
                elif step == "experts":
                    use = dense_use(step, i)
                    t, u = i
                    tok = slice((t % TH) * P, (t % TH + 1) * P)
                    pe.wait_ge(sem("h_low"), 8 * (t // TH) + 8)
                    pe.wait_ge(sem("piece_low"), 5 + 2 * u + 2)
                    pe.wait_ge(sem("taken"), use - 3)
                    split_products(
                        ps[:, DENSE_B[use % 4], :],
                        [([hT[:, 1, a, k, tok] for a in range(2)], [w2[:, u, a, k, :] for a in range(2)])
                         for k in range(HID // P)]).then_inc(sem("products"), 1)

        @block.vector
        def _(dve):
            steps = [0]
            roots = [0]
            squares = [0]
            zs = [0]

            def link(ins):
                steps[0] += 1
                ins.then_inc(sem("dve_step"), 1)
                dve.wait_ge(sem("dve_step"), steps[0])

            def roots_of(src, eps, lo, hi):
                roots[0] += 1
                dve.tensor_scalar(ve[:, lo:hi], src, eps, None, ALU.add).then_inc(sem("var"), 1)
                dve.wait_ge(sem("rstd"), roots[0])

            def normalise(src, dst, lo, hi):
                for t in range(lo, hi):
                    last = dve.bn_stats(st[:, t, :], src[:, t, :])
                link(last)
                for t in range(lo, hi):
                    last = dve.bn_aggr(mv[:, t, :], st[:, t, :])
                link(last)
                roots_of(mv[:, lo:hi, 1], LN_EPS, lo, hi)
                for t in range(lo, hi):
                    last = dve.tensor_scalar(dst[:, t, :], src[:, t, :], mv[:, t, 0:1], rstd[:, t:t + 1],
                                             ALU.subtract, ALU.mult)
                return last

            def rms_scaled(w, lo, hi):
                squares[0] += hi - lo
                dve.wait_ge(sem("ms"), squares[0])
                roots_of(ms[:, lo:hi], RMS_EPS, lo, hi)
                for t in range(lo, hi):
                    last = dve.scalar_tensor_tensor(out=Z[:, t, :], in0=Z[:, t, :], scalar=rstd[:, t:t + 1],
                                                    in1=rows[:, w, :], op0=ALU.mult, op1=ALU.mult)
                return last

            def to_z(ins):
                zs[0] += 1
                ins.then_inc(sem("z"), 1)
                dve.wait_ge(sem("z"), zs[0])

            def queries(src):
                for hl in range(2):
                    last = dve.tensor_scalar(qp[:, :, hl, :], src, parity(hl), None, ALU.mult)
                last.then_inc(sem("qp"), 1)

            def gates(g):
                n = TH
                got = ps[:, CHAIN_B + 3, 0:16 * TH].rearrange("p (t c) -> p t c", c=16)[:, :, 0:GRP + E]
                dve.tensor_tensor(lg[:, :, :], got, ebias[:, :].unsqueeze(1).to_broadcast([P, n, GRP + E]),
                                  ALU.add).then_inc(sem("logits"), 1)
                dve.wait_ge(sem("logits"), g + 1)
                link(dve.tensor_reduce(gm[:, :], lg[:, :, 0:GRP], AX.X, ALU.max))
                dve.tensor_tensor(eg[:, :, :], lg[:, :, 0:GRP], gm[:, :].unsqueeze(2).to_broadcast([P, n, GRP]),
                                  ALU.subtract).then_inc(sem("gates_a"), 1)
                dve.wait_ge(sem("eg"), g + 1)
                link(dve.tensor_reduce(gsum[:, :], eg[:, :, :], AX.X, ALU.add))
                link(dve.reciprocal(gprob[:, :], gsum[:, :]))
                link(dve.tensor_tensor(ind[:, :, 0], eg[:, :, 0], eg[:, :, 1], ALU.is_ge))
                link(dve.tensor_scalar(ind[:, :, 1], ind[:, :, 0], -1.0, 1.0, ALU.mult, ALU.add))
                link(dve.tensor_scalar(off[:, :, :], ind[:, :, :], -LOW, LOW, ALU.mult, ALU.add))
                by_group = lg[:, :, GRP:GRP + E].rearrange("p t (g e) -> p t g e", g=GRP)
                em4 = em[:, :, :].rearrange("p t (g e) -> p t g e", g=GRP)
                wide = [P, n, GRP, E // GRP]
                link(dve.tensor_tensor(em4, by_group, ind[:, :, :].unsqueeze(3).to_broadcast(wide), ALU.mult))
                link(dve.tensor_tensor(em4, em4, off[:, :, :].unsqueeze(3).to_broadcast(wide), ALU.add))
                link(dve.tensor_reduce(emax[:, :], em[:, :, :], AX.X, ALU.max))
                dve.tensor_tensor(em[:, :, :], em[:, :, :], emax[:, :].unsqueeze(2).to_broadcast([P, n, E]),
                                  ALU.subtract).then_inc(sem("gates_b"), 1)
                dve.wait_ge(sem("ee"), g + 1)
                link(dve.tensor_reduce(esum[:, :], pe8[:, :, :], AX.X, ALU.add))
                link(dve.reciprocal(erec[:, :], esum[:, :]))
                link(dve.tensor_tensor(erec[:, :], erec[:, :], gprob[:, :], ALU.mult))
                link(dve.tensor_tensor(pe8[:, :, :], pe8[:, :, :], erec[:, :].unsqueeze(2).to_broadcast([P, n, E]), ALU.mult))
                for t in range(n):
                    last = dve.max(top[:, t, :], pe8[:, t, :])
                link(last)
                for t in range(n):
                    last = dve.max_index(topi[:, t, :], top[:, t, :], pe8[:, t, :])
                link(last)
                link(dve.tensor_copy(topf[:, :, :], topi[:, :, :]))
                for t in range(n):
                    for k, dst in enumerate((w8a, w8)):
                        last = dve.tensor_scalar(dst[:, TH * g + t, :], const("iota"), topf[:, t, k:k + 1],
                                                 top[:, t, k:k + 1], ALU.is_equal, ALU.mult)
                link(last)
                both = slice(TH * g, TH * g + TH)
                link(dve.tensor_tensor(w8[:, both, :], w8[:, both, :], w8a[:, both, :], ALU.add))

            for step, i in plan:
                if step == "norm0":
                    dve.wait_ge(sem("x_in"), 16)
                    to_z(normalise(X, Z, 0, T))
                elif step == "masked":
                    dve.wait_ge(sem("mask_in"), 16)
                    link(dve.tensor_reduce(flag[:, 0:1], mask[:, :].bitcast(I32), AX.X, ALU.max))
                    dve.tensor_scalar(flags[:, :], const("tile_of"), flag[:, 0:1], 0.0, ALU.mult, ALU.is_gt).then_inc(sem("flag"), 1)
                    dve.tensor_tensor(X[:, :, :], X[:, :, :], rows[:, 1, :].unsqueeze(1).to_broadcast([P, T, D]), ALU.add)
                    dve.wait_ge(sem("flags"), 1)
                    dve.tensor_scalar(nan_a[:, :], ps[:, CHAIN_B + 2, 0:T], -LOW, -LOW, ALU.mult, ALU.mult).then_inc(sem("nan"), 1)
                    dve.wait_ge(sem("nan"), 1)
                    link(dve.tensor_tensor(nan_b[:, :], nan_a[:, :], nan_a[:, :], ALU.subtract))
                    dve.wait_ge(sem("turned"), 2)
                    for t in range(T):
                        last = dve.scalar_tensor_tensor(out=Z[:, t, :], in0=Z[:, t, :], scalar=nan_b[:, t:t + 1],
                                                        in1=rows[:, 2, :], op0=ALU.add, op1=ALU.add)
                    link(last)
                elif step == "split":
                    c = i % CH_B
                    dve.wait_ge(sem("high_done"), i + 1)
                    if i >= CH_B:
                        dve.wait_ge(sem("gram_chunk"), i - CH_B + 1)
                    for p, lo, hi in [(P, 0, ROWS)] + ([(TAIL, ROWS, ROWS + 1)] if c == CH_B - 1 else []):
                        last = dve.tensor_tensor(halves(cl[0:p, c, lo:hi, :]),
                                                 halves(raw[0:p, ROWS * c + lo:ROWS * c + hi, :]),
                                                 halves(f32(ch[0:p, c, lo:hi, :]))[:, :, :, 0:P], ALU.subtract)
                    last.then_inc(sem("low_done"), 1)
                elif step == "evac":
                    dve.wait_ge(sem("gram_chunk"), CH_B * (i + 1))
                    if i >= 2:
                        dve.wait_ge(sem("gpre"), i - 1)
                    dve.tensor_copy(gab[:, i % 2, 1, :, :].rearrange("p c n -> p (c n)"),
                                    ps[:, GRAM_B[1], 0:3 * GBLK]).then_inc(sem("gb"), 1)
                elif step == "cross1":
                    dve.wait_ge(sem("g_turned"), i + 1)
                    dve.wait_ge(sem("gpre"), i + 1)
                    if i:
                        dve.wait_ge(sem("u"), i)
                    turned = ps[:, CROSS_B[0], :].rearrange("p (c n) -> p c n", n=P)
                    dve.tensor_tensor(gs[:, 0:2, :], gpre[:, i % 2, :, 0:P], turned[:, 0:2, :], ALU.add)
                    dve.wait_ge(sem("ga"), i + 1)
                    dve.tensor_tensor(gs[:, 2, :], gab[:, i % 2, 0, 2, 0:P], turned[:, 2, :], ALU.add)
                    dve.tensor_tensor(gs[:, 3, :], gab[:, i % 2, 1, 0, 0:P], turned[:, 3, :], ALU.add).then_inc(sem("gs"), 1)
                elif step == "cross2":
                    if i == 0:
                        dve.wait_ge(sem("rows_in"), 16)
                        dve.wait_ge(sem("cols_in"), 16)
                    dve.wait_ge(sem("sv"), i + 1)
                    dve.scalar_tensor_tensor(out=svn[:, :], in0=rows[:, 3, :], scalar=float(N),
                                             in1=ps[:, CROSS_B[0], 0:D], op0=ALU.mult, op1=ALU.add)
                    dve.wait_ge(sem("u"), i + 1)
                    dve.wait_ge(sem("gpre"), i + 1)
                    if i:
                        dve.wait_ge(sem("kv"), i)
                    for ib in range(KC):
                        last = dve.scalar_tensor_tensor(out=cv[:, ib, :], in0=rows[:, 3, :], scalar=gpre[:, i % 2, ib, P:P + 1],
                                                        in1=ps[:, CROSS_B[1], ib * D:(ib + 1) * D],
                                                        op0=ALU.mult, op1=ALU.add)
                    last.then_inc(sem("cv"), 1)
                elif step == "cross3":
                    dve.wait_ge(sem("kv"), i + 1)
                    for ob in range(KC):
                        last = dve.scalar_tensor_tensor(
                            out=m1[:, ob, :], in0=svn[:, ob * P:(ob + 1) * P], scalar=cols[:, 2 + ob:3 + ob],
                            in1=ps[:, CROSS_B[0], D + ob * P:D + (ob + 1) * P], op0=ALU.mult, op1=ALU.add)
                    link(last)
                    if i:
                        dve.wait_ge(sem("ctx"), i)
                    dve.tensor_tensor(mb[:, :, :], m1[:, :, :], const("heads").unsqueeze(1).to_broadcast([P, KC, P]),
                                      ALU.mult).then_inc(sem("mb"), 1)
                elif step == "xo":
                    lo, hi = TH * i, TH * i + TH
                    dve.wait_ge(sem("xo"), i + 1)
                    dve.tensor_tensor(Z[:, lo:hi, :], Z[:, lo:hi, :],
                                      ps[:, CHAIN_B, :].rearrange("p (t n) -> p t n", t=TH), ALU.add).then_inc(sem("y"), 1)
                    dve.wait_ge(sem("y"), i + 1)
                    link(normalise(Z, Z, lo, hi))
                    link(dve.tensor_tensor(Z[:, lo:hi, :], Z[:, lo:hi, :],
                                           rows[:, 0, :].unsqueeze(1).to_broadcast([P, TH, D]), ALU.mult))
                    link(dve.tensor_tensor(X[:, lo:hi, :], X[:, lo:hi, :], Z[:, lo:hi, :], ALU.add))
                elif step == "norm1":
                    to_z(normalise(X, Z, TH * i, TH * i + TH))
                elif step == "proj1":
                    dve.wait_ge(sem("q1"), i + 1)
                    if i:
                        dve.wait_ge(sem("scores"), 4 * i)
                    queries(ps[:, CHAIN_B + 2, :].rearrange("p (c n) -> p c n", n=S))
                elif step == "score":
                    k = i % 2
                    rows_of = prob[:, k, :, :].rearrange("p c (b k) -> p (c b) k", b=2)
                    wide = [P, H, S]
                    dve.wait_ge(sem("scores"), i + 1)
                    got = ps[:, CHAIN_B + 2 * k:CHAIN_B + 2 * k + 2, :].rearrange("p b (c k) -> p (b c) k", k=S)
                    if i // 2 % 2 == 0:
                        link(dve.tensor_tensor(rows_of, got, const("causal").unsqueeze(1).to_broadcast(wide), ALU.add))
                        got = rows_of
                    link(dve.tensor_reduce(mx[:, k, :], got, AX.X, ALU.max))
                    dve.tensor_tensor(rows_of, got, mx[:, k, :].unsqueeze(2).to_broadcast(wide),
                                      ALU.subtract).then_inc(sem("shifted"), 1)
                elif step == "turn_p":
                    k = i % 2
                    dve.wait_ge(sem("prob"), i + 1)
                    link(dve.tensor_reduce(sm[:, k, :], prob[:, k, :, :].rearrange("p c (b k) -> p (c b) k", b=2), AX.X, ALU.add))
                    link(dve.reciprocal(rs[:, k, :], sm[:, k, :]))
                elif step == "values":
                    k = i % 2
                    dve.wait_ge(sem("pv"), i + 1)
                    shape = [P, H // 2, 2, 2 * HD]
                    dve.tensor_tensor(on[k][:, :, :, :, :].rearrange("p b j r d -> p (j r) b d"),
                                      ps[:, CHAIN_B + 2 * k, :].rearrange("p (c b d) -> p c b d", b=2, d=2 * HD),
                                      rs[:, k, :].rearrange("p (c b) -> p c b", b=2).unsqueeze(3).to_broadcast(shape),
                                      ALU.mult).then_inc(sem("on"), 1)
                elif step == "turn_o":
                    k = i % 2
                    dve.wait_ge(sem("o_turned"), i + 1)
                    both = ps[:, CHAIN_B + 2 * k, :].rearrange("p (c h q) -> p c h q", h=2, q=S)
                    a = aT[k][:, :, :, :].rearrange("p j b q -> p (j b) q")
                    link(dve.tensor_scalar(a, both[:, :, 0, :], parity(0), None, ALU.mult))
                    dve.scalar_tensor_tensor(out=a, in0=both[:, :, 1, :], scalar=parity(1), in1=a,
                                             op0=ALU.mult, op1=ALU.add).then_inc(sem("aT"), 1)
                elif step == "project":
                    kind, t = i // 2 % 2, TH * (i // 4) + i % 2
                    dve.wait_ge(sem("ao"), i + 1)
                    o = ps[:, CHAIN_B + 2 * (i % 2) + 1, 0:D]
                    if kind == 0:
                        dve.tensor_tensor(X[:, t, :], X[:, t, :], o, ALU.add).then_inc(sem("x2"), 1)
                    else:
                        dve.tensor_tensor(Z[:, t, :], Z[:, t, :], o, ALU.add).then_inc(sem("s2"), 1)
                elif step == "norm2":
                    dve.wait_ge(sem("x2"), TH * i + TH)
                    to_z(normalise(X, Z, TH * i, TH * i + TH))
                elif step == "proj2":
                    dve.wait_ge(sem("scores"), 4 * i + 2)
                    sin = const("sin").unsqueeze(1).to_broadcast([P, KC * BH, S])
                    for n, (src, bank) in enumerate(((qs, CHAIN_B + 2), (ks, CHAIN_B))):
                        dve.wait_ge(sem("rot"), 2 * i + n + 1)
                        link(dve.tensor_tensor(ropet[:, :, :], ps[:, bank, :].rearrange("p (c n) -> p c n", n=S), sin, ALU.mult))
                        dve.wait_ge(sem("by_cos"), 2 * i + n + 1)
                        if n == 0:
                            dve.tensor_tensor(qs[:, :, :], qs[:, :, :], ropet[:, :, :], ALU.add).then_inc(sem("roped"), 1)
                            dve.wait_ge(sem("roped"), 2 * i + 1)
                            queries(qs[:, :, :])
                        else:
                            for r in range(4):
                                q = slice(32 * r, 32 * r + 32)
                                last = dve.tensor_tensor(kblk[q, :, r, :], ks[q, :, :], ropet[q, :, :], ALU.add)
                            last.then_inc(sem("roped"), 1)
                elif step == "rms1":
                    to_z(rms_scaled(4, TH * i, TH * i + TH))
                elif step == "turn_x":
                    dve.wait_ge(sem("xH"), i + 1)
                    dve.tensor_tensor(xHL[:, 1, :, :], xT[:, :, :], f32(xHL[:, 0, :, :]), ALU.subtract).then_inc(sem("xL"), 1)
                elif step == "gate":
                    dve.wait_ge(sem("gates"), i + 1)
                    gates(i)
                elif step == "hidden":
                    use = dense_use(step, i)
                    m = i % 8
                    dve.wait_ge(sem("silu"), i + 1)
                    dve.tensor_tensor(sa[:, m % 2, :], sa[:, m % 2, :], ps[:, DENSE_B[use % 4], TOK:2 * TOK],
                                      ALU.mult).then_inc(sem("taken"), 1)
                elif step == "shared":
                    use = dense_use(step, i)
                    dve.wait_ge(sem("products"), use + 1)
                    dve.tensor_tensor(Z[:, i, :], Z[:, i, :], ps[:, DENSE_B[use % 4], 0:D], ALU.add).then_inc(sem("taken"), 1)
                    dve.wait_ge(sem("taken"), use + 1)
                elif step == "experts":
                    use = dense_use(step, i)
                    t, u = i
                    dve.wait_ge(sem("products"), use + 1)
                    for e in range(2):
                        ins = dve.scalar_tensor_tensor(
                            out=Z[:, t, :], in0=ps[:, DENSE_B[use % 4], e * D:(e + 1) * D],
                            scalar=w8[:, t, 2 * u + e:2 * u + e + 1], in1=Z[:, t, :], op0=ALU.mult, op1=ALU.add)
                        if e == 0:
                            link(ins)
                    ins.then_inc(sem("taken"), 1)
                    dve.wait_ge(sem("taken"), use + 1)
                elif step == "finish":
                    link(rms_scaled(5, i, i + 1))
                    dve.tensor_tensor(X[:, i, :], X[:, i, :], Z[:, i, :], ALU.add).then_inc(sem("x3"), 1)


def kernel(x, ctx_1024, mask_Bx1xSxS2_bf0, L0_xattn_wq_w, L0_xattn_wq_b, L0_xattn_wk_w, L0_xattn_wk_b, L0_xattn_wv_w,
           L0_xattn_wv_b, L0_xattn_wo_w, L0_xattn_wo_b, L0_xattn_ln_g, L0_xattn_ln_b, L0_attn_Wq, L0_attn_Wk,
           L0_attn_Wv, L0_attn_Wo, L0_ffn_Wq, L0_ffn_Wk_c, L0_ffn_Wv_c, L0_ffn_Wk, L0_ffn_Wv, L0_ffn_Wo,
           L0_ffn_W_shared_in, L0_ffn_W_shared_out, L0_ffn_W1_shared, L0_ffn_W2_experts, L0_ffn_Wg_gate,
           L0_ffn_We_gate, L0_ffn_group_bias, L0_ffn_expert_bias, L0_ffn_norm1_w, L0_ffn_norm2_w):
    import concourse.bacc as bacc
    from concourse.bass_utils import run_bass_kernel_spmd as run

    def a(v):
        return np.asarray(v)

    def chunks(w):
        w = a(w)
        return w.reshape(w.shape[0] // P, P, w.shape[1]).transpose(1, 0, 2)

    arrays = {
        "x": a(x).reshape(T, P, D).transpose(1, 0, 2),
        "ctx": a(ctx_1024),
        "mask": a(mask_Bx1xSxS2_bf0).reshape(P, B * S * N // P),
        "const": constants(),
        "w0": np.stack([chunks(a(w).T) for w in (L0_xattn_wq_w, L0_xattn_wk_w, L0_xattn_wv_w, L0_xattn_wo_w)], 1),
        "w1": np.stack([chunks(a(w).T) for w in (L0_attn_Wq, L0_attn_Wk, L0_attn_Wv, L0_attn_Wo)], 1),
        "wq": chunks(L0_ffn_Wq),
        "wkvc": np.concatenate([chunks(L0_ffn_Wk_c), chunks(L0_ffn_Wv_c)], 2),
        "wkv": np.concatenate([a(L0_ffn_Wk), a(L0_ffn_Wv)], 0),
        "wo": chunks(L0_ffn_Wo),
        "gate": np.concatenate([chunks(L0_ffn_Wg_gate), chunks(L0_ffn_We_gate)], 2),
        "dense": np.concatenate([chunks(L0_ffn_W_shared_in), chunks(L0_ffn_W1_shared),
                                 chunks(L0_ffn_W_shared_out).reshape(P, 1, 4 * D)], 1),
        "w2": a(L0_ffn_W2_experts).reshape(E // 2, 2, HID // P, P, D).transpose(3, 0, 2, 1, 4).reshape(P, 8, 1024),
        "cols": np.concatenate([a(L0_xattn_wq_b).reshape(KC, P).T, a(L0_xattn_wk_b).reshape(KC, P).T], 1),
        "rows": np.stack([a(r) for r in (L0_xattn_ln_g, L0_xattn_ln_b, L0_xattn_wo_b, L0_xattn_wv_b,
                                         L0_ffn_norm1_w, L0_ffn_norm2_w)], 0),
        "ebias": np.concatenate([a(L0_ffn_group_bias), a(L0_ffn_expert_bias)], 0),
    }
    arrays = {k: np.ascontiguousarray(v) for k, v in arrays.items()}
    nc = bacc.Bacc("TRN2", target_bir_lowering=False, num_devices=1)
    args = [nc.dram_tensor("in_" + k, v.shape, mybir.dt.from_np(v.dtype), kind="ExternalInput").ap()
            for k, v in arrays.items()]
    o = nc.dram_tensor("out_x", (B * S, D), F32, kind="ExternalOutput").ap()
    layer(nc, *args, o)
    r = run(nc, [{"in_" + k: v for k, v in arrays.items()}], core_ids=[0])
    return r.results[0]["out_x"].reshape(B, S, D)
```

```python
from contextlib import ExitStack

import numpy as np

import concourse.bass as bass
from concourse import mybir

ALU = mybir.AluOpType
ACT = mybir.ActivationFunctionType
AX = mybir.AxisListType
F32 = mybir.dt.float32
F32R = mybir.dt.float32r
U8 = mybir.dt.uint8
I32 = mybir.dt.int32
U32 = mybir.dt.uint32

P = 128
B, S, D = 8, 64, 256
N = 1601
H, HD = 16, 16
KC = D // P
T = B * S // P
HALVES = 2
TH = T // HALVES
BH = B // HALVES
TOK = TH * P
ROWS = 4
CH_B = 3
TAIL = N - CH_B * ROWS * P
SLOT = ROWS + 1
HROW = D + 4
HID = 512
E = 8
GRP = 2
LN_EPS = 1e-5
RMS_EPS = 1e-6
LOW = -3.0e38
SCALE = 1.0 / float(np.sqrt(HD))
XSCALE = 1.0 / float(np.float32(np.float16(np.sqrt(np.float16(HD)))) + np.float32(1e-8))

CONST = {}
_at = 0
for _name, _width in (("ident", P), ("parity", 2), ("heads", P), ("causal", S), ("cos", S), ("sin", S),
                      ("rot", P), ("side", P), ("tile_of", T), ("iota", E)):
    CONST[_name] = (_at, _at + _width)
    _at += _width
NCONST = _at


def constants():
    c = np.zeros((P, NCONST), np.float32)
    p = np.arange(P)

    def put(name, a):
        lo, hi = CONST[name]
        c[:, lo:hi] = a

    put("ident", np.eye(P))
    put("parity", (p[:, None] // HD) % 2 == np.arange(2)[None, :])
    put("heads", (p[:, None] // HD == p[None, :] // HD) * XSCALE)
    put("causal", np.where(np.arange(S)[None, :] <= p[:, None] % S, 0.0, LOW))
    freq = (1.0 / np.float32(10000.0) ** (np.arange(0, HD, 2, dtype=np.float32) / np.float32(HD))).astype(np.float32)
    ang = np.arange(S, dtype=np.float32)[None, :] * freq[(p % HD) // 2][:, None]
    put("cos", np.cos(ang.astype(np.float32)))
    put("sin", np.sin(ang.astype(np.float32)))
    rot = np.zeros((P, P), np.float32)
    rot[p[1::2], p[0::2]] = -1.0
    rot[p[0::2], p[1::2]] = 1.0
    put("rot", rot)
    put("side", (p[:, None] // (P // B)) % 2 == p[None, :] // S)
    put("tile_of", p[:, None] // (2 * P // B) == np.arange(T)[None, :])
    put("iota", np.arange(E)[None, :])
    return c


NU = 5 + 8
STAGED = 4
GBLK = P + 2
GRAM_B = (0, 1)
CROSS_B = (6, 7)
CHAIN_B = 2
DENSE_B = (0, 1, 6, 7)
USES = 8 + TH * (1 + E // 2)


def context_steps():
    out = [("split", 0), ("split", 1)]
    for b in range(BH + 1):
        for c in range(CH_B):
            n = CH_B * b + c
            out += [("split", n + 2), ("gram", n)]
            if c == CH_B - 1:
                out.append(("evac", b))
            if b > 1 and c == 0:
                out.append(("cross4", b - 2))
            if b:
                if c == 1:
                    out.append(("cross2_product", b - 1))
                out.append((f"cross{c + 1}", b - 1))
            if n in (2, 7):
                out.append(("norm0", n // 6))
            if n in (4, 10):
                out.append(("pre", n // 6))
            if n in (6, 11, 12):
                out.append(({6: "flag", 11: "flags", 12: "masked"}[n], 0))
    n = CH_B * (BH + 1)
    return out + [("split", n + 2), ("gram", n), ("cross4", BH - 1)]


def dense_of_tile(t):
    parts = [("shared", t)] + [("experts", (t, u)) for u in range(E // 2)]
    return [(name + "_product", i) for name, i in parts], parts


def first_chain_steps():
    b = BH
    n = CH_B * (b + 1)
    return [
        ("cross1", b), ("split", n + 3), ("xo_product", 0), ("xo", 0),
        ("cross2_product", b), ("cross2", b), ("gram", n + 1), ("norm1", 0), ("gram", n + 2), ("evac", b + 1),
        ("gram", n + 3), ("split", n + 4), ("turn_z", (0, 0)), ("cross3", b), ("split", n + 5), ("proj1_product", 0), ("proj1", 0),
        ("cross4", b), ("cross1", b + 1), ("split", n + 6), ("piece", 0),
        ("score_product", 0), ("score", 0), ("cross2_product", b + 1), ("cross2", b + 1), ("score_product", 1), ("gram", n + 4),
        ("turn_p", 0), ("score", 1), ("sums", 0), ("cross3", b + 1), ("gram", n + 5), ("turn_p", 1), ("evac", b + 2), ("sums", 1),
        ("values", 0), ("cross4", b + 1), ("values", 1), ("cross1", b + 2), ("piece", 1),
        ("turn_o", 0), ("turn_o", 1), ("cross2_product", b + 2), ("cross2", b + 2), ("project", 0), ("project", 1), ("split", n + 7),
        ("norm2", 0), ("gram", n + 6), ("gram", n + 7), ("turn_z", (0, 1)), ("cross3", b + 2), ("split", n + 8),
        ("proj2", 0), ("gram", n + 8), ("evac", b + 3), ("cross4", b + 2), ("cross1", b + 3),
        ("score_product", 2), ("score", 2), ("score_product", 3), ("cross2_product", b + 3), ("turn_p", 2), ("score", 3),
        ("cross2", b + 3), ("sums", 2), ("turn_p", 3), ("sums", 3), ("piece", 2), ("cross3", b + 3), ("values", 2), ("values", 3),
        ("piece", 3), ("turn_o", 2), ("turn_o", 3), ("cross4", b + 3), ("project", 2), ("project", 3),
        ("xo_product", 1), ("rms1", 0), ("turn_x", 0), ("xo", 1), ("piece", 4),
    ]


def second_chain_steps():
    product, hidden = [[(name, m) for m in range(8)] for name in ("hidden_product", "hidden")]
    piece = [("piece", u) for u in range(5, NU)]
    (a, add_a), (b, add_b) = (dense_of_tile(t) for t in range(TH))
    return [
        ("norm1", 1), *product[0:2], ("gates", 0), *product[2:4], *hidden[0:4], piece[0], *product[4:7],
        ("turn_z", (1, 0)), product[7], ("proj1_product", 1), ("gate_groups", 0), *hidden[4:8], ("gate_experts", 0), ("proj1", 1),
        ("gate_best", 0), *piece[1:4],
        ("score_product", 4), ("score", 4), ("score_product", 5), piece[4], a[0], b[0], a[1], ("turn_p", 4), ("score", 5), ("sums", 4),
        a[2], ("turn_p", 5), ("sums", 5), piece[5], add_a[0], add_b[0], add_a[1], ("values", 4), ("values", 5),
        ("turn_o", 4), ("turn_o", 5), piece[6], ("project", 4), ("project", 5), ("norm2", 1), a[3], add_a[2], add_a[3],
        ("turn_z", (1, 1)), piece[7], ("proj2", 1), a[4], add_a[4],
        ("score_product", 6), ("score", 6), ("score_product", 7), b[1], ("turn_p", 6), ("score", 7), ("sums", 6),
        b[2], ("turn_p", 7), ("sums", 7), add_b[1], ("values", 6), ("values", 7), ("turn_o", 6), ("turn_o", 7),
        ("project", 6), ("project", 7), ("rms1", 1), b[3], add_b[2], add_b[3], ("turn_x", 1), b[4], add_b[4], ("gates", 1),
    ]


def second_dense_steps():
    a, b = ([step for pair in zip(*dense_of_tile(t)) for step in pair] for t in range(TH, T))
    product, hidden = [[(name, 8 + m) for m in range(8)] for name in ("hidden_product", "hidden")]
    hidden = product[0:2] + [step for m in range(6) for step in (hidden[m], product[m + 2])] + hidden[6:8]
    gate = [("gate_groups", 1), ("gate_experts", 1), ("gate_best", 1)]
    return [*hidden, *a[0:2], *b[0:2], *gate, *a[2:6], ("finish", 0), *a[6:8], ("finish", 1), *a[8:10],
            *b[2:4], ("finish", TH), *b[4:], ("finish", TH + 1)]


def steps_in_order():
    return context_steps() + first_chain_steps() + second_chain_steps() + second_dense_steps()


def layer(nc, d_x, d_ctx, d_mask, d_const, d_w0, d_w1, d_wq, d_wkvc, d_wkv, d_wo, d_gate, d_dense, d_w2,
          d_cols, d_rows, d_ebias, out):
    sb_at = (nc.sbuf_base + 63) // 64 * 64
    where = {}

    def place(name, shape, dt=F32, at=None):
        nonlocal sb_at
        size = int(np.prod(shape[1:])) * (1 if dt == U8 else 4)
        size = (size + 31) // 32 * 32
        if at is None:
            at = sb_at
            sb_at += size
        where[name] = at
        return nc.alloc_sbuf_tensor_at(name, shape, dt, offset=at), at + size

    half_arena = E // 4 * 2 * (HID // P) * 2 * D * 4
    w2, _ = place("w2", [P, E // 2, 2, HID // P, 2 * D], F32R)
    arena = where["w2"]
    ch, nxt = place("ch", [P, CH_B, SLOT, HROW], F32R, at=arena)
    cl, nxt = place("cl", [P, CH_B, SLOT, D], F32R, at=nxt)
    svn, nxt = place("svn", [P, D], at=nxt)
    assert nxt <= arena + half_arena
    w0, nxt = place("w0", [P, 4, KC, D], at=arena + half_arena)
    q0T, nxt = place("q0T", [P, KC, T * P], at=nxt)
    gab, nxt = place("gab", [P, 2, KC, 3, GBLK], at=nxt)
    gpre, nxt = place("gpre", [P, 2, KC, GBLK], at=nxt)
    gs, nxt = place("gs", [P, 4, P], at=nxt)
    crep, nxt = place("crep", [P, KC, P], at=nxt)
    cv, nxt = place("cv", [P, KC, D], at=nxt)
    m1, nxt = place("m1", [P, KC, P], at=nxt)
    mb, nxt = place("mb", [P, KC, P], at=nxt)
    ctxT, nxt = place("ctxT", [P, HALVES, KC, TOK], at=nxt)
    assert nxt <= arena + 2 * half_arena
    dense, _ = place("dense", [P, 2, 5, 1024], F32R)
    raw, _ = place("raw", [P, CH_B * ROWS + 1, D])
    cst, _ = place("cst", [P, NCONST])
    w1, _ = place("w1", [P, 4, KC, D])
    wq, _ = place("wq", [P, KC, D])
    wkvc, _ = place("wkvc", [P, KC, P])
    wkv, _ = place("wkv", [P, D])
    wo, _ = place("wo", [P, KC, D])
    gate, _ = place("gate", [P, KC, GRP + E])
    cols, _ = place("cols", [P, 4])
    rows, _ = place("rows", [P, 6, D])
    ebias, _ = place("ebias", [P, GRP + E])
    X, _ = place("X", [P, T, D])
    Z, _ = place("Z", [P, T, D])
    zT, _ = place("zT", [P, KC, TOK])
    st, _ = place("st", [P, T, 6])
    mv, _ = place("mv", [P, T, 2])
    ve, _ = place("ve", [P, T])
    rstd, _ = place("rstd", [P, T])
    half_exp, _ = place("half_exp", [P, T])
    flag, _ = place("flag", [P, 1])
    flags, _ = place("flags", [P, T])
    nan_a, _ = place("nan_a", [P, T])
    nan_b, _ = place("nan_b", [P, T])
    qp, _ = place("qp", [P, KC * BH, 2, S])
    z0T, _ = place("z0T", [P, KC, T * P], at=where["qp"])
    kblk, _ = place("kblk", [P, KC * BH, 4, S])
    vblk, _ = place("vblk", [P, TH, H // 2, 2, 2 * HD])
    prob, _ = place("prob", [P, TH, H // 2, 2 * S])
    on = [place(f"on{k}", [P, 2, KC, 4, 2 * HD], at=where["prob"] + k * 4096)[0] for k in range(TH)]
    aT = [place(f"aT{k}", [P, KC, 2, S], at=where["prob"] + k * 4096 + 2048)[0] for k in range(TH)]
    probT, _ = place("probT", [P, TH, H // 2, P])
    xT, _ = place("xT", [P, KC, TOK], at=where["probT"])
    qs, _ = place("qs", [P, KC * BH, S], at=where["probT"] + 2048)
    ropet, _ = place("ropet", [P, KC * BH, S], at=where["probT"] + 4096)
    ks, _ = place("ks", [P, KC * BH, S], at=where["probT"] + 6144)
    kvcT, _ = place("kvcT", [P, TOK], at=where["prob"])
    kcos, _ = place("kcos", [P, KC * BH, S], at=where["prob"] + 4096)
    mx, _ = place("mx", [P, TH, H])
    sm, _ = place("sm", [P, TH, H])
    rs, _ = place("rs", [P, TH, H])
    hT, _ = place("hT", [P, 2, 2, HID // P, TOK], F32R)
    mask, _ = place("mask", [P, B * S * N // P], U8, at=where["hT"])
    stage, _ = place("stage", [P, STAGED, 1024], at=where["hT"])
    sa, _ = place("sa", [P, 4, TOK])
    xHL, _ = place("xHL", [P, 2, KC, TOK], F32R)
    ms, _ = place("ms", [P, T])
    lg, _ = place("lg", [P, TH, GRP + E])
    gm, _ = place("gm", [P, TH])
    eg, _ = place("eg", [P, TH, GRP])
    gsum, _ = place("gsum", [P, TH])
    gprob, _ = place("gprob", [P, TH])
    ind, _ = place("ind", [P, TH, GRP])
    off, _ = place("off", [P, TH, GRP])
    em, _ = place("em", [P, TH, E])
    emax, _ = place("emax", [P, TH])
    esum, _ = place("esum", [P, TH])
    erec, _ = place("erec", [P, TH])
    pe8, _ = place("pe8", [P, TH, E])
    top, _ = place("top", [P, TH, 8])
    topi, _ = place("topi", [P, TH, 8], U32)
    topf, _ = place("topf", [P, TH, 8])
    w8a, _ = place("w8a", [P, T, E])
    w8, _ = place("w8", [P, T, E])
    assert sb_at <= nc.sbuf_usable_end, (sb_at, nc.sbuf_usable_end)

    def const(name):
        lo, hi = CONST[name]
        return cst[:, lo:hi]

    ident = const("ident")
    sq = raw[:, CH_B * ROWS, :]

    def parity(hl):
        lo, _ = CONST["parity"]
        return cst[:, lo + hl:lo + hl + 1]

    def f32(ap):
        return ap.bitcast(F32)

    def halves(ap):
        return ap.rearrange("p r (h n) -> p r h n", h=KC)

    def raw_piece(u):
        if u < STAGED:
            return stage[:, u, :]
        c = (u - STAGED) % CH_B
        return raw[:, ROWS * c:ROWS * (c + 1), :].rearrange("p r d -> p (r d)")

    def piece(u, part):
        if u < 5:
            return dense[:, part, u, :]
        u -= 5
        return w2[:, u // 2, part, 2 * (u % 2):2 * (u % 2) + 2, :].rearrange("p k n -> p (k n)")

    def dense_use(step, i):
        if step == "hidden":
            return USES * (i // 8) + i % 8
        if step == "shared":
            return USES * (i // TH) + 8 + i % TH
        return USES * (i[0] // TH) + 8 + TH + E // 2 * (i[0] % TH) + i[1]

    def tile_bank(n):
        return CHAIN_B + 2 - 2 * (n % 2)

    plan = steps_in_order()

    with ExitStack() as stack:
        ps = stack.enter_context(nc.psum_tensor("ps", [P, 8, 512], F32))
        sems = {}

        def sem(name):
            if name not in sems:
                sems[name] = stack.enter_context(nc.semaphore(name))
            return sems[name]

        block = stack.enter_context(nc.Block())

        @block.sync
        def _(sp):
            beside = {
                2: [(cst[:, :], d_const, "const_in")],
                3: [(w0[:, :, :, :], d_w0, "w0_in")],
                4: [(X[:, :, :], d_x, "x_in"), (cols[:, :], d_cols, "cols_in"),
                    (rows[:, :, :], d_rows.partition_broadcast(P), "rows_in")],
                5: [(mask[:, :], d_mask, "mask_in")],
                6: [(w1[:, :, :, :], d_w1, "w_in")],
                7: [(wq[:, :, :], d_wq, "w_in"), (wkvc[:, :, :], d_wkvc, "w_in")],
                8: [(wkv[:, :], d_wkv, "w_in"), (wo[:, :, :], d_wo, "w_in")],
                9: [(gate[:, :, :], d_gate, "w_in"), (ebias[:, :], d_ebias.partition_broadcast(P), "w_in")],
            }
            for n in range(CH_B * B):
                b, c = divmod(n, CH_B)
                if b:
                    sp.wait_ge(sem("low_done"), n - CH_B + 1)
                sp.dma_start(raw[:, ROWS * c:ROWS * (c + 1), :], d_ctx[b, 0:CH_B * ROWS * P, :].rearrange(
                    "(p r) d -> p r d", r=CH_B * ROWS)[:, c * ROWS:(c + 1) * ROWS, :]).then_inc(sem(f"raw{c}"), 16)
                if c == CH_B - 1:
                    sp.dma_start(raw[0:TAIL, ROWS * CH_B, :], d_ctx[b, CH_B * ROWS * P:N, :]).then_inc(sem(f"raw{c}"), 16)
                for dst, src, name in beside.get(n, ()):
                    sp.dma_start(dst, src).then_inc(sem(name), 16)
                if CH_B * BH <= n < CH_B * BH + STAGED:
                    u = n - CH_B * BH
                    sp.wait_ge(sem("flag"), 1)
                    sp.dma_start(raw_piece(u), d_dense[:, u, :]).then_inc(sem(f"staged{u}"), 16)
            for u in range(STAGED, NU):
                if u < STAGED + CH_B:
                    sp.wait_ge(sem("low_done"), CH_B * (B - 1) + u - STAGED + 1)
                else:
                    sp.wait_ge(sem("piece_low"), u - CH_B + 1)
                src = d_dense[:, u, :] if u < 5 else d_w2[:, u - 5, :]
                sp.dma_start(raw_piece(u), src).then_inc(sem(f"raw{(u - STAGED) % CH_B}"), 16)
            for t in range(T):
                sp.wait_ge(sem("x3"), t + 1)
                sp.dma_start(out[t * P:(t + 1) * P, :], X[:, t, :]).then_inc(sem("stored"), 16)
            sp.wait_ge(sem("stored"), 16 * T)

        def chunk_landed(eng, n):
            b, c = divmod(n, CH_B)
            eng.wait_ge(sem(f"raw{c}"), (32 if c == CH_B - 1 else 16) * (b + 1))

        def piece_landed(eng, u):
            if u < STAGED:
                eng.wait_ge(sem(f"staged{u}"), 16)
            else:
                k, c = divmod(u - STAGED, CH_B)
                eng.wait_ge(sem(f"raw{c}"), (32 if c == CH_B - 1 else 16) * B + 16 * (k + 1))

        @block.gpsimd
        def _(pool):
            ones = f32(ch[:, :, :, :]).rearrange("p c r (h n) -> p c r h n", h=KC)
            for c in range(CH_B):
                pool.memset(ones[:, c, :, :, P:P + 2], 1.0).then_inc(sem("ones"), 1)
            pool.memset(half_exp[:, :], -0.5).then_inc(sem("ones"), 1)
            pool.memset(kblk[:, :, :, :], 0.0).then_inc(sem("zeros"), 1)
            pool.memset(vblk[:, :, :, :, :], 0.0).then_inc(sem("zeros"), 1)
            pool.wait_ge(sem("ones"), CH_B + 1)
            pool.wait_ge(sem("const_in"), 16)
            roots = [0]

            def inverse_roots(lo, hi):
                roots[0] += 1
                pool.wait_ge(sem("var"), roots[0])
                pool.tensor_tensor(rstd[:, lo:hi], ve[:, lo:hi], half_exp[:, lo:hi], ALU.pow).then_inc(sem("rstd"), 1)

            for step, i in plan:
                if step == "norm0":
                    inverse_roots(TH * i, TH * i + TH)
                elif step == "masked":
                    pool.wait_ge(sem("rows_in"), 16)
                    pool.wait_ge(sem("z"), HALVES)
                    pool.tensor_tensor(X[:, :, :], X[:, :, :], rows[:, 1, :].unsqueeze(1).to_broadcast([P, T, D]),
                                       ALU.add).then_inc(sem("x_biased"), 1)
                elif step == "cross1":
                    pool.wait_ge(sem("g"), i + 1)
                    if i >= 2:
                        pool.wait_ge(sem("cv"), i - 1)
                        pool.wait_ge(sem("crep"), i - 1)
                    for k in range(KC):
                        last = pool.tensor_tensor(gpre[:, i % 2, k, :], gab[:, i % 2, k, k, :], gab[:, i % 2, k, k + 1, :], ALU.add)
                    last.then_inc(sem("gpre"), 1)
                elif step in ("xo", "norm1", "norm2", "rms1"):
                    inverse_roots(TH * i, TH * i + TH)
                elif step == "proj2":
                    pool.wait_ge(sem("rot"), 2 * i + 1)
                    pool.tensor_tensor(qs[:, :, :], qs[:, :, :], const("cos").unsqueeze(1).to_broadcast([P, KC * BH, S]),
                                       ALU.mult).then_inc(sem("by_cos"), 1)
                elif step == "piece":
                    pool.wait_ge(sem("piece_high"), i + 1)
                    pool.tensor_tensor(piece(i, 1), raw_piece(i), f32(piece(i, 0)), ALU.subtract).then_inc(sem("piece_low"), 1)
                elif step == "hidden":
                    m = i % 8
                    pool.wait_ge(sem("h_high"), i + 1)
                    pool.tensor_tensor(hT[:, m // 4, 1, m % 4, :], sa[:, m % 4, :], f32(hT[:, m // 4, 0, m % 4, :]),
                                       ALU.subtract).then_inc(sem("h_low"), 1)
                elif step == "finish":
                    inverse_roots(i, i + 1)

        @block.scalar
        def _(act):
            squares = [0]

            def copy(dst, src, name):
                act.activation(dst, src, ACT.Copy).then_inc(sem(name), 1)

            def z_out(dst, bank):
                copy(dst.rearrange("p k (t c) -> p t k c", c=P),
                     ps[:, bank, :].rearrange("p (t k c) -> p t k c", k=KC, c=P), "zT")

            def block_values(bank):
                for bb in range(2):
                    q = slice(bb * S, bb * S + S)
                    last = act.activation(vblk[q, :, :, bb, :].rearrange("p t c d -> p (t c) d"),
                                          ps[q, bank, :].rearrange("p (c d) -> p c d", d=2 * HD), ACT.Copy)
                last.then_inc(sem("v"), 1)

            def mean_square(t):
                if squares[0]:
                    act.wait_ge(sem("ms"), squares[0])
                else:
                    act.wait_ge(sem("low_done"), CH_B * B)
                squares[0] += 1
                act.activation(sq, Z[:, t, :], ACT.Square, scale=D ** -0.5,
                               accum_out=ms[:, t:t + 1]).then_inc(sem("ms"), 1)

            for step, i in plan:
                if step == "pre":
                    if i == 0:
                        act.wait_ge(sem("cols_in"), 16)
                    act.wait_ge(sem("turned"), i + 1)
                    z_out(z0T[:, :, i * TOK:(i + 1) * TOK], CHAIN_B + i)
                    act.wait_ge(sem("q0"), i + 1)
                    for ob in range(KC):
                        last = act.activation(q0T[:, ob, i * TOK:(i + 1) * TOK], ps[:, CHAIN_B + 2 + i, ob * TOK:(ob + 1) * TOK],
                                              ACT.Identity, bias=cols[:, ob:ob + 1])
                    last.then_inc(sem("q0T"), 1)
                elif step == "split":
                    c = i % CH_B
                    chunk_landed(act, i)
                    if i >= CH_B:
                        act.wait_ge(sem("gram_chunk"), i - CH_B + 1)
                    if i == 0:
                        act.wait_ge(sem("ones"), CH_B)
                    for p, lo, hi in [(P, 0, ROWS)] + ([(TAIL, ROWS, ROWS + 1)] if c == CH_B - 1 else []):
                        last = act.activation(halves(ch[0:p, c, lo:hi, :])[:, :, :, 0:P],
                                              halves(raw[0:p, ROWS * c + lo:ROWS * c + hi, :]), ACT.Copy)
                    last.then_inc(sem("high_done"), 1)
                elif step == "evac":
                    act.wait_ge(sem("gram_chunk"), CH_B * (i + 1))
                    if i >= 2:
                        act.wait_ge(sem("gs"), i - 1)
                    copy(gab[:, i % 2, :, :, :].rearrange("p k c n -> p k (c n)"), ps[:, GRAM_B[0]:GRAM_B[1] + 1, 0:3 * GBLK], "g")
                elif step == "cross1":
                    act.wait_ge(sem("gpre"), i + 1)
                    if i == 0:
                        act.wait_ge(sem("const_in"), 16)
                    if i:
                        act.wait_ge(sem("sv"), i)
                    for k in range(KC):
                        last = act.activation(crep[:, k, :], ident, ACT.Identity, scale=0.0,
                                              bias=gpre[:, i % 2, k, P:P + 1])
                    last.then_inc(sem("crep"), 1)
                elif step == "cross4":
                    act.wait_ge(sem("ctx"), i + 1)
                    copy(ctxT[:, i // BH, :, (i % BH) * S:(i % BH + 1) * S],
                         ps[:, CROSS_B[1], 0:KC * S].rearrange("p (k n) -> p k n", k=KC), "ctxT")
                elif step == "turn_z":
                    g, k = i
                    act.wait_ge(sem("turned"), 3 + 3 * g + k)
                    z_out(zT[:, :, :], CHAIN_B + 1)
                elif step == "proj1":
                    act.wait_ge(sem("k1"), i + 1)
                    if i:
                        act.wait_ge(sem("scores"), 4 * i)
                    else:
                        act.wait_ge(sem("zeros"), 2)
                    for r in range(4):
                        q = slice(32 * r, 32 * r + 32)
                        last = act.activation(kblk[q, :, r, :], ps[q, CHAIN_B + 3, :].rearrange("p (c n) -> p c n", n=S), ACT.Copy)
                    last.then_inc(sem("kblk"), 1)
                    act.wait_ge(sem("v1"), i + 1)
                    if i:
                        act.wait_ge(sem("pv"), 4 * i)
                    block_values(CHAIN_B)
                elif step == "score":
                    act.wait_ge(sem("shifted"), i + 1)
                    act.activation(prob[:, i % 2, :, :], prob[:, i % 2, :, :], ACT.Exp,
                                   scale=SCALE).then_inc(sem("prob"), 1)
                elif step == "turn_p":
                    for j in range(2):
                        act.wait_ge(sem("p_turned"), 2 * i + j + 1)
                        if i >= 2:
                            act.wait_ge(sem("pv"), i - 1)
                        copy(probT[:, i % 2, 4 * j:4 * j + 4, :],
                             ps[:, tile_bank(i) + j, :].rearrange("p (c n) -> p c n", n=P), "probT")
                elif step == "proj2":
                    act.wait_ge(sem("q2"), i + 1)
                    copy(qs[:, :, :], ps[:, CHAIN_B, :].rearrange("p (c n) -> p c n", n=S), "qs")
                    act.wait_ge(sem("kvc"), i + 1)
                    if i:
                        act.wait_ge(sem("v2"), i)
                    copy(kvcT[:, :], ps[:, CHAIN_B + 1, 0:TOK], "kvcT")
                    act.wait_ge(sem("k2"), i + 1)
                    copy(ks[:, :, :], ps[:, CHAIN_B + 3, :].rearrange("p (c n) -> p c n", n=S), "ks")
                    act.wait_ge(sem("v2"), i + 1)
                    act.wait_ge(sem("pv"), 4 * i + 2)
                    block_values(CHAIN_B + 1)
                    act.wait_ge(sem("roped"), 2 * i + 1)
                    act.wait_ge(sem("scores"), 4 * i + 2)
                    for hl in range(2):
                        last = act.activation(qp[:, :, hl, :], qs[:, :, :], ACT.Copy, scale=parity(hl))
                    last.then_inc(sem("qp"), 1)
                    act.wait_ge(sem("k_sum"), i + 1)
                    for r in range(2, 4):
                        q = slice(32 * r, 32 * r + 32)
                        last = act.activation(kblk[q, :, r, :], kcos[q, :, :], ACT.Copy)
                    last.then_inc(sem("kblk"), 1)
                elif step == "rms1":
                    act.wait_ge(sem("s2"), TH * i + TH)
                    for t in range(TH * i, TH * i + TH):
                        mean_square(t)
                elif step == "turn_x":
                    act.wait_ge(sem("turned"), 5 + 3 * i)
                    if i:
                        act.wait_ge(sem("products"), USES * (i - 1) + 8)
                    turned = ps[:, CHAIN_B + 2, :].rearrange("p (t k c) -> p t k c", k=KC, c=P)
                    copy(xHL[:, 0, :, :].rearrange("p k (t c) -> p t k c", c=P), turned, "xH")
                    act.wait_ge(sem("xL"), i + 1)
                    copy(xT[:, :, :].rearrange("p k (t c) -> p t k c", c=P), turned, "xT")
                elif step == "gate_groups":
                    act.wait_ge(sem("gates_a"), i + 1)
                    act.activation(eg[:, :, :], eg[:, :, :], ACT.Exp).then_inc(sem("eg"), 1)
                elif step == "gate_experts":
                    act.wait_ge(sem("gates_b"), i + 1)
                    act.activation(pe8[:, :, :], em[:, :, :], ACT.Exp).then_inc(sem("ee"), 1)
                elif step == "piece":
                    piece_landed(act, i)
                    if i >= 5:
                        act.wait_ge(sem("xo"), HALVES)
                    copy(piece(i, 0), raw_piece(i), "piece_high")
                elif step == "hidden_product":
                    use = dense_use("hidden", i)
                    act.wait_ge(sem("products"), use + 1)
                    if i >= 4:
                        act.wait_ge(sem("h_low"), i - 3)
                    act.activation(sa[:, i % 4, :], ps[:, DENSE_B[use % 4], 0:TOK], ACT.Silu).then_inc(sem("silu"), 1)
                elif step == "hidden":
                    use = dense_use(step, i)
                    m = i % 8
                    act.wait_ge(sem("taken"), use + 1)
                    if m == 0 and i:
                        act.wait_ge(sem("products"), USES)
                    copy(hT[:, m // 4, 0, m % 4, :], sa[:, m % 4, :], "h_high")
                elif step == "finish":
                    act.wait_ge(sem("taken"), dense_use("experts", (i, E // 2 - 1)) + 1)
                    mean_square(i)

        @block.tensor
        def _(pe):
            def mm(o, l, r, start, stop, check=True):
                return pe.matmul(o, l, r, start=start, stop=stop, skip_group_check=not check)

            def turn(o, src):
                return pe.transpose(o, src, ident)

            def turn_rows(lo_tile, bank):
                for t in range(TH):
                    for k in range(KC):
                        last = turn(ps[:, bank, t * D + k * P:t * D + (k + 1) * P], Z[:, lo_tile + t, k * P:(k + 1) * P])
                last.then_inc(sem("turned"), 1)

            def gram_tile(slot, r, p, first, last):
                row = ch[0:p, slot, r, :].rearrange("p (h n) -> p h n", h=KC)
                h0, h1 = row[:, 0, 0:P], row[:, 1, 0:P]
                l0, l1 = cl[0:p, slot, r, 0:P], cl[0:p, slot, r, P:2 * P]
                a, b = (ps[:, bank, 0:3 * GBLK].rearrange("p (c n) -> p c n", n=GBLK) for bank in GRAM_B)
                mm(a[:, 0, :], h0, row[:, 0, :], first, False, False)
                mm(a[:, 1:3, :], l0, row, False, last, False)
                mm(b[:, 0:2, :], h1, row, first, False, False)
                return mm(b[:, 0:3:2, :], l1, row, False, last, False)

            def split_products(o, pairs):
                todo = [(l[a], r[c]) for l, r in pairs for a, c in ((0, 0), (0, 1), (1, 0))]
                for k, (l, r) in enumerate(todo):
                    last = mm(o, l, r, k == 0, k == len(todo) - 1)
                return last

            def project(bank, width, weights, rows_, name):
                for ob in range(KC):
                    for k in range(KC):
                        last = mm(ps[:, bank, ob * width:(ob + 1) * width], weights[:, k, ob * P:(ob + 1) * P],
                                  rows_[k], k == 0, k == KC - 1)
                last.then_inc(sem(name), 1)

            for step, i in plan:
                if step == "pre":
                    pe.wait_ge(sem("z"), i + 1)
                    turn_rows(TH * i, CHAIN_B + i)
                    pe.wait_ge(sem("zT"), i + 1)
                    project(CHAIN_B + 2 + i, TOK, w0[:, 0, :, :], [z0T[:, k, i * TOK:(i + 1) * TOK] for k in range(KC)], "q0")
                elif step == "flags":
                    pe.wait_ge(sem("flag"), 1)
                    mm(ps[:, CHAIN_B, 0:T], const("side"), flags[:, :], True, True).then_inc(sem("flags"), 1)
                elif step == "gram":
                    b, c = divmod(i, CH_B)
                    pe.wait_ge(sem("high_done"), i + 1)
                    pe.wait_ge(sem("low_done"), i + 1)
                    if b and c == 0:
                        pe.wait_ge(sem("g"), b)
                    for r in range(ROWS):
                        last = gram_tile(c, r, P, c == 0 and r == 0, False)
                    if c == CH_B - 1:
                        last = gram_tile(c, ROWS, TAIL, False, True)
                    last.then_inc(sem("gram_chunk"), 1)
                elif step == "cross1":
                    s = i % 2
                    if i == 0:
                        pe.wait_ge(sem("const_in"), 16)
                        pe.wait_ge(sem("w0_in"), 16)
                    pe.wait_ge(sem("g"), i + 1)
                    if i:
                        pe.wait_ge(sem("mb"), i)
                    bank = ps[:, CROSS_B[0], :]
                    turn(bank[:, 0:P], gab[:, s, 0, 1, 0:P])
                    turn(bank[:, P:2 * P], gab[:, s, 1, 2, 0:P])
                    turn(bank[:, 2 * P:3 * P], gab[:, s, 1, 0, 0:P])
                    turn(bank[:, 3 * P:4 * P], gab[:, s, 0, 2, 0:P]).then_inc(sem("g_turned"), 1)
                elif step == "cross2_product":
                    pe.wait_ge(sem("gs"), i + 1)
                    if i:
                        pe.wait_ge(sem("ctxT"), i)
                    lhs = ((gs[:, 0, :], gs[:, 3, :]), (gs[:, 2, :], gs[:, 1, :]))
                    for ib in range(KC):
                        for k in range(KC):
                            last = mm(ps[:, CROSS_B[1], ib * D:(ib + 1) * D], lhs[ib][k], w0[:, 2, k, :],
                                      k == 0, k == KC - 1)
                    last.then_inc(sem("u"), 1)
                    pe.wait_ge(sem("crep"), i + 1)
                    for k in range(KC):
                        last = mm(ps[:, CROSS_B[0], 0:D], crep[:, k, :], w0[:, 2, k, :], k == 0, k == KC - 1)
                    last.then_inc(sem("sv"), 1)
                elif step == "cross3":
                    pe.wait_ge(sem("cv"), i + 1)
                    for ob in range(KC):
                        for k in range(KC):
                            last = mm(ps[:, CROSS_B[0], D + ob * P:D + (ob + 1) * P], w0[:, 1, k, ob * P:(ob + 1) * P],
                                      cv[:, k, ob * P:(ob + 1) * P], k == 0, k == KC - 1)
                    last.then_inc(sem("kv"), 1)
                elif step == "cross4":
                    pe.wait_ge(sem("mb"), i + 1)
                    pe.wait_ge(sem("q0T"), i // BH + 1)
                    for ob in range(KC):
                        last = mm(ps[:, CROSS_B[1], ob * S:(ob + 1) * S], mb[:, ob, :], q0T[:, ob, i * S:(i + 1) * S],
                                  True, True)
                    last.then_inc(sem("ctx"), 1)
                elif step == "xo_product":
                    pe.wait_ge(sem("ctxT"), BH * (i + 1))
                    if i:
                        pe.wait_ge(sem("aT"), 4 * i)
                    else:
                        pe.wait_ge(sem("nan"), 1)
                    for t in range(TH):
                        for ob in range(KC):
                            last = mm(ps[:, CHAIN_B, t * D:(t + 1) * D], ctxT[:, i, ob, t * P:(t + 1) * P],
                                      w0[:, 3, ob, :], ob == 0, ob == KC - 1)
                    last.then_inc(sem("xo"), 1)
                elif step == "turn_z":
                    g, k = i
                    pe.wait_ge(sem("z"), 3 + 3 * g + k)
                    if g and k == 0:
                        pe.wait_ge(sem("s2"), TH * g)
                    if k:
                        pe.wait_ge(sem("x2"), TH * g + TH)
                    turn_rows(TH * g, CHAIN_B + 1)
                elif step == "proj1_product":
                    pe.wait_ge(sem("w_in"), 16 * 7)
                    pe.wait_ge(sem("zT"), 3 + 2 * i)
                    if i:
                        pe.wait_ge(sem("xT"), i)
                        pe.wait_ge(sem("logits"), i)
                    else:
                        pe.wait_ge(sem("q0T"), HALVES)
                    z = [zT[:, k, :] for k in range(KC)]
                    project(CHAIN_B + 2, TOK, w1[:, 0, :, :], z, "q1")
                    project(CHAIN_B + 3, TOK, w1[:, 1, :, :], z, "k1")
                    pe.wait_ge(sem("y"), i + 1)
                    for t in range(TH):
                        for k in range(KC):
                            last = mm(ps[:, CHAIN_B, t * D:(t + 1) * D], zT[:, k, t * P:(t + 1) * P],
                                      w1[:, 2, k, :], k == 0, k == KC - 1)
                    last.then_inc(sem("v1"), 1)
                elif step == "score_product":
                    g, kind = i // 4, i // 2 % 2
                    pe.wait_ge(sem("qp"), 2 * g + kind + 1)
                    if i % 2:
                        pe.wait_ge(sem("v"), 2 * g + kind + 1)
                    pe.wait_ge(sem("kblk"), 2 * g + kind + 1)
                    if kind:
                        pe.wait_ge(sem("roped"), 2 * g + 2)
                    for j in range(KC):
                        for bb in range(2):
                            jb = j * BH + 2 * (i % 2) + bb
                            last = mm(ps[:, tile_bank(i) + j, :].rearrange("p (r b k) -> p r b k", b=2, k=S)[:, :, bb, :],
                                      qp[:, jb, :, :].rearrange("p h q -> p (h q)"), kblk[:, jb, :, :], True, True)
                    last.then_inc(sem("scores"), 1)
                elif step == "turn_p":
                    pe.wait_ge(sem("prob"), i + 1)
                    for half in range(2):
                        for c in range(4):
                            last = turn(ps[:, tile_bank(i) + half, c * P:(c + 1) * P],
                                        prob[:, i % 2, 4 * half + c, :])
                        last.then_inc(sem("p_turned"), 1)
                elif step == "values":
                    pe.wait_ge(sem("v"), 2 * (i // 4) + i // 2 % 2 + 1)
                    pe.wait_ge(sem("probT"), 2 * i + 2)
                    for c in range(H // 2):
                        last = mm(ps[:, tile_bank(i), c * 4 * HD:(c + 1) * 4 * HD], probT[:, i % 2, c, :],
                                  vblk[:, i % 2, c, :, :].rearrange("p b d -> p (b d)"), True, True)
                    last.then_inc(sem("pv"), 1)
                elif step == "turn_o":
                    pe.wait_ge(sem("on"), i + 1)
                    for bb in range(2):
                        for j in range(KC):
                            c = 2 * j + bb
                            last = turn(ps[:, tile_bank(i), c * P:(c + 1) * P],
                                        on[i % 2][:, bb, j, :, :].rearrange("p i d -> p (i d)"))
                    last.then_inc(sem("o_turned"), 1)
                elif step == "project":
                    pe.wait_ge(sem("aT"), i + 1)
                    w = wo if i // 2 % 2 else w1[:, 3, :, :]
                    for j in range(KC):
                        last = mm(ps[:, tile_bank(i) + 1, 0:D], aT[i % 2][:, j, :, :].rearrange("p b q -> p (b q)"),
                                  w[:, j, :], j == 0, j == KC - 1)
                    last.then_inc(sem("ao"), 1)
                elif step == "proj2":
                    pe.wait_ge(sem("zT"), 4 + 2 * i)
                    z = [zT[:, k, :] for k in range(KC)]
                    project(CHAIN_B, TOK, wq, z, "q2")
                    for k in range(KC):
                        last = mm(ps[:, CHAIN_B + 1, 0:TOK], wkvc[:, k, :], z[k], k == 0, k == KC - 1)
                    last.then_inc(sem("kvc"), 1)
                    pe.wait_ge(sem("qs"), i + 1)
                    mm(ps[:, CHAIN_B + 2, :], const("rot"), qs[:, :, :].rearrange("p c n -> p (c n)"),
                       True, True).then_inc(sem("rot"), 1)
                    pe.wait_ge(sem("kvcT"), i + 1)
                    for ob in range(KC):
                        last = mm(ps[:, CHAIN_B + 3, ob * TOK:(ob + 1) * TOK], wkv[0:P // 2, ob * P:(ob + 1) * P],
                                  kvcT[0:P // 2, :], True, True)
                    last.then_inc(sem("k2"), 1)
                    for t in range(TH):
                        last = mm(ps[:, CHAIN_B + 1, t * D:(t + 1) * D], kvcT[P // 2:P, t * P:(t + 1) * P],
                                  wkv[P // 2:P, :], True, True)
                    last.then_inc(sem("v2"), 1)
                    pe.wait_ge(sem("ks"), i + 1)
                    mm(ps[:, CHAIN_B, :], const("rot"), ks[:, :, :].rearrange("p c n -> p (c n)"),
                       True, True).then_inc(sem("rot"), 1)
                elif step == "turn_x":
                    pe.wait_ge(sem("z"), 5 + 3 * i)
                    turn_rows(TH * i, CHAIN_B + 2)
                elif step == "gates":
                    pe.wait_ge(sem("xT"), i + 1)
                    pe.wait_ge(sem("s2"), TH * i + TH)
                    for t in range(TH):
                        for k in range(KC):
                            last = mm(ps[:, CHAIN_B + 3, t * 16:t * 16 + GRP + E], xT[:, k, t * P:(t + 1) * P],
                                      gate[:, k, :], k == 0, k == KC - 1)
                    last.then_inc(sem("gates"), 1)
                elif step == "hidden_product":
                    use = dense_use("hidden", i)
                    m = i % 8
                    if m == 0:
                        pe.wait_ge(sem("xL"), i // 8 + 1)
                        pe.wait_ge(sem("piece_low"), 4)
                    if use == 0:
                        pe.wait_ge(sem("g"), B)
                        pe.wait_ge(sem("mb"), B)
                        pe.wait_ge(sem("ctxT"), B)
                    if use >= 4:
                        pe.wait_ge(sem("taken"), use - 3)
                    for side in range(2):
                        col = side * HID + (m % 4) * P
                        last = split_products(
                            ps[:, DENSE_B[use % 4], side * TOK:(side + 1) * TOK],
                            [([dense[:, a, 2 * (m // 4) + k, col:col + P] for a in range(2)],
                              [xHL[:, a, k, :] for a in range(2)]) for k in range(KC)])
                    last.then_inc(sem("products"), 1)
                elif step == "shared_product":
                    use = dense_use(step.removesuffix("_product"), i)
                    tok = slice((i % TH) * P, (i % TH + 1) * P)
                    pe.wait_ge(sem("h_low"), 8 * (i // TH) + 4)
                    pe.wait_ge(sem("piece_low"), 5)
                    pe.wait_ge(sem("taken"), use - 3)
                    split_products(
                        ps[:, DENSE_B[use % 4], 0:D],
                        [([hT[:, 0, a, k, tok] for a in range(2)], [dense[:, a, 4, k * D:(k + 1) * D] for a in range(2)])
                         for k in range(HID // P)]).then_inc(sem("products"), 1)
                elif step == "experts_product":
                    use = dense_use(step.removesuffix("_product"), i)
                    t, u = i
                    tok = slice((t % TH) * P, (t % TH + 1) * P)
                    pe.wait_ge(sem("h_low"), 8 * (t // TH) + 8)
                    pe.wait_ge(sem("piece_low"), 5 + 2 * u + 2)
                    pe.wait_ge(sem("taken"), use - 3)
                    split_products(
                        ps[:, DENSE_B[use % 4], :],
                        [([hT[:, 1, a, k, tok] for a in range(2)], [w2[:, u, a, k, :] for a in range(2)])
                         for k in range(HID // P)]).then_inc(sem("products"), 1)

        @block.vector
        def _(dve):
            steps = [0]
            roots = [0]
            squares = [0]
            zs = [0]

            def link(ins):
                steps[0] += 1
                ins.then_inc(sem("dve_step"), 1)
                dve.wait_ge(sem("dve_step"), steps[0])

            def roots_of(src, eps, lo, hi):
                roots[0] += 1
                dve.tensor_scalar(ve[:, lo:hi], src, eps, None, ALU.add).then_inc(sem("var"), 1)

            def moments(src, lo, hi):
                for t in range(lo, hi):
                    last = dve.bn_stats(st[:, t, :], src[:, t, :])
                link(last)
                for t in range(lo, hi):
                    last = dve.bn_aggr(mv[:, t, :], st[:, t, :])
                link(last)
                roots_of(mv[:, lo:hi, 1], LN_EPS, lo, hi)

            def normalise(src, dst, lo, hi):
                moments(src, lo, hi)
                dve.wait_ge(sem("rstd"), roots[0])
                for t in range(lo, hi):
                    last = dve.tensor_scalar(dst[:, t, :], src[:, t, :], mv[:, t, 0:1], rstd[:, t:t + 1],
                                             ALU.subtract, ALU.mult)
                return last

            def rms_scaled(w, lo, hi):
                squares[0] += hi - lo
                dve.wait_ge(sem("ms"), squares[0])
                roots_of(ms[:, lo:hi], RMS_EPS, lo, hi)
                dve.wait_ge(sem("rstd"), roots[0])
                for t in range(lo, hi):
                    last = dve.scalar_tensor_tensor(out=Z[:, t, :], in0=Z[:, t, :], scalar=rstd[:, t:t + 1],
                                                    in1=rows[:, w, :], op0=ALU.mult, op1=ALU.mult)
                return last

            def to_z(ins):
                zs[0] += 1
                ins.then_inc(sem("z"), 1)
                dve.wait_ge(sem("z"), zs[0])

            def queries(src):
                for hl in range(2):
                    last = dve.tensor_scalar(qp[:, :, hl, :], src, parity(hl), None, ALU.mult)
                last.then_inc(sem("qp"), 1)

            def gate_groups(g):
                n = TH
                got = ps[:, CHAIN_B + 3, 0:16 * TH].rearrange("p (t c) -> p t c", c=16)[:, :, 0:GRP + E]
                dve.tensor_tensor(lg[:, :, :], got, ebias[:, :].unsqueeze(1).to_broadcast([P, n, GRP + E]),
                                  ALU.add).then_inc(sem("logits"), 1)
                dve.wait_ge(sem("logits"), g + 1)
                link(dve.tensor_reduce(gm[:, :], lg[:, :, 0:GRP], AX.X, ALU.max))
                dve.tensor_tensor(eg[:, :, :], lg[:, :, 0:GRP], gm[:, :].unsqueeze(2).to_broadcast([P, n, GRP]),
                                  ALU.subtract).then_inc(sem("gates_a"), 1)

            def gate_experts():
                n = TH
                link(dve.tensor_reduce(gsum[:, :], eg[:, :, :], AX.X, ALU.add))
                link(dve.reciprocal(gprob[:, :], gsum[:, :]))
                link(dve.tensor_tensor(ind[:, :, 0], eg[:, :, 0], eg[:, :, 1], ALU.is_ge))
                link(dve.tensor_scalar(ind[:, :, 1], ind[:, :, 0], -1.0, 1.0, ALU.mult, ALU.add))
                link(dve.tensor_scalar(off[:, :, :], ind[:, :, :], -LOW, LOW, ALU.mult, ALU.add))
                by_group = lg[:, :, GRP:GRP + E].rearrange("p t (g e) -> p t g e", g=GRP)
                em4 = em[:, :, :].rearrange("p t (g e) -> p t g e", g=GRP)
                wide = [P, n, GRP, E // GRP]
                link(dve.tensor_tensor(em4, by_group, ind[:, :, :].unsqueeze(3).to_broadcast(wide), ALU.mult))
                link(dve.tensor_tensor(em4, em4, off[:, :, :].unsqueeze(3).to_broadcast(wide), ALU.add))
                link(dve.tensor_reduce(emax[:, :], em[:, :, :], AX.X, ALU.max))
                dve.tensor_tensor(em[:, :, :], em[:, :, :], emax[:, :].unsqueeze(2).to_broadcast([P, n, E]),
                                  ALU.subtract).then_inc(sem("gates_b"), 1)

            def gate_best(g):
                n = TH
                link(dve.tensor_reduce(esum[:, :], pe8[:, :, :], AX.X, ALU.add))
                link(dve.reciprocal(erec[:, :], esum[:, :]))
                link(dve.tensor_tensor(erec[:, :], erec[:, :], gprob[:, :], ALU.mult))
                link(dve.tensor_tensor(pe8[:, :, :], pe8[:, :, :], erec[:, :].unsqueeze(2).to_broadcast([P, n, E]), ALU.mult))
                for t in range(n):
                    last = dve.max(top[:, t, :], pe8[:, t, :])
                link(last)
                for t in range(n):
                    last = dve.max_index(topi[:, t, :], top[:, t, :], pe8[:, t, :])
                link(last)
                link(dve.tensor_copy(topf[:, :, :], topi[:, :, :]))
                for t in range(n):
                    for k, dst in enumerate((w8a, w8)):
                        last = dve.tensor_scalar(dst[:, TH * g + t, :], const("iota"), topf[:, t, k:k + 1],
                                                 top[:, t, k:k + 1], ALU.is_equal, ALU.mult)
                link(last)
                both = slice(TH * g, TH * g + TH)
                link(dve.tensor_tensor(w8[:, both, :], w8[:, both, :], w8a[:, both, :], ALU.add))

            for step, i in plan:
                if step == "norm0":
                    if i == 0:
                        dve.wait_ge(sem("x_in"), 16)
                    to_z(normalise(X, Z, TH * i, TH * i + TH))
                elif step == "flag":
                    dve.wait_ge(sem("mask_in"), 16)
                    dve.wait_ge(sem("const_in"), 16)
                    link(dve.tensor_reduce(flag[:, 0:1], mask[:, :].bitcast(I32), AX.X, ALU.max))
                    dve.tensor_scalar(flags[:, :], const("tile_of"), flag[:, 0:1], 0.0, ALU.mult, ALU.is_gt).then_inc(sem("flag"), 1)
                elif step == "masked":
                    dve.wait_ge(sem("flags"), 1)
                    dve.tensor_scalar(nan_a[:, :], ps[:, CHAIN_B, 0:T], -LOW, -LOW, ALU.mult, ALU.mult).then_inc(sem("nan"), 1)
                    dve.wait_ge(sem("nan"), 1)
                    link(dve.tensor_tensor(nan_b[:, :], nan_a[:, :], nan_a[:, :], ALU.subtract))
                    dve.wait_ge(sem("turned"), 2)
                    for t in range(T):
                        last = dve.scalar_tensor_tensor(out=Z[:, t, :], in0=Z[:, t, :], scalar=nan_b[:, t:t + 1],
                                                        in1=rows[:, 2, :], op0=ALU.add, op1=ALU.add)
                    link(last)
                elif step == "split":
                    c = i % CH_B
                    dve.wait_ge(sem("high_done"), i + 1)
                    if i >= CH_B:
                        dve.wait_ge(sem("gram_chunk"), i - CH_B + 1)
                    for p, lo, hi in [(P, 0, ROWS)] + ([(TAIL, ROWS, ROWS + 1)] if c == CH_B - 1 else []):
                        last = dve.tensor_tensor(halves(cl[0:p, c, lo:hi, :]),
                                                 halves(raw[0:p, ROWS * c + lo:ROWS * c + hi, :]),
                                                 halves(f32(ch[0:p, c, lo:hi, :]))[:, :, :, 0:P], ALU.subtract)
                    last.then_inc(sem("low_done"), 1)
                elif step == "cross1":
                    dve.wait_ge(sem("g_turned"), i + 1)
                    dve.wait_ge(sem("gpre"), i + 1)
                    if i:
                        dve.wait_ge(sem("u"), i)
                    turned = ps[:, CROSS_B[0], :].rearrange("p (c n) -> p c n", n=P)
                    dve.tensor_tensor(gs[:, 0:2, :], gpre[:, i % 2, :, 0:P], turned[:, 0:2, :], ALU.add)
                    dve.wait_ge(sem("g"), i + 1)
                    dve.tensor_tensor(gs[:, 2, :], gab[:, i % 2, 0, 2, 0:P], turned[:, 2, :], ALU.add)
                    dve.tensor_tensor(gs[:, 3, :], gab[:, i % 2, 1, 0, 0:P], turned[:, 3, :], ALU.add).then_inc(sem("gs"), 1)
                elif step == "cross2":
                    if i == 0:
                        dve.wait_ge(sem("rows_in"), 16)
                        dve.wait_ge(sem("cols_in"), 16)
                    dve.wait_ge(sem("sv"), i + 1)
                    dve.scalar_tensor_tensor(out=svn[:, :], in0=rows[:, 3, :], scalar=float(N),
                                             in1=ps[:, CROSS_B[0], 0:D], op0=ALU.mult, op1=ALU.add)
                    dve.wait_ge(sem("u"), i + 1)
                    dve.wait_ge(sem("gpre"), i + 1)
                    if i:
                        dve.wait_ge(sem("kv"), i)
                    for ib in range(KC):
                        last = dve.scalar_tensor_tensor(out=cv[:, ib, :], in0=rows[:, 3, :], scalar=gpre[:, i % 2, ib, P:P + 1],
                                                        in1=ps[:, CROSS_B[1], ib * D:(ib + 1) * D],
                                                        op0=ALU.mult, op1=ALU.add)
                    last.then_inc(sem("cv"), 1)
                elif step == "cross3":
                    dve.wait_ge(sem("kv"), i + 1)
                    for ob in range(KC):
                        last = dve.scalar_tensor_tensor(
                            out=m1[:, ob, :], in0=svn[:, ob * P:(ob + 1) * P], scalar=cols[:, 2 + ob:3 + ob],
                            in1=ps[:, CROSS_B[0], D + ob * P:D + (ob + 1) * P], op0=ALU.mult, op1=ALU.add)
                    link(last)
                    if i:
                        dve.wait_ge(sem("ctx"), i)
                    dve.tensor_tensor(mb[:, :, :], m1[:, :, :], const("heads").unsqueeze(1).to_broadcast([P, KC, P]),
                                      ALU.mult).then_inc(sem("mb"), 1)
                elif step == "xo":
                    lo, hi = TH * i, TH * i + TH
                    dve.wait_ge(sem("xo"), i + 1)
                    dve.tensor_tensor(Z[:, lo:hi, :], Z[:, lo:hi, :],
                                      ps[:, CHAIN_B, :].rearrange("p (t n) -> p t n", t=TH), ALU.add).then_inc(sem("y"), 1)
                    dve.wait_ge(sem("y"), i + 1)
                    moments(Z, lo, hi)
                    for t in range(lo, hi):
                        last = dve.scalar_tensor_tensor(out=Z[:, t, :], in0=Z[:, t, :], scalar=mv[:, t, 0:1],
                                                        in1=rows[:, 0, :], op0=ALU.subtract, op1=ALU.mult)
                    link(last)
                    dve.wait_ge(sem("rstd"), roots[0])
                    if i == 0:
                        dve.wait_ge(sem("x_biased"), 1)
                    for t in range(lo, hi):
                        last = dve.scalar_tensor_tensor(out=X[:, t, :], in0=Z[:, t, :], scalar=rstd[:, t:t + 1],
                                                        in1=X[:, t, :], op0=ALU.mult, op1=ALU.add)
                    link(last)
                elif step == "norm1":
                    to_z(normalise(X, Z, TH * i, TH * i + TH))
                elif step == "proj1":
                    dve.wait_ge(sem("q1"), i + 1)
                    if i:
                        dve.wait_ge(sem("scores"), 4 * i)
                    queries(ps[:, CHAIN_B + 2, :].rearrange("p (c n) -> p c n", n=S))
                elif step == "score":
                    k = i % 2
                    rows_of = prob[:, k, :, :].rearrange("p c (b k) -> p (c b) k", b=2)
                    wide = [P, H, S]
                    dve.wait_ge(sem("scores"), i + 1)
                    got = ps[:, tile_bank(k):tile_bank(k) + 2, :].rearrange("p b (c k) -> p (b c) k", k=S)
                    if i // 2 % 2 == 0:
                        link(dve.tensor_tensor(rows_of, got, const("causal").unsqueeze(1).to_broadcast(wide), ALU.add))
                        got = rows_of
                    link(dve.tensor_reduce(mx[:, k, :], got, AX.X, ALU.max))
                    dve.tensor_tensor(rows_of, got, mx[:, k, :].unsqueeze(2).to_broadcast(wide),
                                      ALU.subtract).then_inc(sem("shifted"), 1)
                elif step == "sums":
                    k = i % 2
                    dve.wait_ge(sem("prob"), i + 1)
                    link(dve.tensor_reduce(sm[:, k, :], prob[:, k, :, :].rearrange("p c (b k) -> p (c b) k", b=2), AX.X, ALU.add))
                    link(dve.reciprocal(rs[:, k, :], sm[:, k, :]))
                elif step == "values":
                    k = i % 2
                    dve.wait_ge(sem("pv"), i + 1)
                    shape = [P, H // 2, 2, 2 * HD]
                    dve.tensor_tensor(on[k][:, :, :, :, :].rearrange("p b j r d -> p (j r) b d"),
                                      ps[:, tile_bank(k), :].rearrange("p (c b d) -> p c b d", b=2, d=2 * HD),
                                      rs[:, k, :].rearrange("p (c b) -> p c b", b=2).unsqueeze(3).to_broadcast(shape),
                                      ALU.mult).then_inc(sem("on"), 1)
                elif step == "turn_o":
                    k = i % 2
                    dve.wait_ge(sem("o_turned"), i + 1)
                    both = ps[:, tile_bank(k), :].rearrange("p (c h q) -> p c h q", h=2, q=S)
                    a = aT[k][:, :, :, :].rearrange("p j b q -> p (j b) q")
                    link(dve.tensor_scalar(a, both[:, :, 0, :], parity(0), None, ALU.mult))
                    dve.scalar_tensor_tensor(out=a, in0=both[:, :, 1, :], scalar=parity(1), in1=a,
                                             op0=ALU.mult, op1=ALU.add).then_inc(sem("aT"), 1)
                elif step == "project":
                    kind, t = i // 2 % 2, TH * (i // 4) + i % 2
                    dve.wait_ge(sem("ao"), i + 1)
                    o = ps[:, tile_bank(i) + 1, 0:D]
                    if kind == 0:
                        dve.tensor_tensor(X[:, t, :], X[:, t, :], o, ALU.add).then_inc(sem("x2"), 1)
                    else:
                        dve.tensor_tensor(Z[:, t, :], Z[:, t, :], o, ALU.add).then_inc(sem("s2"), 1)
                elif step == "norm2":
                    dve.wait_ge(sem("x2"), TH * i + TH)
                    to_z(normalise(X, Z, TH * i, TH * i + TH))
                elif step == "proj2":
                    dve.wait_ge(sem("scores"), 4 * i + 2)
                    sin = const("sin").unsqueeze(1).to_broadcast([P, KC * BH, S])
                    cos = const("cos").unsqueeze(1).to_broadcast([P, KC * BH, S])
                    dve.wait_ge(sem("rot"), 2 * i + 1)
                    link(dve.tensor_tensor(ropet[:, :, :], ps[:, CHAIN_B + 2, :].rearrange("p (c n) -> p c n", n=S), sin, ALU.mult))
                    dve.wait_ge(sem("by_cos"), i + 1)
                    dve.tensor_tensor(qs[:, :, :], qs[:, :, :], ropet[:, :, :], ALU.add).then_inc(sem("roped"), 1)
                    dve.wait_ge(sem("ks"), i + 1)
                    dve.tensor_tensor(kcos[:, :, :], ks[:, :, :], cos, ALU.mult)
                    dve.wait_ge(sem("roped"), 2 * i + 1)
                    dve.wait_ge(sem("rot"), 2 * i + 2)
                    link(dve.tensor_tensor(ropet[:, :, :], ps[:, CHAIN_B, :].rearrange("p (c n) -> p c n", n=S), sin, ALU.mult))
                    low = slice(P // 2, P)
                    dve.tensor_tensor(kcos[low, :, :], kcos[low, :, :], ropet[low, :, :], ALU.add).then_inc(sem("k_sum"), 1)
                    for r in range(2):
                        q = slice(32 * r, 32 * r + 32)
                        last = dve.tensor_tensor(kblk[q, :, r, :], kcos[q, :, :], ropet[q, :, :], ALU.add)
                    last.then_inc(sem("roped"), 1)
                    dve.wait_ge(sem("roped"), 2 * i + 2)
                elif step == "rms1":
                    to_z(rms_scaled(4, TH * i, TH * i + TH))
                elif step == "turn_x":
                    dve.wait_ge(sem("xH"), i + 1)
                    high, low = (xHL[:, part, :, :].rearrange("p k (t c) -> p t k c", c=P) for part in range(2))
                    for t in range(TH):
                        last = dve.tensor_tensor(low[:, t, :, :],
                                                 ps[:, CHAIN_B + 2, t * D:(t + 1) * D].rearrange("p (k c) -> p k c", c=P),
                                                 f32(high[:, t, :, :]), ALU.subtract)
                    last.then_inc(sem("xL"), 1)
                elif step == "gates":
                    dve.wait_ge(sem("gates"), i + 1)
                    gate_groups(i)
                elif step == "gate_experts":
                    dve.wait_ge(sem("eg"), i + 1)
                    gate_experts()
                elif step == "gate_best":
                    dve.wait_ge(sem("ee"), i + 1)
                    gate_best(i)
                elif step == "hidden":
                    use = dense_use(step, i)
                    m = i % 8
                    dve.wait_ge(sem("silu"), i + 1)
                    dve.tensor_tensor(sa[:, m % 4, :], sa[:, m % 4, :], ps[:, DENSE_B[use % 4], TOK:2 * TOK],
                                      ALU.mult).then_inc(sem("taken"), 1)
                elif step == "shared":
                    use = dense_use(step, i)
                    dve.wait_ge(sem("products"), use + 1)
                    dve.tensor_tensor(Z[:, i, :], Z[:, i, :], ps[:, DENSE_B[use % 4], 0:D], ALU.add).then_inc(sem("taken"), 1)
                    dve.wait_ge(sem("taken"), use + 1)
                elif step == "experts":
                    use = dense_use(step, i)
                    t, u = i
                    dve.wait_ge(sem("products"), use + 1)
                    for e in range(2):
                        ins = dve.scalar_tensor_tensor(
                            out=Z[:, t, :], in0=ps[:, DENSE_B[use % 4], e * D:(e + 1) * D],
                            scalar=w8[:, t, 2 * u + e:2 * u + e + 1], in1=Z[:, t, :], op0=ALU.mult, op1=ALU.add)
                        if e == 0:
                            link(ins)
                    ins.then_inc(sem("taken"), 1)
                    dve.wait_ge(sem("taken"), use + 1)
                elif step == "finish":
                    link(rms_scaled(5, i, i + 1))
                    dve.tensor_tensor(X[:, i, :], X[:, i, :], Z[:, i, :], ALU.add).then_inc(sem("x3"), 1)


def kernel(x, ctx_1024, mask_Bx1xSxS2_bf0, L0_xattn_wq_w, L0_xattn_wq_b, L0_xattn_wk_w, L0_xattn_wk_b, L0_xattn_wv_w,
           L0_xattn_wv_b, L0_xattn_wo_w, L0_xattn_wo_b, L0_xattn_ln_g, L0_xattn_ln_b, L0_attn_Wq, L0_attn_Wk,
           L0_attn_Wv, L0_attn_Wo, L0_ffn_Wq, L0_ffn_Wk_c, L0_ffn_Wv_c, L0_ffn_Wk, L0_ffn_Wv, L0_ffn_Wo,
           L0_ffn_W_shared_in, L0_ffn_W_shared_out, L0_ffn_W1_shared, L0_ffn_W2_experts, L0_ffn_Wg_gate,
           L0_ffn_We_gate, L0_ffn_group_bias, L0_ffn_expert_bias, L0_ffn_norm1_w, L0_ffn_norm2_w):
    import concourse.bacc as bacc
    from concourse.bass_utils import run_bass_kernel_spmd as run

    def a(v):
        return np.asarray(v)

    def chunks(w):
        w = a(w)
        return w.reshape(w.shape[0] // P, P, w.shape[1]).transpose(1, 0, 2)

    arrays = {
        "x": a(x).reshape(T, P, D).transpose(1, 0, 2),
        "ctx": a(ctx_1024),
        "mask": a(mask_Bx1xSxS2_bf0).reshape(P, B * S * N // P),
        "const": constants(),
        "w0": np.stack([chunks(a(w).T) for w in (L0_xattn_wq_w, L0_xattn_wk_w, L0_xattn_wv_w, L0_xattn_wo_w)], 1),
        "w1": np.stack([chunks(a(w).T) for w in (L0_attn_Wq, L0_attn_Wk, L0_attn_Wv, L0_attn_Wo)], 1),
        "wq": chunks(L0_ffn_Wq),
        "wkvc": np.concatenate([chunks(L0_ffn_Wk_c), chunks(L0_ffn_Wv_c)], 2),
        "wkv": np.concatenate([a(L0_ffn_Wk), a(L0_ffn_Wv)], 0),
        "wo": chunks(L0_ffn_Wo),
        "gate": np.concatenate([chunks(L0_ffn_Wg_gate), chunks(L0_ffn_We_gate)], 2),
        "dense": np.concatenate([chunks(L0_ffn_W_shared_in), chunks(L0_ffn_W1_shared),
                                 chunks(L0_ffn_W_shared_out).reshape(P, 1, 4 * D)], 1),
        "w2": a(L0_ffn_W2_experts).reshape(E // 2, 2, HID // P, P, D).transpose(3, 0, 2, 1, 4).reshape(P, 8, 1024),
        "cols": np.concatenate([a(L0_xattn_wq_b).reshape(KC, P).T, a(L0_xattn_wk_b).reshape(KC, P).T], 1),
        "rows": np.stack([a(r) for r in (L0_xattn_ln_g, L0_xattn_ln_b, L0_xattn_wo_b, L0_xattn_wv_b,
                                         L0_ffn_norm1_w, L0_ffn_norm2_w)], 0),
        "ebias": np.concatenate([a(L0_ffn_group_bias), a(L0_ffn_expert_bias)], 0),
    }
    arrays = {k: np.ascontiguousarray(v) for k, v in arrays.items()}
    nc = bacc.Bacc("TRN2", target_bir_lowering=False, num_devices=1)
    args = [nc.dram_tensor("in_" + k, v.shape, mybir.dt.from_np(v.dtype), kind="ExternalInput").ap()
            for k, v in arrays.items()]
    o = nc.dram_tensor("out_x", (B * S, D), F32, kind="ExternalOutput").ap()
    layer(nc, *args, o)
    r = run(nc, [{"in_" + k: v for k, v in arrays.items()}], core_ids=[0])
    return r.results[0]["out_x"].reshape(B, S, D)
```
